# Optimizing a Trainium2 kernel written in Bass

```python
import numpy as np
import jax
import jax.numpy as jnp

def _softmax(x, axis=-1):
    return jax.nn.softmax(x, axis=axis)

def _gelu(x):
    return jax.nn.gelu(x, approximate=True)

def _silu(x):
    return jax.nn.silu(x)

def _sigmoid(x):
    return jax.nn.sigmoid(x)

def _layernorm(x, axis=-1, eps=1e-05):
    m = jnp.mean(x, axis=axis, keepdims=True)
    v = jnp.var(x, axis=axis, keepdims=True)
    return (x - m) / jnp.sqrt(v + eps)

def _scatter_add(tgt, idx, src, axis=0):
    return tgt.at[idx].add(src)

def _segment_sum(src, seg, n):
    return jax.ops.segment_sum(src, seg, n)
kernel_name = 'mk_gnn_preln_d4_gnn_r64_797dbd'

def setup_inputs(seed: int=0):
    np.random.seed(seed)
    _w = jnp.asarray

    def _rec_inputs():
        import jax
        import jax.numpy as jnp
        _gk = jax.random.key(seed)
        x = -0.000202 + 1 * jax.random.normal(jax.random.fold_in(_gk, 1), (50000, 64), jnp.float32)
        src = jax.random.randint(jax.random.fold_in(_gk, 2), (25000,), 0, 50000, jnp.int32)
        dst = jnp.minimum((50000 * jax.random.uniform(jax.random.fold_in(_gk, 3), (25000,)) ** 2.0).astype(jnp.int32), 49999)
        _o = jnp.argsort(dst, stable=True)
        src = src[_o]
        dst = dst[_o]
        edge_attr_64 = 0.000189758 + 1.00013 * jax.random.normal(jax.random.fold_in(_gk, 12), (25000, 64), jnp.float32)
        edge_weight = jax.random.uniform(jax.random.fold_in(_gk, 14), (25000,), jnp.float32, 0.0, 1)
        return (x, src, dst, edge_attr_64, edge_weight)
    x, src, dst, edge_attr_64, edge_weight = _rec_inputs()

    def _L0_gnn_setup():
        import jax, jax.numpy as jnp
        import numpy as np
        N_NODES = 100000
        N_EDGES = 25000
        N_FEAT = 64
        EPS = 1e-08
        key = jax.random.key(seed)
        kx, ke = jax.random.split(key)
        x = jax.random.normal(kx, (N_NODES, N_FEAT), dtype=jnp.float32)
        edge_index = jax.random.randint(ke, (2, N_EDGES), 0, N_NODES, dtype=jnp.int32)
        return {'x': x, 'edge_index': edge_index}
    _L0_gnn_all = _L0_gnn_setup()
    _L0_gnn_in = {k: v for k, v in _L0_gnn_all.items() if k in ()}
    del _L0_gnn_all

    def _L1_gnn_setup():
        import jax, jax.numpy as jnp
        import numpy as np
        N = 50000
        E = 12500
        D = 64
        H = 5
        C = 64
        NEG_SLOPE = 0.2
        LN_EPS = 1e-05

        def _layernorm(x, g, b):
            m = x.mean(-1, keepdims=True)
            v = ((x - m) ** 2).mean(-1, keepdims=True)
            return (x - m) * jax.lax.rsqrt(v + LN_EPS) * g + b

        def _gatv2_conv(x, edge_index, edge_attr, Wl, bl, Wr, br, We, att, conv_bias):
            src, dst = (edge_index[0], edge_index[1])
            n = x.shape[0]
            cnt = jax.ops.segment_sum(jnp.ones((edge_attr.shape[0],), x.dtype), dst, num_segments=n)
            loop_attr = jax.ops.segment_sum(edge_attr, dst, num_segments=n) / jnp.maximum(cnt, 1.0)[:, None]
            ar = jnp.arange(n, dtype=src.dtype)
            src2 = jnp.concatenate([src, ar])
            dst2 = jnp.concatenate([dst, ar])
            ea = jnp.concatenate([edge_attr, loop_attr], axis=0)
            xl = (x @ Wl + bl).reshape(n, H, C)
            xr = (x @ Wr + br).reshape(n, H, C)
            em = (ea @ We).reshape(-1, H, C)
            m = jax.nn.leaky_relu(xl[src2] + xr[dst2] + em, NEG_SLOPE)
            logits = jnp.einsum('ehc,hc->eh', m, att)
            mx = jax.lax.stop_gradient(jax.ops.segment_max(logits, dst2, num_segments=n))
            z = jnp.exp(logits - mx[dst2])
            den = jax.ops.segment_sum(z, dst2, num_segments=n)
            alpha = z / den[dst2]
            out = jax.ops.segment_sum(xl[src2] * alpha[:, :, None], dst2, num_segments=n)
            return out.mean(axis=1) + conv_bias
        key = jax.random.key(seed)
        ks = jax.random.split(key, 16)
        s = 0.05
        return {'features': jax.random.normal(ks[0], (N, D), dtype=jnp.float32), 'edge_index': jax.random.randint(ks[1], (2, E), 0, N, dtype=jnp.int64), 'rel_emb_vector': jax.random.normal(ks[2], (E, D), dtype=jnp.float32), 'Wl': jax.random.normal(ks[3], (D, H * C), dtype=jnp.float32) * s, 'bl': jnp.zeros((H * C,), jnp.float32), 'Wr': jax.random.normal(ks[4], (D, H * C), dtype=jnp.float32) * s, 'br': jnp.zeros((H * C,), jnp.float32), 'We': jax.random.normal(ks[5], (D, H * C), dtype=jnp.float32) * s, 'att': jax.random.normal(ks[6], (H, C), dtype=jnp.float32) * s, 'conv_bias': jnp.zeros((C,), jnp.float32), 'ln_g': jnp.ones((D,), jnp.float32), 'ln_b': jnp.zeros((D,), jnp.float32), 'ln1_g': jnp.ones((D,), jnp.float32), 'ln1_b': jnp.zeros((D,), jnp.float32), 'fc_w': jax.random.normal(ks[7], (D, 2 * D), dtype=jnp.float32) * s, 'fc_b': jnp.zeros((2 * D,), jnp.float32), 'fc1_w': jax.random.normal(ks[8], (2 * D, D), dtype=jnp.float32) * s, 'fc1_b': jnp.zeros((D,), jnp.float32)}
    _L1_gnn_all = _L1_gnn_setup()
    _L1_gnn_in = {k: v for k, v in _L1_gnn_all.items() if k in ('Wl', 'bl', 'Wr', 'br', 'We', 'att', 'conv_bias', 'ln_g', 'ln_b', 'ln1_g', 'ln1_b', 'fc_w', 'fc_b', 'fc1_w', 'fc1_b')}
    del _L1_gnn_all

    def _L2_gnn_setup():
        import jax, jax.numpy as jnp
        import numpy as np
        N = 100000
        NNZ = 25000
        D = 64
        key = jax.random.key(seed)
        k1, k2, k3, k4 = jax.random.split(key, 4)
        x = jax.random.normal(k1, (N, D), dtype=jnp.float32)
        row = jax.random.randint(k2, (NNZ,), 0, N, dtype=jnp.int64)
        col = jax.random.randint(k3, (NNZ,), 0, N, dtype=jnp.int64)
        value = jax.random.uniform(k4, (NNZ,), dtype=jnp.float32)
        return {'x': x, 'row': row, 'col': col, 'value': value, 'size': N}
    _L2_gnn_all = _L2_gnn_setup()
    _L2_gnn_in = {k: v for k, v in _L2_gnn_all.items() if k in ()}
    del _L2_gnn_all

    def _L3_gnn_setup():
        import jax, jax.numpy as jnp
        import numpy as np
        N_NODES = 100000
        key = jax.random.key(seed)
        k1, k2, k3, k4 = jax.random.split(key, 4)
        feats = jax.random.normal(k1, (N_NODES, 64), dtype=jnp.float32)
        src = jax.random.randint(k2, (25000,), 0, N_NODES, dtype=jnp.int32)
        dst = jax.random.randint(k3, (25000,), 0, N_NODES, dtype=jnp.int32)
        W = jax.random.normal(k4, (64, 64), dtype=jnp.float32) * (1.0 / jnp.sqrt(64.0))
        b = jnp.zeros((64,), dtype=jnp.float32)
        return {'feats': feats, 'src': src, 'dst': dst, 'W': W, 'b': b}
    _L3_gnn_all = _L3_gnn_setup()
    _L3_gnn_in = {k: v for k, v in _L3_gnn_all.items() if k in ('W', 'b')}
    del _L3_gnn_all
    return {'x': x, 'src': src, 'dst': dst, 'edge_attr_64': edge_attr_64, 'edge_weight': edge_weight, 'L1_gnn_Wl': _L1_gnn_in['Wl'], 'L1_gnn_bl': _L1_gnn_in['bl'], 'L1_gnn_Wr': _L1_gnn_in['Wr'], 'L1_gnn_br': _L1_gnn_in['br'], 'L1_gnn_We': _L1_gnn_in['We'], 'L1_gnn_att': _L1_gnn_in['att'], 'L1_gnn_conv_bias': _L1_gnn_in['conv_bias'], 'L1_gnn_ln_g': _L1_gnn_in['ln_g'], 'L1_gnn_ln_b': _L1_gnn_in['ln_b'], 'L1_gnn_ln1_g': _L1_gnn_in['ln1_g'], 'L1_gnn_ln1_b': _L1_gnn_in['ln1_b'], 'L1_gnn_fc_w': _L1_gnn_in['fc_w'], 'L1_gnn_fc_b': _L1_gnn_in['fc_b'], 'L1_gnn_fc1_w': _L1_gnn_in['fc1_w'], 'L1_gnn_fc1_b': _L1_gnn_in['fc1_b'], 'L3_gnn_W': _L3_gnn_in['W'], 'L3_gnn_b': _L3_gnn_in['b']}

def reference(x, src, dst, edge_attr_64, edge_weight, L1_gnn_Wl, L1_gnn_bl, L1_gnn_Wr, L1_gnn_br, L1_gnn_We, L1_gnn_att, L1_gnn_conv_bias, L1_gnn_ln_g, L1_gnn_ln_b, L1_gnn_ln1_g, L1_gnn_ln1_b, L1_gnn_fc_w, L1_gnn_fc_b, L1_gnn_fc1_w, L1_gnn_fc1_b, L3_gnn_W, L3_gnn_b):
    import jax
    import jax.numpy as jnp

    def _L0_gnn_ref(x, edge_index):
        import jax, jax.numpy as jnp
        import numpy as np
        N_NODES = 100000
        N_EDGES = 25000
        N_FEAT = 64
        EPS = 1e-08
        src = edge_index[0]
        tgt = edge_index[1]
        num_nodes = x.shape[0]
        messages = jnp.take(x, src, axis=0)
        ones = jnp.ones((messages.shape[0], 1), dtype=messages.dtype)
        count = jax.ops.segment_sum(ones, tgt, num_segments=num_nodes)
        sum_msgs = jax.ops.segment_sum(messages, tgt, num_segments=num_nodes)
        safe_count = jnp.maximum(count, jnp.asarray(EPS, dtype=count.dtype))
        mean = sum_msgs / safe_count
        mean_per_edge = jnp.take(mean, tgt, axis=0)
        squared_diff = jnp.square(messages - mean_per_edge)
        sum_sq = jax.ops.segment_sum(squared_diff, tgt, num_segments=num_nodes)
        variance = sum_sq / safe_count
        std_dev = jnp.sqrt(jnp.maximum(variance, jnp.zeros_like(variance)))
        std_dev = jnp.where(count <= 1, jnp.zeros_like(std_dev), std_dev)
        return std_dev

    def _L1_gnn_ref(features, edge_index, rel_emb_vector, Wl, bl, Wr, br, We, att, conv_bias, ln_g, ln_b, ln1_g, ln1_b, fc_w, fc_b, fc1_w, fc1_b):
        import jax, jax.numpy as jnp
        import numpy as np
        N = 50000
        E = 12500
        D = 64
        H = 5
        C = 64
        NEG_SLOPE = 0.2
        LN_EPS = 1e-05

        def _layernorm(x, g, b):
            m = x.mean(-1, keepdims=True)
            v = ((x - m) ** 2).mean(-1, keepdims=True)
            return (x - m) * jax.lax.rsqrt(v + LN_EPS) * g + b

        def _gatv2_conv(x, edge_index, edge_attr, Wl, bl, Wr, br, We, att, conv_bias):
            src, dst = (edge_index[0], edge_index[1])
            n = x.shape[0]
            cnt = jax.ops.segment_sum(jnp.ones((edge_attr.shape[0],), x.dtype), dst, num_segments=n)
            loop_attr = jax.ops.segment_sum(edge_attr, dst, num_segments=n) / jnp.maximum(cnt, 1.0)[:, None]
            ar = jnp.arange(n, dtype=src.dtype)
            src2 = jnp.concatenate([src, ar])
            dst2 = jnp.concatenate([dst, ar])
            ea = jnp.concatenate([edge_attr, loop_attr], axis=0)
            xl = (x @ Wl + bl).reshape(n, H, C)
            xr = (x @ Wr + br).reshape(n, H, C)
            em = (ea @ We).reshape(-1, H, C)
            m = jax.nn.leaky_relu(xl[src2] + xr[dst2] + em, NEG_SLOPE)
            logits = jnp.einsum('ehc,hc->eh', m, att)
            mx = jax.lax.stop_gradient(jax.ops.segment_max(logits, dst2, num_segments=n))
            z = jnp.exp(logits - mx[dst2])
            den = jax.ops.segment_sum(z, dst2, num_segments=n)
            alpha = z / den[dst2]
            out = jax.ops.segment_sum(xl[src2] * alpha[:, :, None], dst2, num_segments=n)
            return out.mean(axis=1) + conv_bias
        conv = _gatv2_conv(features, edge_index, rel_emb_vector, Wl, bl, Wr, br, We, att, conv_bias)
        x = _layernorm(features + conv, ln_g, ln_b)
        h = (x @ fc_w + fc_b) @ fc1_w + fc1_b
        return _layernorm(x + h, ln1_g, ln1_b)

    def _L2_gnn_ref(x, row, col, value, size):
        import jax, jax.numpy as jnp
        import numpy as np
        N = 100000
        NNZ = 25000
        D = 64
        gathered = value[:, None] * x[col]
        y = jax.ops.segment_sum(gathered, row, num_segments=size)
        return y

    def _L3_gnn_ref(feats, src, dst, W, b):
        import jax, jax.numpy as jnp
        import numpy as np
        N_NODES = 100000
        n = feats.shape[0]
        ones = jnp.ones_like(src, dtype=feats.dtype)
        out_deg = jax.ops.segment_sum(ones, src, num_segments=n)
        in_deg = jax.ops.segment_sum(ones, dst, num_segments=n)
        norm_src = jnp.where(out_deg > 0, jax.lax.rsqrt(jnp.maximum(out_deg, 1.0)), 0.0)
        norm_dst = jnp.where(in_deg > 0, jax.lax.rsqrt(jnp.maximum(in_deg, 1.0)), 0.0)
        h = feats * norm_src[:, None]
        msgs = jnp.take(h, src, axis=0)
        agg = jax.ops.segment_sum(msgs, dst, num_segments=n)
        agg = agg * norm_dst[:, None]
        out = agg @ W + b
        return jax.nn.relu(out)
    edge_index = jnp.stack([src, dst])
    h = jnp.maximum(_layernorm(x, axis=-1), 0.0)
    x = x + _L0_gnn_ref(h, edge_index)
    h = jnp.maximum(_layernorm(x, axis=-1), 0.0)
    x = x + _L1_gnn_ref(h, edge_index, edge_attr_64, L1_gnn_Wl, L1_gnn_bl, L1_gnn_Wr, L1_gnn_br, L1_gnn_We, L1_gnn_att, L1_gnn_conv_bias, L1_gnn_ln_g, L1_gnn_ln_b, L1_gnn_ln1_g, L1_gnn_ln1_b, L1_gnn_fc_w, L1_gnn_fc_b, L1_gnn_fc1_w, L1_gnn_fc1_b)
    h = jnp.maximum(_layernorm(x, axis=-1), 0.0)
    x = x + _L2_gnn_ref(h, src, dst, edge_weight, 50000)
    h = jnp.maximum(_layernorm(x, axis=-1), 0.0)
    x = x + _L3_gnn_ref(h, src, dst, L3_gnn_W, L3_gnn_b)
    return x

_drawn_inputs = setup_inputs


def setup_inputs(seed=0):
    import zlib

    import numpy as np

    out = dict(_drawn_inputs(seed))
    spreads = {'L1_gnn_bl': (0.0, 0.1),
     'L1_gnn_br': (0.0, 0.8),
     'L1_gnn_conv_bias': (0.0, 0.1),
     'L1_gnn_ln_g': (1.0, 0.2),
     'L1_gnn_ln_b': (0.0, 0.1),
     'L1_gnn_ln1_g': (1.0, 0.2),
     'L1_gnn_ln1_b': (0.0, 0.1),
     'L1_gnn_fc_b': (0.0, 0.1),
     'L1_gnn_fc1_b': (0.0, 0.1),
     'L3_gnn_b': (0.0, 0.1)}
    factors = {'edge_attr_64': 8.0, 'L1_gnn_Wr': 8.0, 'L1_gnn_We': 8.0, 'L1_gnn_att': 8.0}
    for name, (base, spread) in spreads.items():
        noise = np.random.default_rng([zlib.crc32(name.encode()), seed]).standard_normal(out[name].shape)
        drawn = base * np.exp(spread * noise) if base else spread * noise
        out[name] = jnp.asarray(drawn.astype(out[name].dtype))
    for name, factor in factors.items():
        out[name] = (out[name] * factor).astype(out[name].dtype)
    return out
```

```python
import concourse.bass as bass
from concourse import mybir
from contextlib import ExitStack

_INS = ["x", "src", "dst", "edge_attr_64", "edge_weight", "L1_gnn_Wl", "L1_gnn_bl", "L1_gnn_Wr", "L1_gnn_br",
        "L1_gnn_We", "L1_gnn_att", "L1_gnn_conv_bias", "L1_gnn_ln_g", "L1_gnn_ln_b", "L1_gnn_ln1_g",
        "L1_gnn_ln1_b", "L1_gnn_fc_w", "L1_gnn_fc_b", "L1_gnn_fc1_w", "L1_gnn_fc1_b", "L3_gnn_W", "L3_gnn_b"]


def gnn_program(nc, x, src, dst, edge_attr, edge_weight, Wl, bl, Wr, br, We, att, conv_bias,
                ln_g, ln_b, ln1_g, ln1_b, fc_w, fc_b, fc1_w, fc1_b, W3, b3, out, STOP=None):
    f32, i32, f16 = mybir.dt.float32, mybir.dt.int32, mybir.dt.float16
    ALU = mybir.AluOpType
    ACT = mybir.ActivationFunctionType
    AX = mybir.AxisListType

    N, D = x.shape
    E = src.shape[0]
    H = att.shape[0]
    HC = H * D
    P = 128
    G = 8
    NT = 200
    NCH = NT // G
    HALF = NT // 2
    NP = 125
    NN = N // NP
    PAD = 65535
    FAR = 1 << 20
    BIG = 1.0e30
    EPS = 1e-5
    W1 = D + 1
    RW = D + 4
    full_rows, rest = E // P, E % P
    assert NP * NN == N and NT * P >= E and NT == NCH * G and D == 64 and P == 2 * D

    dstP = nc.dram_tensor("dstP", (NT * P,), f32, kind="Internal").ap()
    srcP = nc.dram_tensor("srcP", (NT * P,), f32, kind="Internal").ap()
    NY = 4
    YR = NT * P + P
    Yk = [nc.dram_tensor(f"Y{k}", (YR, D), f32, kind="Internal").ap() for k in range(NY)]
    Y = nc.dram_tensor("Y", (YR, D), f32, kind="Internal").ap()
    XT = nc.dram_tensor("XT", (N, RW), f32, kind="Internal").ap()
    T1 = nc.dram_tensor("T1", (NT * P, D), f32, kind="Internal").ap()
    T2 = nc.dram_tensor("T2", (NT * P, D), f32, kind="Internal").ap()
    FLd = nc.dram_tensor("FLd", (2, NT, W1), f32, kind="Internal").ap()
    CAd = nc.dram_tensor("CAd", (2, NT, W1), f32, kind="Internal").ap()
    SPT = -(-6 * (NT // 25) * P // W1)
    Msp = nc.dram_tensor("Msp", (P, SPT, W1), f32, kind="Internal").ap()
    SMd = nc.dram_tensor("SMd", (2, NT * H), f32, kind="Internal").ap()
    SCd = nc.dram_tensor("SCd", (2, NT * H), f32, kind="Internal").ap()

    SFd = nc.dram_tensor("SFd", (P, NT), f32, kind="Internal").ap()
    SId = nc.dram_tensor("SId", (4, P, NT), i32, kind="Internal").ap()

    top = ExitStack()

    def sb_in(stack, name, shape, dt=f32):
        return stack.enter_context(nc.sbuf_tensor(name, shape, dt))

    def ps_in(stack, name, shape, dt=f32):
        return stack.enter_context(nc.psum_tensor(name, shape, dt))

    def sem(name):
        s = nc.alloc_semaphore(name)
        phase_sems.append(s)
        return s

    phase_sems = []

    def phase():
        phase_sems.clear()
        stack = ExitStack()

        def end():
            nc.clear_and_free_semaphores(list(phase_sems))
            nc.all_engine_barrier()
        stack.callback(end)
        return stack

    def bc(ap, dim, shape):
        return ap.unsqueeze(dim).broadcast_to(shape)

    class Steps:

        def __init__(self, eng, name):
            self.eng, self.sem, self.base, self.k = eng, sem(name), 0, 0

        def __call__(self, ins):
            ins.then_inc(self.sem, 1)
            self.k += 1
            self.eng.wait_ge(self.sem, self.base + self.k)

        def chunk(self, c, per, before=0):
            self.base, self.k, self.per = c * per + before, 0, per

        def end(self):
            assert self.k == self.per, self.k

    def chunks(body):
        def run(eng):
            with eng.Fori(0, NCH // 2) as i:
                body(eng, i, 0)
                body(eng, i, 1)
            body(eng, NCH // 2, 0)
        return run

    with top:
        sb = lambda name, shape, dt=f32: sb_in(top, name, shape, dt)
        XS = sb("XS", [P, NT, D])
        XD = sb("XD", [P, NT, D])
        M = sb("M", [P, NT, W1])
        ident = sb("ident", [P, P])
        dstF = sb("dstF", [P, NT])
        repF = sb("repF", [P, NT])
        ewF = sb("ewF", [P, NT])
        dstS = sb("dstS", [P, NT], i32)
        riI = sb("riI", [P, NT], i32)
        OD = sb("OD", [P, NT])
        RC = sb("RC", [P, NT])
        RCM = sb("RCM", [P, NT])
        SFL = sb("SFL", [P, NT, 2])
        BLF = sb("BLF", [HALF, 2, NT])
        BFL = sb("BFL", [HALF, 2, NT])
        eps = sb("eps", [P, 1])
        ones = sb("ones", [1, P])
        BDc = sb("BDc", [P, P])
        BDj = sb("BDj", [P, P])
        BD2 = sb("BD2", [P, P])
        BD2g = sb("BD2g", [P, P])
        BD3 = sb("BD3", [P, P])
        biasR = sb("biasR", [1, 4, D])
        cD = sb("cD", [P, 3, D])
        WA = sb("WA", [P, HC])
        WBr = sb("WBr", [D, HC])
        WS = sb("WS", [P, HC])
        WlS = sb("WlS", [P, 3, D])
        attC = sb("attC", [P, 3, H])
        mb = sb("mb", [P, 3])
        lin = sb("lin", [P, 4, H])
        def source_columns(stack, n):
            srcF = sb_in(stack, f"srcF{n}", [P, NT])
            idY = sb_in(stack, f"idY{n}", [P, NT], i32)
            csI = sb_in(stack, f"csI{n}", [P, NT], i32)
            cdI = sb_in(stack, f"cdI{n}", [P, NT], i32)
            srcS = sb_in(stack, f"srcS{n}", [P, NT], i32)
            return srcF, idY, csI, cdI, srcS

        def move_columns(columns, out_of_chip):
            with phase(), nc.Block() as block:
                s_m = sem("mv_out" if out_of_chip else "mv_back")

                @block.sync
                def _(sp):
                    for n, col in enumerate(columns):
                        kept = SFd if n == 0 else SId[n - 1]
                        to, of = (kept, col[:, :]) if out_of_chip else (col[:, :], kept)
                        sp.dma_start(to, of).then_inc(s_m, 16)
                    sp.wait_ge(s_m, 16 * len(columns))

        columns_st = ExitStack()
        srcF, idY, csI, cdI, srcS = source_columns(columns_st, 1)
        early = ExitStack()
        srcG = sb_in(early, "srcG", [P, NT], i32)
        dstG = sb_in(early, "dstG", [P, NT], i32)
        RI = sb_in(early, "RI", [P, NT])
        CS = sb_in(early, "CS", [P, NT])
        CD = sb_in(early, "CD", [P, NT])
        tab_st = ExitStack()
        TAB = sb_in(tab_st, "TAB", [P, 3, NN])

        def bias8(n, a=0):
            return biasR[0:1, n, :].unsqueeze(1).broadcast_to([1, G, D])

        def load_rows(eng, to, of, count, s):
            rows, last = count // P, count % P
            eng.dma_start(to[0:HALF, 0, :], of[0:HALF * P].rearrange("(p j) -> p j", j=P)).then_inc(s, 16)
            eng.dma_start(to[0:rows - HALF, 1, :],
                          of[HALF * P:rows * P].rearrange("(p j) -> p j", j=P)).then_inc(s, 16)
            eng.dma_start(to[rows - HALF:rows - HALF + 1, 1, 0:last],
                          of[rows * P:count].rearrange("(p j) -> p j", p=1)).then_inc(s, 16)

        def borrowed():
            flat = XS[:, :, :].rearrange("p t d -> p (t d)")
            used = [0]

            def room(shape):
                n = 1
                for v in shape[1:]:
                    n *= v
                ap = flat[0:shape[0], used[0]:used[0] + n]
                used[0] += n
                assert used[0] <= NT * D
                names = "abc"[:len(shape) - 1]
                return ap if len(shape) == 2 else ap.rearrange(
                    f"p ({' '.join(names)}) -> p {' '.join(names)}", **dict(zip(names[1:], shape[2:])))
            return room

        def setup():
            st = phase()
            with st:
                t = lambda name, shape, dt=f32: sb_in(st, name, shape, dt)
                rI = t("rI", [HALF, 3, 2, P], i32)
                room = borrowed()
                rF = room([HALF, 5, 2, P])
                kb = room([HALF, 2, 2, P])
                kFr = room([P, NT])
                kLr = room([P, NT])
                bd = room([P, 3, NT])
                wl = room([D, H, D]); wr = room([D, H, D])
                fw = room([D, P]); fwT = room([P, D]); f1 = room([P, D])
                fbc = room([P, 1]); gcol = room([D, 1]); bcol = room([D, 1])
                w = room([D, 6, D]); wst = room([D, 4, 1])
                w3 = room([D, D])
                rows = room([1, 8, D]); blr = room([1, H, D]); rst = room([1, 4])
                bcolsl = room([P, 3]); bcolsr = room([P, 3])
                g1b = room([P, D])
                b3b = room([P, D])
                b1b = room([P, D])
                brr = room([1, H, D])
                attb, prod = XD[:, 0:H, :], XD[:, H:2 * H, :]
                pI = ps_in(st, "pI", [P, 4, 512])
                pK = ps_in(st, "pK", [P, 2, 512])
                pW = ps_in(st, "pW", [P, 2, 512])
                s_zero = sem("su_zero"); s_in = sem("su_in"); s_w = sem("su_w")
                s_fl = sem("su_floats"); s_id = sem("su_ident"); s_tp = sem("su_transposed")
                s_kb = sem("su_keys"); s_kr = sem("su_keyrows"); s_b = sem("su_masks"); s_out = sem("su_out")
                s_w1 = sem("su_w1"); s_w2 = sem("su_w2"); s_w3 = sem("su_w3"); s_w4 = sem("su_w4")
                with nc.Block() as block:
                    @block.sync
                    def _(sp):
                        sp.wait_ge(s_zero, 1)
                        load_rows(sp, rI[:, 0], src, E, s_in)
                        load_rows(sp, rI[:, 1], dst, E, s_in)
                        load_rows(sp, rI[:, 2], dst[1:E], E - 1, s_in)
                        load_rows(sp, rF[:, 3], edge_weight, E, s_in)
                        sp.wait_ge(s_fl, 1)
                        sp.dma_start(dstP.rearrange("(c p j) -> p c j", c=2, j=P), rF[:, 1]).then_inc(s_out, 16)
                        sp.dma_start(srcP.rearrange("(c p j) -> p c j", c=2, j=P), rF[:, 0]).then_inc(s_out, 16)
                        sp.wait_ge(s_out, 32)

                    @block.scalar
                    def _(act):
                        def ld(to, of):
                            act.dma_start(to, of).then_inc(s_w, 16)
                        row = lambda v: v.rearrange("(a n) -> a n", a=1)
                        col = lambda v: v.rearrange("(n a) -> n a", a=1)
                        act.wait_ge(s_zero, 1)
                        ld(wl[:, :, :], Wl.rearrange("k (h c) -> k h c", h=H))
                        ld(wr[:, :, :], Wr.rearrange("k (h c) -> k h c", h=H))
                        ld(WA[0:D, :], Wl); ld(WA[D:P, :], We); ld(WBr[:, :], Wr)
                        ld(WS[D:P, :], We)
                        ld(fw[:, :], fc_w); ld(f1[:, :], fc1_w); ld(w3[:, :], W3)
                        ld(fbc[:, :], col(fc_b)); ld(gcol[:, :], col(ln_g)); ld(bcol[:, :], col(ln_b))
                        ld(blr[:, :, :], bl.rearrange("(a h c) -> a h c", a=1, h=H))
                        ld(rows[:, 0, :], row(conv_bias)); ld(rows[:, 1, :], row(fc1_b))
                        ld(rows[:, 2, :], row(ln1_g)); ld(rows[:, 3, :], row(b3))
                        for h in range(H):
                            lo = D * (h % 2)
                            ld(attC[lo:lo + D, h // 2, h:h + 1], att[h:h + 1, :].rearrange("a c -> c a"))
                            ld(bcolsl[lo:lo + D, h // 2:h // 2 + 1], col(bl[h * D:(h + 1) * D]))
                            ld(bcolsr[lo:lo + D, h // 2:h // 2 + 1], col(br[h * D:(h + 1) * D]))
                            ld(WlS[lo:lo + D, h // 2, :], Wl[:, h * D:(h + 1) * D])
                        ld(attb, att.rearrange("(a h) c -> a h c", a=1).broadcast_to([P, H, D]))
                        ld(brr[:, :, :], br.rearrange("(a h c) -> a h c", a=1, h=H))
                        ld(g1b[:, :], row(ln1_g).broadcast_to([P, D]))
                        ld(b1b[:, :], row(ln1_b).broadcast_to([P, D]))
                        ld(b3b[:, :], row(b3).broadcast_to([P, D]))
                    NLOAD = 22 + 4 * H

                    @block.gpsimd
                    def _(pool):
                        pool.memset(ident[:, :], 0.0).then_inc(s_id, 1)
                        pool.wait_ge(s_id, 1)
                        pool.affine_select(out=ident[:, :], in_=ident[:, :], compare_op=ALU.not_equal, fill=1.0,
                                           base=0, pattern=[[-1, P]], channel_multiplier=1).then_inc(s_id, 1)
                        pool.wait_ge(s_b, 1)
                        for c in range(2):
                            pool.affine_select(out=BLF[:, c, :], in_=BLF[:, c, :], compare_op=ALU.is_gt, fill=0.0,
                                               base=-c * HALF, pattern=[[1, NT]], channel_multiplier=-1)
                            pool.affine_select(out=BFL[:, c, :], in_=BFL[:, c, :], compare_op=ALU.is_gt, fill=0.0,
                                               base=c * HALF, pattern=[[-1, NT]], channel_multiplier=1)

                    @block.vector
                    def _(dve):
                        step = Steps(dve, "su_dve")
                        dve.memset(rI[:, 0:2], PAD)
                        dve.memset(rI[:, 2], -1)
                        dve.memset(rF[:, 3], 0.0)
                        dve.memset(attC[:, :, :], 0.0)
                        dve.memset(mb[:, :], 0.0)
                        dve.memset(bcolsl[:, :], 0.0)
                        dve.memset(bcolsr[:, :], 0.0)
                        dve.memset(WlS[:, :, :], 0.0)
                        dve.memset(eps[:, :], EPS)
                        dve.memset(ones[:, :], 1.0)
                        for b_ in (BDc, BDj, BD2, BD2g, BD3):
                            dve.memset(b_[:, :], 0.0)
                        step(dve.memset(rF[:, 4], 0.0))
                        dve.sem_inc(s_zero, 1)
                        dve.wait_ge(s_in, 16 * 12)
                        step(dve.tensor_copy(rF[:, 0:3].rearrange("p a c j -> p (a c j)"),
                                             rI[:, :].rearrange("p a c j -> p (a c j)")))
                        dve.sem_inc(s_fl, 1)
                        for k, end in enumerate((0, P - 1)):
                            for c in range(2):
                                dve.tensor_copy(kb[:, k, c, :],
                                                rF[:, 1, c, end:end + 1].broadcast_to([HALF, P]))
                        step(dve.tensor_tensor(rF[:, 4].rearrange("p c j -> p (c j)"),
                                               rF[:, 1].rearrange("p c j -> p (c j)"),
                                               rF[:, 2].rearrange("p c j -> p (c j)"), ALU.not_equal))
                        dve.sem_inc(s_kb, 1)
                        dve.wait_ge(s_tp, 1)
                        for n, to in enumerate((srcF, dstF, ewF, repF)):
                            dve.tensor_copy(to[:, :], pI[:, n, 0:NT])
                        dve.tensor_copy(kFr[:, :], pK[:, 0, 0:NT])
                        step(dve.tensor_copy(kLr[:, :], pK[:, 1, 0:NT]))
                        for c in range(2):
                            dve.tensor_scalar(BLF[:, c, :], kFr[0:HALF, :], rF[:, 1, c, P - 1:P], None, ALU.is_equal)
                            dve.tensor_scalar(BFL[:, c, :], kLr[0:HALF, :], rF[:, 1, c, 0:1], None, ALU.is_equal)
                        dve.tensor_tensor(SFL[:, :, 0], dstF[:, :], kFr[:, :], ALU.is_equal)
                        step(dve.tensor_tensor(SFL[:, :, 1], dstF[:, :], kLr[:, :], ALU.is_equal))
                        dve.sem_inc(s_b, 1)
                        for f, g in ((srcF, srcG), (dstF, dstG)):
                            step(dve.tensor_scalar(bd[:, 0, :], f[:, :], float(N), None, ALU.is_lt))
                            step(dve.tensor_tensor(bd[:, 1, :], bd[:, 0, :], f[:, :], ALU.mult))
                            step(dve.tensor_copy(g[:, :], bd[:, 1, :]))
                        step(dve.tensor_scalar(bd[:, 0, :], repF[:, :], -float(FAR), float(FAR), ALU.mult, ALU.add))
                        step(dve.tensor_tensor(bd[:, 1, :], bd[:, 0, :], dstF[:, :], ALU.add))
                        step(dve.tensor_copy(dstS[:, :], bd[:, 1, :]))
                        dve.wait_ge(s_w, 16 * NLOAD)
                        dve.wait_ge(s_id, 2)
                        I64 = ident[0:D, 0:D]

                        def centre(ap, acc):
                            step(dve.tensor_reduce(acc, ap, AX.X, ALU.add))
                            step(dve.tensor_scalar(acc, acc, -1.0 / D, None, ALU.mult))
                            step(dve.tensor_scalar(ap, ap, acc, None, ALU.add))

                        def mean_heads(to, of):
                            step(dve.tensor_tensor(to, of[:, 0, :], of[:, 1, :], ALU.add))
                            for h in range(2, H):
                                step(dve.tensor_tensor(to, to, of[:, h, :], ALU.add))
                            step(dve.tensor_scalar(to, to, 1.0 / H, None, ALU.mult))

                        def diagonal(bd_, ap):
                            dve.tensor_copy(bd_[0:D, 0:D], ap)
                            step(dve.tensor_copy(bd_[D:P, D:P], ap))

                        mean_heads(w[:, 0, :], wl)
                        step(dve.tensor_tensor(w[:, 0, :], w[:, 0, :], I64, ALU.add))
                        centre(w[:, 0, :], wst[:, 0, :])
                        diagonal(BDc, w[:, 0, :])
                        step(dve.tensor_copy(w[:, 1, :], I64))
                        centre(w[:, 1, :], wst[:, 1, :])
                        diagonal(BDj, w[:, 1, :])
                        diagonal(BD3, w3[:, :])
                        mean_heads(rows[:, 4, :], blr)
                        step(dve.tensor_tensor(rows[:, 4, :], rows[:, 4, :], rows[:, 0, :], ALU.add))
                        centre(rows[:, 4, :], rst[:, 0:1])
                        for k in range(3):
                            centre(WlS[:, k, :], bd[:, 2, k:k + 1])
                        step(dve.tensor_tensor(WS[0:D, :], wl[:, :, :].rearrange("k h c -> k (h c)"),
                                               wr[:, :, :].rearrange("k h c -> k (h c)"), ALU.add))
                        step(dve.tensor_scalar(attC[:, :, :], attC[:, :, :], 0.8, None, ALU.mult))
                        step(dve.tensor_scalar(attb, attb, 0.2, None, ALU.mult))
                        step(dve.tensor_tensor(brr[:, :, :], brr[:, :, :], blr[:, :, :], ALU.add))
                        heads = lambda a: a.rearrange("k (h c) -> k h c", h=H)
                        for n, (of, p_) in enumerate(((heads(WA[:, :]), P), (heads(WBr[:, :]), D),
                                                      (heads(WS[:, :]), P), (brr[:, :, :], 1))):
                            step(dve.tensor_tensor(prod[0:p_], of, attb[0:p_], ALU.mult))
                            step(dve.tensor_reduce(lin[0:p_, n, :], prod[0:p_], AX.X, ALU.add))
                        step(dve.tensor_tensor(mb[:, :], bcolsl[:, :], bcolsr[:, :], ALU.add))
                        dve.tensor_copy(cD[:, 0, :], b1b[:, :])
                        step(dve.tensor_scalar(cD[:, 2, :], b3b[:, :], 0.0, None, ALU.max))
                        step(dve.tensor_tensor(cD[:, 1, :], cD[:, 2, :], b1b[:, :], ALU.add))
                        dve.wait_ge(s_w1, 1)
                        step(dve.tensor_copy(fwT[:, :], pW[:, 0, 0:D]))
                        dve.sem_inc(s_w2, 1)
                        dve.wait_ge(s_w1, 2)
                        step(dve.tensor_tensor(w[:, 2, :], pW[0:D, 0, D:P], I64, ALU.add))
                        dve.sem_inc(s_w2, 1)
                        dve.wait_ge(s_w1, 3)
                        step(dve.tensor_tensor(rows[:, 5, :], pW[0:1, 1, 0:D], rows[:, 1, :], ALU.add))
                        centre(rows[:, 5, :], rst[:, 1:2])
                        step(dve.tensor_tensor(rows[:, 6, :], rows[:, 5, :], rows[:, 2, :], ALU.mult))
                        centre(w[:, 2, :], wst[:, 2, :])
                        step(dve.tensor_scalar(w[:, 3, :], w[:, 2, :], gcol[:, :], None, ALU.mult))
                        diagonal(BD2, w[:, 3, :])
                        step(dve.tensor_tensor(w[:, 4, :], w[:, 3, :], g1b[0:D, :], ALU.mult))
                        diagonal(BD2g, w[:, 4, :])
                        for n, r in enumerate((4, 5, 6, 3)):
                            step(dve.tensor_copy(biasR[:, n, :], rows[:, r, :]))

                    @block.tensor
                    def _(pe):
                        pe.wait_ge(s_id, 2)
                        pe.wait_ge(s_kb, 1)
                        for n, r in enumerate((0, 1, 3, 4)):
                            for c in range(2):
                                pe.transpose(pI[:, n, c * HALF:(c + 1) * HALF], rF[:, r, c, :],
                                             ident[0:HALF, 0:HALF])
                        for k in range(2):
                            for c in range(2):
                                last = pe.matmul(pK[:, k, c * HALF:(c + 1) * HALF], kb[:, k, c, :],
                                                 ident[0:HALF, 0:HALF], start=True, stop=True)
                        last.then_inc(s_tp, 1)
                        pe.wait_ge(s_w, 16 * NLOAD)
                        pe.transpose(pW[:, 0, 0:D], fw[:, :], ident[0:D, 0:D]).then_inc(s_w1, 1)
                        pe.wait_ge(s_w2, 1)
                        pe.matmul(pW[0:D, 0, D:P], fwT[:, :], f1[:, :], start=True, stop=True).then_inc(s_w1, 1)
                        pe.wait_ge(s_w2, 2)
                        pe.matmul(pW[0:1, 1, 0:D], fbc[:, :], f1[:, :], start=True, stop=False)
                        pe.matmul(pW[0:1, 1, 0:D], bcol[:, :], w[:, 2, :], start=False, stop=True).then_inc(s_w1, 1)

        setup()

        def gather_setup(st, name, width, slots=2):
            return dict(ring=sb_in(st, name + "_ring", [P, slots, G, width]),
                        idx=sb_in(st, name + "_idx", [P, slots, G], i32),
                        sems=[sem(f"{name}_rows{u}") for u in range(slots)], free=sem(name + "_free"),
                        pool=sem(name + "_pool"), go=sem(name + "_go"), width=width)

        def gather_chunk(pool, i, u, g, table, index, bound, old=None):
            c = i * 2 + u
            per = 2 if old is not None else 1
            pool.wait_ge(g["free"], c + 1)
            pool.wait_ge(g["sems"][u], i * (16 * G))
            pool.tensor_copy(g["idx"][:, u, :], index[:, bass.ds(c * G, G)]).then_inc(g["pool"], 1)
            if old is not None:
                was = old[:, bass.ds(c * G, G), :] if old.shape[1] == NT else old[:, :, :]
                pool.tensor_copy(g["ring"][:, u, :, :], was).then_inc(g["pool"], 1)
            pool.wait_ge(g["pool"], c * per + per)
            pool.sem_inc(g["go"], 1)
            for j in range(G):
                pool.indirect_dma_start(
                    out=g["ring"][:, u, j, :], out_offset=None, in_=table,
                    in_offset=bass.IndirectOffsetOnAxis(ap=g["idx"][:, u, j:j + 1], axis=0),
                    bounds_check=bound, oob_is_err=False).then_inc(g["sems"][u], 16)

        def tables():
            st = phase()
            with st:
                t = lambda name, shape, dt=f32: sb_in(st, name, shape, dt)
                iN = t("iN", [P, NN], i32); loI = t("loI", [P, NN], f16)
                iH = t("iH", [P, P], i32); hiI = t("hiI", [P, P], f16)
                iT = t("iT", [P, NT], i32); iP = t("iP", [P, NT], i32)
                room = borrowed()
                tnum = room([P, NT]); pnum = room([P, NT])
                hi32 = t("hi32", [P, NT], i32)
                hi = room([P, 2, NT]); lo = room([P, 2, NT]); tmp = room([P, NT])
                U = 2
                ohl = t("ohl", [P, 2, U, 2, NN], f16)
                ohh = t("ohh", [P, 2, U, 3, P], f16)
                pT = ps_in(st, "pT", [P, 3, 512])
                lower = t("lower", [P, NP]); total = t("total", [P, 1]); offs = t("offs", [P, 1])
                has = room([P, 2, NN])
                pO = ps_in(st, "pO", [P, 512])
                s_lo = sem("tb_lower"); s_tot = sem("tb_total"); s_of = sem("tb_offsets")
                s_z = sem("tb_zero"); s_y = sem("tb_yzero")
                s_i = sem("tb_iota"); s_oh = sem("tb_onehots"); s_fr = sem("tb_free"); s_t = sem("tb_tables")
                TURNS = NT // U // 2
                with nc.Block() as block:
                    @block.gpsimd
                    def _(pool):
                        pool.iota(iN[:, :], [[1, NN]], channel_multiplier=0)
                        pool.iota(iH[:, :], [[1, P]], channel_multiplier=0)
                        pool.iota(iT[:, :], [[1, NT]], channel_multiplier=0)
                        pool.iota(iP[:, :], [[0, NT]], base=1, channel_multiplier=1).then_inc(s_i, 1)
                        pool.memset(lower[:, :], 1.0).then_inc(s_lo, 1)
                        pool.wait_ge(s_lo, 1)
                        pool.affine_select(out=lower[:, :], in_=lower[:, :], compare_op=ALU.is_gt, fill=0.0,
                                           base=0, pattern=[[1, NP]], channel_multiplier=-1).then_inc(s_lo, 1)

                    @block.sync
                    def _(sp):
                        sp.wait_ge(s_z, 1)
                        zeros = M[:, :, :].rearrange("p t d -> p (t d)")[:, 0:YR // P * D]
                        for k in range(NY):
                            sp.dma_start(Yk[k].rearrange("(p r) d -> p (r d)", p=P), zeros).then_inc(s_y, 16)
                        sp.wait_ge(s_y, 16 * NY)

                    @block.vector
                    def _(dve):
                        step = Steps(dve, "tb_dve")
                        step(dve.memset(M[:, :, :], 0.0))
                        dve.sem_inc(s_z, 1)
                        dve.wait_ge(s_i, 1)
                        dve.tensor_copy(loI[:, :], iN[:, :])
                        dve.tensor_copy(hiI[:, :], iH[:, :])
                        dve.tensor_copy(tnum[:, :], iT[:, :])
                        step(dve.tensor_copy(pnum[:, :], iP[:, :]))
                        for k, f in enumerate((srcF, dstF)):
                            step(dve.tensor_scalar(tmp[:, :], f[:, :], (1.0 - NN) / 2, 1.0 / NN, ALU.add, ALU.mult))
                            step(dve.tensor_copy(hi32[:, :], tmp[:, :]))
                            step(dve.tensor_copy(hi[:, k, :], hi32[:, :]))
                            step(dve.tensor_scalar(tmp[:, :], hi[:, k, :], -float(NN), None, ALU.mult))
                            step(dve.tensor_tensor(lo[:, k, :], tmp[:, :], f[:, :], ALU.add))
                        step(dve.tensor_tensor(tnum[:, :], tnum[:, :], repF[:, :], ALU.mult))
                        step(dve.tensor_tensor(pnum[:, :], pnum[:, :], repF[:, :], ALU.mult))

                        def body(i, u):
                            c = i * 2 + u
                            dve.wait_ge(s_fr, c + 1)
                            for j in range(U):
                                t_ = c * U + j
                                for k in range(2):
                                    dve.tensor_scalar(ohl[:, u, j, k, :], loI[:, :], lo[:, k, bass.ds(t_, 1)],
                                                      None, ALU.is_equal)
                                dve.tensor_scalar(ohh[:, u, j, 0, :], hiI[:, :], hi[:, 0, bass.ds(t_, 1)],
                                                  None, ALU.is_equal)
                                dve.tensor_scalar(ohh[:, u, j, 1, :], hiI[:, :], hi[:, 1, bass.ds(t_, 1)],
                                                  tnum[:, bass.ds(t_, 1)], ALU.is_equal, ALU.mult)
                                last = dve.tensor_scalar(ohh[:, u, j, 2, :], hiI[:, :], hi[:, 1, bass.ds(t_, 1)],
                                                         pnum[:, bass.ds(t_, 1)], ALU.is_equal, ALU.mult)
                            last.then_inc(s_oh, 1)
                        with dve.Fori(0, TURNS) as i:
                            body(i, 0)
                            body(i, 1)
                        dve.wait_ge(s_t, 1)
                        dve.tensor_copy(TAB[:, 1, :], pT[:, 0, 0:NN])
                        step(dve.tensor_scalar(TAB[:, 2, :], pT[:, 1, 0:NN], float(P), None, ALU.mult))
                        step(dve.tensor_tensor(TAB[:, 0, :], pT[:, 2, 0:NN], TAB[:, 2, :], ALU.add))
                        step(dve.tensor_scalar(has[:, 0, :], TAB[:, 1, :], 0.0, None, ALU.is_gt))
                        step(dve.memset(has[:, 1, :], 1.0))
                        step(dve.tensor_tensor_scan(TAB[:, 2, :], has[:, 1, :], has[:, 0, :], 0.0, ALU.mult, ALU.add))
                        step(dve.tensor_copy(total[:, :], TAB[:, 2, NN - 1:NN]))
                        dve.sem_inc(s_tot, 1)
                        dve.wait_ge(s_of, 1)
                        step(dve.tensor_copy(offs[0:NP, :], pO[0:NP, 0:1]))
                        step(dve.tensor_scalar(TAB[0:NP, 2, :], TAB[0:NP, 2, :], offs[0:NP, :], -1.0, ALU.add, ALU.add))
                        step(dve.tensor_scalar(has[:, 1, :], has[:, 0, :], -float(FAR), float(FAR), ALU.mult, ALU.add))
                        step(dve.tensor_tensor(TAB[:, 2, :], TAB[:, 2, :], has[:, 1, :], ALU.add))

                    @block.tensor
                    def _(pe):
                        pe.sem_inc(s_fr, 2)
                        def body(i, u, first=False, stop=False):
                            c = i * 2 + u
                            pe.wait_ge(s_oh, c + 1)
                            for j in range(U):
                                for n, (a, b) in enumerate(((0, 0), (1, 1), (2, 1))):
                                    last = pe.matmul(pT[:, n, 0:NN], ohh[:, u, j, a, :], ohl[:, u, j, b, :],
                                                     start=first and j == 0, stop=stop and j == U - 1)
                            last.then_inc(s_fr, 1)
                            return last
                        body(0, 0, first=True)
                        body(0, 1)
                        with pe.Fori(1, TURNS - 1) as i:
                            body(i, 0)
                            body(i, 1)
                        body(TURNS - 1, 0)
                        body(TURNS - 1, 1, stop=True)
                        pe.wait_ge(s_fr, 2 * TURNS + 2)
                        pe.sem_inc(s_t, 1)
                        pe.wait_ge(s_lo, 2)
                        pe.wait_ge(s_tot, 1)
                        pe.matmul(pO[0:NP, 0:1], lower[0:NP, :], total[0:NP, :], start=True, stop=True).then_inc(s_of, 1)

        tables()

        NB = NN // (2 * G)
        assert NB == NCH
        x_v = x.rearrange("(p n) d -> p n d", p=NP)
        out_v = out.rearrange("(p n) d -> p n d", p=NP)
        XT_v = XT.rearrange("(p n) d -> p n d", p=NP)
        CUT = 112

        def node_dma(eng, to, of, s):
            eng.dma_start(to[0:CUT], of[0:CUT]).then_inc(s, 16)
            eng.dma_start(to[CUT:NP], of[CUT:NP]).then_inc(s, 16)

        def widen():
            st = phase()
            with st:
                W = sb_in(st, "wd_W", [P, 2, 2 * G, RW])
                s_l = [sem(f"wd_load{u}") for u in range(2)]; s_s = [sem(f"wd_store{u}") for u in range(2)]
                s_z = sem("wd_zero"); s_c = sem("wd_cols")
                with nc.Block() as block:
                    @block.vector
                    def _(dve):
                        dve.memset(W[:, :, :, D + 3:RW], 0.0).then_inc(s_z, 1)
                        def body(eng, i, u):
                            c = i * 2 + u
                            eng.wait_ge(s_s[u], i * 32)
                            for k in range(3):
                                last = eng.tensor_scalar(W[:, u, :, D + k], TAB[:, k, bass.ds(c * 2 * G, 2 * G)],
                                                         1.0, None, ALU.mult)
                            last.then_inc(s_c, 1)
                        chunks(body)(dve)

                    @block.sync
                    def _(sp):
                        def body(eng, i, u):
                            c = i * 2 + u
                            eng.wait_ge(s_s[u], i * 32)
                            node_dma(eng, W[0:NP, u, :, 0:D], x_v[:, bass.ds(c * 2 * G, 2 * G), :], s_l[u])
                        chunks(body)(sp)

                    @block.scalar
                    def _(act):
                        act.wait_ge(s_z, 1)
                        def body(eng, i, u):
                            c = i * 2 + u
                            eng.wait_ge(s_c, c + 1)
                            eng.wait_ge(s_l[u], (i + 1) * 32)
                            node_dma(eng, XT_v[:, bass.ds(c * 2 * G, 2 * G), :], W[0:NP, u, :, :], s_s[u])
                        chunks(body)(act)
                        act.wait_ge(s_s[0], 32 * (NCH // 2 + 1))
                        act.wait_ge(s_s[1], 32 * (NCH // 2))

        widen()
        tab_st.close()

        def norm_setup(st, name, tiles, xc=None, sq=None):
            return dict(s=sb_in(st, name + "_s", [P, 4, tiles]),
                        xc=sb_in(st, name + "_xc", [P, tiles, D]) if xc is None else xc,
                        sq=sb_in(st, name + "_sq", [P, tiles, D]) if sq is None else sq, v=sem(name + "_var"), sd=sem(name + "_sd"))

        NORM_STEPS = 5

        def norm_dve(dve, step, n, c, xin, emit, p=P, tiles=G, w=0):
            s, xc, sq = n["s"], n["xc"], n["sq"]
            step(dve.tensor_reduce(s[0:p, 0, :], xin, AX.X, ALU.add))
            step(dve.tensor_scalar(s[0:p, 1, :], s[0:p, 0, :], -1.0 / D, None, ALU.mult))
            step(dve.tensor_tensor(xc[0:p], xin, bc(s[0:p, 1, :], 2, [p, tiles, D]), ALU.add))
            step(dve.tensor_tensor(sq[0:p], xc[0:p], xc[0:p], ALU.mult))
            dve.tensor_reduce(s[0:p, 2, :], sq[0:p], AX.X, ALU.add).then_inc(n["v"], 1)
            dve.wait_ge(n["sd"], w + 1)
            step(dve.reciprocal(s[0:p, 0, :], s[0:p, 3, :]))
            emit(xc[0:p], bc(s[0:p, 0, :], 2, [p, tiles, D]))

        def norm_act(act, n, p=P, w=0):
            act.wait_ge(n["v"], w + 1)
            act.activation(n["s"][0:p, 3, :], n["s"][0:p, 2, :], ACT.Sqrt, bias=eps[0:p, 0:1],
                           scale=1.0 / D).then_inc(n["sd"], 1)

        def relu_into(dve, to):
            return lambda xc, r: dve.scalar_tensor_tensor(to, xc, 0.0, r, ALU.max, ALU.mult)

        def tail_setup(st, name):
            return dict(hT=sb_in(st, name + "_hT", [P, 4, P]), n=sb_in(st, name + "_n", [P, G, D]),
                        nT=sb_in(st, name + "_nT", [P, 4, P]), sq=sb_in(st, name + "_sq", [P, G, D]),
                        s=sb_in(st, name + "_s", [P, 6, G]), t=sb_in(st, name + "_t", [P, G, D]),
                        pt=ps_in(st, name + "_pt", [P, 512]), py=ps_in(st, name + "_py", [P, 512]),
                        pz=ps_in(st, name + "_pz", [P, 512]), pg=ps_in(st, name + "_pg", [P, 512]),
                        h=sem(name + "_h"), ht=sem(name + "_ht"), hT_=sem(name + "_hTr"), y=sem(name + "_y"),
                        sqd=sem(name + "_sqd"), v=sem(name + "_v"), sd=sem(name + "_sd"), nn=sem(name + "_n"),
                        nt=sem(name + "_nt"), nT_=sem(name + "_nTr"), z=sem(name + "_z"), done=sem(name + "_done"))

        TAIL_STEPS = 4

        def tail_pe(pe, q, w, h, weights, p=P, extra=None):
            pe.wait_ge(q["h"], w + 1)
            pe.wait_ge(q["done"], w + 1)
            for j in range(4):
                last = pe.transpose(q["pt"][:, j * P:j * P + p],
                                    h[0:p, 2 * j:2 * j + 2, :].rearrange("p a d -> p (a d)"), ident[0:p, 0:p])
            last.then_inc(q["ht"], 1)
            pe.wait_ge(q["hT_"], w + 1)
            pe.matmul(q["py"][0:p, :], ones[0:1, 0:p], bias8(0),
                      start=True, stop=False)
            for j in range(4):
                last = pe.matmul(q["py"][0:p, j * P:(j + 1) * P], q["hT"][:, j, 0:p], weights[:, :],
                                 start=False, stop=extra is None and j == 3)
            if extra is not None:
                last = extra()
            last.then_inc(q["y"], 1)
            pe.wait_ge(q["nn"], w + 1)
            for j in range(4):
                last = pe.transpose(q["pt"][:, j * P:j * P + p],
                                    q["n"][0:p, 2 * j:2 * j + 2, :].rearrange("p a d -> p (a d)"), ident[0:p, 0:p])
            last.then_inc(q["nt"], 1)
            pe.wait_ge(q["nT_"], w + 1)
            for to, b, wt in ((q["pz"], 1, BD2), (q["pg"], 2, BD2g)):
                pe.matmul(to[0:p, :], ones[0:1, 0:p], bias8(b),
                          start=True, stop=False)
                for j in range(4):
                    last = pe.matmul(to[0:p, j * P:(j + 1) * P], q["nT"][:, j, 0:p], wt[:, :],
                                     start=False, stop=j == 3)
            last.then_inc(q["z"], 1)

        def tail_act(act, q, w, p=P):
            g3 = lambda a: a[0:p, :].rearrange("p (g d) -> p g d", d=D)
            c3 = lambda a: a[:, :].rearrange("q (j p) -> q j p", p=P)[:, :, 0:p]
            act.wait_ge(q["ht"], w + 1)
            act.activation(q["hT"][:, :, 0:p], c3(q["pt"]), ACT.Copy).then_inc(q["hT_"], 1)
            act.wait_ge(q["y"], w + 1)
            act.activation(q["sq"][0:p], g3(q["py"]), ACT.Square).then_inc(q["sqd"], 1)
            act.wait_ge(q["v"], 2 * w + 1)
            act.activation(q["s"][0:p, 1, :], q["s"][0:p, 0, :], ACT.Sqrt, bias=eps[0:p, 0:1],
                           scale=1.0 / D).then_inc(q["sd"], 1)
            act.wait_ge(q["nt"], w + 1)
            act.activation(q["nT"][:, :, 0:p], c3(q["pt"]), ACT.Copy).then_inc(q["nT_"], 1)
            act.wait_ge(q["z"], w + 1)
            act.activation(q["sq"][0:p], g3(q["pz"]), ACT.Square).then_inc(q["sqd"], 1)
            act.wait_ge(q["v"], 2 * w + 2)
            act.activation(q["s"][0:p, 4, :], q["s"][0:p, 3, :], ACT.Sqrt, bias=eps[0:p, 0:1],
                           scale=1.0 / D).then_inc(q["sd"], 1)

        def tail_dve(dve, step, q, w, xin, to, const, p=P):
            g3 = lambda a: a[0:p, :].rearrange("p (g d) -> p g d", d=D)
            s = q["s"]
            dve.wait_ge(q["sqd"], 2 * w + 1)
            dve.tensor_reduce(s[0:p, 0, :], q["sq"][0:p], AX.X, ALU.add).then_inc(q["v"], 1)
            dve.wait_ge(q["sd"], 2 * w + 1)
            step(dve.reciprocal(s[0:p, 2, :], s[0:p, 1, :]))
            dve.tensor_tensor(q["n"][0:p], g3(q["py"]), bc(s[0:p, 2, :], 2, [p, G, D]), ALU.mult).then_inc(q["nn"], 1)
            dve.wait_ge(q["sqd"], 2 * w + 2)
            dve.tensor_reduce(s[0:p, 3, :], q["sq"][0:p], AX.X, ALU.add).then_inc(q["v"], 1)
            dve.wait_ge(q["sd"], 2 * w + 2)
            step(dve.reciprocal(s[0:p, 5, :], s[0:p, 4, :]))
            step(dve.tensor_tensor(q["t"][0:p], g3(q["pg"]), bc(s[0:p, 5, :], 2, [p, G, D]), ALU.mult))
            dve.sem_inc(q["done"], 1)
            step(dve.tensor_tensor(q["t"][0:p], q["t"][0:p], bc(cD[0:p, const, :], 1, [p, G, D]), ALU.add))
            return dve.tensor_tensor(to, q["t"][0:p], xin, ALU.add)

        def dense():
            st = phase()
            with st:
                g1 = gather_setup(st, "g1", RW)
                g0 = gather_setup(st, "g0", RW)
                XR = M[:, :, :].rearrange("p t d -> p (t d)")[:, 0:8 * G * D]\
                    .rearrange("p (a u g d) -> p a u g d", a=2, u=2, d=D)
                X, R = XR[:, 0], XR[:, 1]
                h = sb_in(st, "dn_h", [P, G, D])
                nm = norm_setup(st, "dn_norm", G)
                q = tail_setup(st, "dn_tail")
                s_l = [sem(f"dn_load{u}") for u in range(2)]; s_st = [sem(f"dn_store{u}") for u in range(2)]
                s_x = sem("dn_xfree"); s_r = sem("dn_result"); s_cp = sem("dn_copied")
                with nc.Block() as block:
                    @block.gpsimd
                    def _(pool):
                        last_row = pool.to_reg(N - 1)
                        def body(eng, i, u):
                            gather_chunk(eng, i, u, g1, XT, srcG, last_row)
                            gather_chunk(eng, i, u, g0, XT, dstG, last_row)
                        chunks(body)(pool)

                    @block.sync
                    def _(sp):
                        def body(eng, i, u):
                            c = i * 2 + u
                            eng.wait_ge(s_x, c + 1)
                            node_dma(eng, X[0:NP, u], x_v[:, bass.ds(c * 2 * G, 2 * G), :], s_l[u])
                            if u:
                                store(eng, c - 1, i, 0)
                        def store(eng, c, i, u):
                            eng.wait_ge(s_r, c + 1)
                            node_dma(eng, out_v[:, bass.ds(c * 2 * G, 2 * G), :], R[0:NP, u], s_st[u])
                        with sp.Fori(0, NCH // 2) as i:
                            for u in range(2):
                                sp.wait_ge(s_x, i * 2 + u + 1)
                                node_dma(sp, X[0:NP, u], x_v[:, bass.ds((i * 2 + u) * 2 * G, 2 * G), :], s_l[u])
                            for u in range(2):
                                store(sp, i * 2 + u, i, u)
                        sp.wait_ge(s_x, NCH)
                        node_dma(sp, X[0:NP, 0], x_v[:, (NCH - 1) * 2 * G:NCH * 2 * G, :], s_l[0])
                        store(sp, NCH - 1, NCH // 2, 0)
                        sp.wait_ge(s_st[0], 32 * (NCH // 2 + 1))
                        sp.wait_ge(s_st[1], 32 * (NCH // 2))

                    @block.vector
                    def _(dve):
                        step = Steps(dve, "dn_dve")
                        dve.sem_inc(s_x, 2)
                        dve.sem_inc(q["done"], 1)
                        def body(eng, i, u):
                            c = i * 2 + u
                            eng.wait_ge(s_l[u], (i + 1) * 32)
                            eng.wait_ge(s_st[u], i * 32)
                            step.chunk(c, 2 * (NORM_STEPS + TAIL_STEPS + 2))
                            for k in range(2):
                                xin = X[0:NP, u, k * G:(k + 1) * G, :]
                                norm_dve(eng, step, nm, c, xin, lambda xc, r: step(relu_into(dve, h[0:NP])(xc, r)),
                                         p=NP, w=c * 2 + k)
                                eng.sem_inc(q["h"], 1)
                                step(tail_dve(eng, step, q, c * 2 + k, xin, R[0:NP, u, k * G:(k + 1) * G, :], 1, p=NP))
                            step.end()
                            eng.sem_inc(s_x, 1)
                            eng.sem_inc(s_r, 1)
                        chunks(body)(dve)

                    @block.scalar
                    def _(act):
                        act.sem_inc(g1["free"], 2)
                        act.sem_inc(g0["free"], 2)
                        def body(eng, i, u):
                            c = i * 2 + u
                            for k in range(2):
                                norm_act(eng, nm, p=NP, w=c * 2 + k)
                                tail_act(eng, q, c * 2 + k, p=NP)
                            eng.wait_ge(g1["sems"][u], (i + 1) * (16 * G))
                            ring = g1["ring"][:, u]
                            eng.activation(XS[:, bass.ds(c * G, G), :], ring[:, :, 0:D], ACT.Copy)
                            eng.activation(RI[:, bass.ds(c * G, G)], ring[:, :, D], ACT.Copy)
                            eng.activation(OD[:, bass.ds(c * G, G)], ring[:, :, D + 1], ACT.Copy)
                            eng.activation(CS[:, bass.ds(c * G, G)], ring[:, :, D + 2], ACT.Copy).then_inc(g1["free"], 1)
                            eng.wait_ge(g0["sems"][u], (i + 1) * (16 * G))
                            ring = g0["ring"][:, u]
                            eng.activation(XD[:, bass.ds(c * G, G), :], ring[:, :, 0:D], ACT.Copy)
                            eng.activation(CD[:, bass.ds(c * G, G)], ring[:, :, D + 2], ACT.Copy).then_inc(g0["free"], 1)
                        chunks(body)(act)

                    @block.tensor
                    def _(pe):
                        def body(eng, i, u):
                            c = i * 2 + u
                            for k in range(2):
                                tail_pe(eng, q, c * 2 + k, h, BDc, p=NP)
                        chunks(body)(pe)

        dense()
        if STOP == "dense":
            return

        def ends_setup(st, name):
            return dict(fl=sb_in(st, name + "_sfl", [P, 2, G, 2]), ev=sb_in(st, name + "_ev", [2, 2, G * W1]),
                        ps=ps_in(st, name + "_ps", [P, 2, 2, 512]), m=sem(name + "_m"), cp=sem(name + "_cp"), go=sem(name + "_go"),
                        d=sem(name + "_sums"), e=sem(name + "_evac"), st=[sem(f"{name}_st{u}") for u in range(2)])

        def ends_pe(pe, i, u, q, w=W1):
            c = i * 2 + u
            pe.wait_ge(q["m"], c + 1)
            pe.wait_ge(q["cp"], c + 1)
            pe.sem_inc(q["go"], 1)
            for j in range(G):
                last = pe.matmul(q["ps"][0:2, u, j // 4, (j % 4) * w:(j % 4 + 1) * w], q["fl"][:, u, j, :],
                                 M[:, bass.ds(c * G + j, 1), 0:w].rearrange("p a d -> p (a d)"),
                                 start=True, stop=True)
            last.then_inc(q["d"], 1)

        def ends_act_before(act, i, u, q):
            c = i * 2 + u
            act.activation(q["fl"][:, u], SFL[:, bass.ds(c * G, G), :], ACT.Copy).then_inc(q["cp"], 1)

        def ends_act(act, i, u, q, w=W1):
            c = i * 2 + u
            act.wait_ge(q["d"], c + 1)
            act.wait_ge(q["st"][u], i * 16)
            act.activation(q["ev"][:, u, 0:G * w].rearrange("k (b n) -> k b n", b=2), q["ps"][0:2, u, :, 0:4 * w], ACT.Copy).then_inc(q["e"], 1)

        def ends_sp(sp, i, u, q, w=W1):
            c = i * 2 + u
            sp.wait_ge(q["e"], c + 1)
            sp.dma_start(FLd[:, bass.ds(c * G, G), 0:w],
                         q["ev"][:, u, 0:G * w].rearrange("k (g d) -> k g d", d=w)).then_inc(q["st"][u], 16)

        def ends_sp_done(sp, q):
            sp.wait_ge(q["st"][0], 16 * (NCH // 2 + 1))
            sp.wait_ge(q["st"][1], 16 * (NCH // 2))

        def carries(name, w=W1):
            st = phase()
            with st:
                fl = sb_in(st, name + "_fl", [HALF, 2, 2, w])
                ca = sb_in(st, name + "_ca", [HALF, 2, 2, w])
                ps = ps_in(st, name + "_ps", [P, 2, 512])
                s_l, s_m, s_e, s_o = sem(name + "_l"), sem(name + "_m"), sem(name + "_e"), sem(name + "_o")
                with nc.Block() as block:
                    @block.sync
                    def _(sp):
                        for k in range(2):
                            sp.dma_start(fl[:, k], FLd[k, :, 0:w].rearrange("(c p) d -> p c d", c=2)).then_inc(s_l, 16)
                        sp.wait_ge(s_e, 1)
                        for k in range(2):
                            sp.dma_start(CAd[k, :, 0:w].rearrange("(c p) d -> p c d", c=2), ca[:, k]).then_inc(s_o, 16)
                        sp.wait_ge(s_o, 32)

                    @block.tensor
                    def _(pe):
                        pe.wait_ge(s_l, 32)
                        for k, (masks, end) in enumerate(((BLF, 1), (BFL, 0))):
                            for c in range(2):
                                for cc in range(2):
                                    last = pe.matmul(ps[0:HALF, k, c * w:(c + 1) * w],
                                                     masks[:, cc, c * HALF:(c + 1) * HALF], fl[:, end, cc, :],
                                                     start=cc == 0, stop=cc == 1)
                        last.then_inc(s_m, 1)

                    @block.vector
                    def _(dve):
                        dve.wait_ge(s_m, 1)
                        dve.tensor_copy(ca[:, :, :, :], ps[0:HALF, :, 0:2 * w].rearrange("p k (c d) -> p k c d", d=w))\
                            .then_inc(s_e, 1)

        def sums_setup(st, name):
            return dict(S=sb_in(st, name + "_S", [P, 2, G, P]),
                        C=sb_in(st, name + "_C", [P, 2, G, W1]), ps=ps_in(st, name + "_ps", [P, 2, 2, 512]),
                        z=sem(name + "_z"), ld=[sem(f"{name}_ld{u}") for u in range(2)], s=sem(name + "_S"),
                        d=sem(name + "_d"), fr=sem(name + "_fr"))

        def sums_sp(sp, i, u, q, w=W1, carry=True):
            c = i * 2 + u
            sp.wait_ge(q["fr"], c + 1)
            sp.dma_start(q["S"][:, u].rearrange("p g j -> p (g j)"),
                         dstP[bass.ds(c * G * P, G * P)].rearrange("(a n) -> a n", a=1).broadcast_to([P, G * P]))\
                .then_inc(q["ld"][u], 16)
            if carry:
                for k, row in enumerate((0, P - 1)):
                    sp.dma_start(q["C"][row:row + 1, u, :, 0:w],
                                 CAd[k:k + 1, bass.ds(c * G, G), 0:w]).then_inc(q["ld"][u], 16)

        def sums_start(dve, step, q):
            step(dve.memset(q["C"][:, :, :, :], 0.0))
            dve.sem_inc(q["z"], 1)

        def sums_dve(dve, i, u, q, carry=True):
            c = i * 2 + u
            dve.wait_ge(q["ld"][u], (i + 1) * (48 if carry else 16))
            dve.tensor_tensor(q["S"][:, u], q["S"][:, u], bc(dstF[:, bass.ds(c * G, G)], 2, [P, G, P]),
                              ALU.is_equal).then_inc(q["s"], 1)

        def sums_pe(pe, i, u, q, w=W1):
            c = i * 2 + u
            pe.wait_ge(q["s"], c + 1)
            for j in range(G):
                to = q["ps"][:, u, j // 4, (j % 4) * w:(j % 4 + 1) * w]
                pe.matmul(to, q["S"][:, u, j, :], M[:, bass.ds(c * G + j, 1), 0:w].rearrange("p a d -> p (a d)"),
                          start=True, stop=False)
                last = pe.matmul(to, q["S"][:, u, j, :], q["C"][:, u, j, 0:w], start=False, stop=True)
            last.then_inc(q["d"], 1)

        def sums_view(q, u, w=W1, a=0, b=D):
            return q["ps"][:, u, :, 0:4 * w].rearrange("p k (g d) -> p k g d", d=w)[:, :, :, a:b]

        def v4(ap):
            return ap.rearrange("p (k g) d -> p k g d", k=2)

        def norms_and_ends(name, emit_for, per, before=None, w=W1, lone=False):
            st = phase()
            with st:
                nm = norm_setup(st, name + "_nm", G)
                q = ends_setup(st, name + "_en")
                if lone:
                    R = sb_in(st, name + "_R", [P, 2, G, D])
                    idx = sb_in(st, name + "_idx", [P, 2, G], i32)
                    s_r = sem(name + "_r"); s_i = sem(name + "_i"); s_go = sem(name + "_go"); s_sc = sem(name + "_sc")
                with nc.Block() as block:
                    @block.vector
                    def _(dve):
                        step = Steps(dve, name + "_dve")
                        if before is not None:
                            before(dve, step)
                        base = step.k
                        def body(eng, i, u):
                            c = i * 2 + u
                            step.chunk(c, NORM_STEPS + per + (2 if lone else 1), base)
                            if lone:
                                eng.wait_ge(s_sc, i * (32 * G))
                                step(eng.tensor_tensor(R[:, u], XS[:, bass.ds(c * G, G), :],
                                                       bc(cD[:, 2, :], 1, [P, G, D]), ALU.add))
                                eng.sem_inc(s_r, 1)
                            to = M[:, bass.ds(c * G, G), 0:D]
                            norm_dve(eng, step, nm, c, XS[:, bass.ds(c * G, G), :],
                                     lambda xc, r: emit_for(eng, step, c, to, xc, r), w=c)
                            eng.sem_inc(q["m"], 1)
                            step.end()
                        chunks(body)(dve)

                    @block.scalar
                    def _(act):
                        def body(eng, i, u):
                            c = i * 2 + u
                            ends_act_before(eng, i, u, q)
                            norm_act(eng, nm, w=c)
                            ends_act(eng, i, u, q, w)
                        chunks(body)(act)

                    @block.tensor
                    def _(pe):
                        chunks(lambda eng, i, u: ends_pe(eng, i, u, q, w))(pe)

                    @block.sync
                    def _(sp):
                        chunks(lambda eng, i, u: ends_sp(eng, i, u, q, w))(sp)
                        ends_sp_done(sp, q)

                    if lone:
                        @block.gpsimd
                        def _(pool):
                            last_row = pool.to_reg(N - 1)
                            def body(eng, i, u):
                                c = i * 2 + u
                                eng.wait_ge(s_sc, c * (16 * G))
                                eng.tensor_copy(idx[:, u, :], srcS[:, bass.ds(c * G, G)]).then_inc(s_i, 1)
                                eng.wait_ge(s_i, c + 1)
                                eng.wait_ge(s_r, c + 1)
                                for j in range(G):
                                    if j:
                                        eng.wait_ge(s_sc, c * (16 * G) + 16 * j)
                                    eng.sem_inc(s_go, 1)
                                    eng.indirect_dma_start(
                                        out=out, out_offset=bass.IndirectOffsetOnAxis(ap=idx[:, u, j:j + 1], axis=0),
                                        in_=R[:, u, j, :], in_offset=None, bounds_check=last_row,
                                        oob_is_err=False).then_inc(s_sc, 16)
                            chunks(body)(pool)
                            pool.wait_ge(s_sc, 16 * G * NCH)

        def after_gather(dve, step):
            step(dve.tensor_scalar(RC[:, :], RI[:, :], 0.0, None, ALU.is_equal))
            step(dve.tensor_scalar(RC[:, :], RC[:, :], float(FAR), -1.0, ALU.mult, ALU.add))
            step(dve.tensor_tensor(RI[:, :], RI[:, :], RC[:, :], ALU.add))
            step(dve.tensor_copy(riI[:, :], RI[:, :]))
            step(dve.tensor_copy(csI[:, :], CS[:, :]))
            step(dve.tensor_copy(cdI[:, :], CD[:, :]))
            step(dve.tensor_scalar(RC[:, :], RI[:, :], float(NT * P), float(FAR), ALU.is_lt, ALU.mult))
            step(dve.tensor_tensor(RC[:, :], RC[:, :], srcF[:, :], ALU.add))
            step(dve.tensor_copy(srcS[:, :], RC[:, :]))
            step(dve.tensor_scalar(OD[:, :], OD[:, :], 1.0, None, ALU.max))

        def plain(eng, step, c, to, xc, r):
            step(relu_into(eng, to)(xc, r))

        with phase(), nc.Block() as block:
            @block.vector
            def _(dve):
                step = Steps(dve, "ri_dve")
                after_gather(dve, step)
                step(dve.memset(M[:, :, D:W1], 1.0))
        early.close()
        norms_and_ends("l0a", plain, 0)
        carries("l0b")

        def means_and_squares():
            st = phase()
            with st:
                q = sums_setup(st, "l0c_s")
                e = ends_setup(st, "l0c_e")
                mean = sb_in(st, "l0c_mean", [P, G, D])
                d = sb_in(st, "l0c_d", [P, 2, G, D])
                cnt = sb_in(st, "l0c_cnt", [P, 2, G])
                s_d = sem("l0c_dev"); s_df = sem("l0c_devfree")
                PER = 7
                with nc.Block() as block:
                    @block.sync
                    def _(sp):
                        sp.wait_ge(q["z"], 1)
                        def body(eng, i, u):
                            sums_sp(eng, i, u, q)
                            if u:
                                ends_sp(eng, i, 0, e, D)
                                ends_sp(eng, i, 1, e, D)
                        chunks(body)(sp)
                        ends_sp(sp, NCH // 2, 0, e, D)
                        ends_sp_done(sp, e)

                    @block.vector
                    def _(dve):
                        step = Steps(dve, "l0c_dve")
                        dve.sem_inc(q["fr"], 2)
                        dve.sem_inc(s_df, 2)
                        sums_start(dve, step, q)
                        def body(eng, i, u):
                            c = i * 2 + u
                            step.chunk(c, PER, 1)
                            sums_dve(eng, i, u, q)
                            eng.wait_ge(q["d"], c + 1)
                            cc = sums_view(q, u, W1, D, W1)
                            t2 = lambda a: a[:, bass.ds(c * G, G)]
                            step(eng.tensor_copy(v4(cnt[:, u, :].unsqueeze(2)), cc))
                            step(eng.reciprocal(t2(RC), cnt[:, u, :]))
                            step(eng.tensor_scalar(cnt[:, u, :], cnt[:, u, :], 1.0, None, ALU.is_gt))
                            step(eng.tensor_tensor(t2(RCM), t2(RC), cnt[:, u, :], ALU.mult))
                            step(eng.tensor_tensor(v4(mean[:, :, :]), sums_view(q, u),
                                                   v4(bc(t2(RC), 2, [P, G, D])), ALU.mult))
                            eng.sem_inc(q["fr"], 1)
                            eng.wait_ge(s_df, c + 1)
                            step(eng.tensor_tensor(d[:, u], M[:, bass.ds(c * G, G), 0:D], mean[:, :, :], ALU.subtract))
                            step(eng.tensor_tensor(M[:, bass.ds(c * G, G), 0:D], d[:, u], d[:, u], ALU.mult))
                            eng.sem_inc(s_df, 1)
                            eng.sem_inc(e["m"], 1)
                            step.end()
                        chunks(body)(dve)

                    @block.scalar
                    def _(act):
                        def body(eng, i, u):
                            ends_act_before(eng, i, u, e)
                            ends_act(eng, i, u, e, D)
                        chunks(body)(act)

                    @block.tensor
                    def _(pe):
                        def body(eng, i, u):
                            sums_pe(eng, i, u, q)
                            ends_pe(eng, i, u, e, D)
                        chunks(body)(pe)

        means_and_squares()
        carries("l0d", D)

        def update(name, table, emit, per, act_fn=None, w=D):
            st = phase()
            with st:
                q = sums_setup(st, name + "_s")
                t = sb_in(st, name + "_t", [P, 2, G, D])
                s_x = sem(name + "_xd"); s_a = sem(name + "_a"); s_b = sem(name + "_b")
                s_st = sem(name + "_st")
                with nc.Block() as block:
                    @block.sync
                    def _(sp):
                        sp.wait_ge(q["z"], 1)
                        chunks(lambda eng, i, u: sums_sp(eng, i, u, q, w))(sp)

                    @block.vector
                    def _(dve):
                        step = Steps(dve, name + "_dve")
                        dve.sem_inc(q["fr"], 2)
                        sums_start(dve, step, q)
                        def body(eng, i, u):
                            c = i * 2 + u
                            step.chunk(c, per, 1)
                            sums_dve(eng, i, u, q)
                            eng.wait_ge(q["d"], c + 1)
                            emit(eng, step, i, u, q, t, s_a, s_b)
                            step.end()
                            eng.sem_inc(s_x, 1)
                        chunks(body)(dve)

                    @block.tensor
                    def _(pe):
                        chunks(lambda eng, i, u: sums_pe(eng, i, u, q, w))(pe)

                    @block.scalar
                    def _(act):
                        def body(eng, i, u):
                            c = i * 2 + u
                            if act_fn is not None:
                                act_fn(eng, i, u, t, s_a, s_b)
                            eng.wait_ge(s_x, c + 1)
                            eng.dma_start(table[bass.ds(c * G * P, G * P), :].rearrange("(g p) d -> p g d", p=P),
                                          XD[:, bass.ds(c * G, G), :]).then_inc(s_st, 16)
                        chunks(body)(act)
                        act.wait_ge(s_st, 16 * NCH)

        def deviation(eng, step, i, u, q, t, s_a, s_b):
            c = i * 2 + u
            xd = XD[:, bass.ds(c * G, G), :]
            eng.tensor_tensor(v4(t[:, u]), sums_view(q, u, D), v4(bc(RCM[:, bass.ds(c * G, G)], 2, [P, G, D])),
                              ALU.mult).then_inc(s_a, 1)
            eng.wait_ge(s_b, c + 1)
            eng.sem_inc(q["fr"], 1)
            step(eng.tensor_tensor(xd, xd, t[:, u], ALU.add))

        def deviation_root(act, i, u, t, s_a, s_b):
            c = i * 2 + u
            act.wait_ge(s_a, c + 1)
            act.activation(t[:, u], t[:, u], ACT.Sqrt).then_inc(s_b, 1)

        update("l0e", T1, deviation, 1, deviation_root)
        if STOP == "l0":
            return

        def attributes():
            st = phase()
            with st:
                q = ends_setup(st, "l1a_en")
                g = gather_setup(st, "l1a_g", D)
                s_e = sem("l1a_ea"); s_z = sem("l1a_z"); s_x = sem("l1a_x"); s_io = sem("l1a_iota")
                S2 = sb_in(st, "l1a_S2", [P, 2, G, P])
                jI = sb_in(st, "l1a_jI", [P, P], i32); jF = sb_in(st, "l1a_jF", [P, P])
                pI_ = sb_in(st, "l1a_pI", [P, 1], i32); pF = sb_in(st, "l1a_pF", [P, 2])
                lastR = sb_in(st, "l1a_last", [P, NT]); tmp = sb_in(st, "l1a_tmp", [P, NT])
                s_sr = [sem(f"l1a_src{u}") for u in range(2)]; s_sf = sem("l1a_srcfree")
                with nc.Block() as block:
                    @block.gpsimd
                    def _(pool):
                        pool.iota(jI[:, :], [[1, P]], channel_multiplier=0)
                        pool.iota(pI_[:, :], [[1, 1]], channel_multiplier=1).then_inc(s_io, 1)
                        last_row = pool.to_reg(NT * P - 1)
                        chunks(lambda eng, i, u: gather_chunk(eng, i, u, g, T1, riI, last_row, old=XS))(pool)

                    @block.vector
                    def _(dve):
                        dve.memset(M[:, full_rows:NT, 0:D], 0.0).then_inc(s_z, 1)
                        dve.wait_ge(s_e, 32)
                        dve.sem_inc(q["m"], NCH)
                        step = Steps(dve, "l1a_dve")
                        dve.sem_inc(s_sf, 2)
                        dve.wait_ge(s_io, 1)
                        dve.tensor_copy(jF[:, :], jI[:, :])
                        step(dve.tensor_copy(pF[:, 0:1], pI_[:, :]))
                        def body(eng, i, u):
                            c = i * 2 + u
                            step.chunk(c, 3, 1)
                            eng.wait_ge(s_sr[u], (i + 1) * 16)
                            step(eng.tensor_tensor(S2[:, u], S2[:, u], bc(srcF[:, bass.ds(c * G, G)], 2, [P, G, P]),
                                                   ALU.is_equal))
                            step(eng.tensor_tensor(S2[:, u], S2[:, u], bc(jF[:, :], 1, [P, G, P]), ALU.mult))
                            step(eng.tensor_reduce(lastR[:, bass.ds(c * G, G)], S2[:, u], AX.X, ALU.max))
                            eng.sem_inc(s_sf, 1)
                            step.end()
                        chunks(body)(dve)
                        step.base, step.k = 3 * NCH + 1, 0
                        step(dve.tensor_scalar(lastR[:, :], lastR[:, :], pF[:, 0:1], None, ALU.is_equal))
                        step(dve.tensor_scalar(tmp[:, :], srcF[:, :], float(N), None, ALU.is_lt))
                        step(dve.tensor_tensor(lastR[:, :], lastR[:, :], tmp[:, :], ALU.mult))
                        step(dve.tensor_scalar(pF[:, 1:2], pF[:, 0:1], float(NT * P), None, ALU.add))
                        step(dve.tensor_copy(tmp[:, :], csI[:, :]))
                        step(dve.tensor_scalar(tmp[:, :], tmp[:, :], pF[:, 1:2], None, ALU.subtract))
                        step(dve.tensor_tensor(tmp[:, :], tmp[:, :], lastR[:, :], ALU.mult))
                        step(dve.tensor_scalar(tmp[:, :], tmp[:, :], pF[:, 1:2], None, ALU.add))
                        step(dve.tensor_copy(idY[:, :], tmp[:, :]))
                        step(dve.tensor_scalar(lastR[:, :], lastR[:, :], -float(FAR), float(FAR), ALU.mult, ALU.add))
                        step(dve.tensor_copy(tmp[:, :], srcS[:, :]))
                        step(dve.tensor_tensor(tmp[:, :], tmp[:, :], lastR[:, :], ALU.add))
                        step(dve.tensor_copy(srcS[:, :], tmp[:, :]))

                    @block.scalar
                    def _(act):
                        act.sem_inc(g["free"], 2)
                        def body(eng, i, u):
                            c = i * 2 + u
                            ends_act_before(eng, i, u, q)
                            ends_act(eng, i, u, q, D)
                            eng.wait_ge(g["sems"][u], (i + 1) * (16 * G))
                            eng.activation(XS[:, bass.ds(c * G, G), :], g["ring"][:, u], ACT.Copy)\
                                .then_inc(g["free"], 1)
                        chunks(body)(act)

                    @block.tensor
                    def _(pe):
                        chunks(lambda eng, i, u: ends_pe(eng, i, u, q, D))(pe)

                    @block.sync
                    def _(sp):
                        sp.dma_start(M[:, 0:full_rows, 0:D],
                                     edge_attr[0:full_rows * P, :].rearrange("(t p) d -> p t d", p=P)).then_inc(s_e, 16)
                        sp.wait_ge(s_z, 1)
                        sp.dma_start(M[0:rest, full_rows, 0:D], edge_attr[full_rows * P:E, :]).then_inc(s_e, 16)
                        def body(eng, i, u):
                            c = i * 2 + u
                            eng.wait_ge(s_sf, c + 1)
                            eng.dma_start(S2[:, u].rearrange("p g j -> p (g j)"),
                                          srcP[bass.ds(c * G * P, G * P)].rearrange("(a n) -> a n", a=1)
                                          .broadcast_to([P, G * P])).then_inc(s_sr[u], 16)
                            ends_sp(eng, i, u, q, D)
                        chunks(body)(sp)
                        ends_sp_done(sp, q)

        attributes()
        move_columns((srcF, idY, csI, cdI, srcS), True)
        columns_st.close()
        carries("l1b", D)

        alive = ExitStack()
        with alive:
            LG = sb_in(alive, "LG", [P, 2, NT, H])

            def logits():
                st = phase()
                with st:
                    q = sums_setup(st, "l1c_s")
                    AB = sb_in(st, "l1c_AB", [P, 2, G, P])
                    nm = norm_setup(st, "l1c_nm", G, xc=AB[:, 0, :, 0:D], sq=AB[:, 0, :, D:P])
                    nm2 = dict(nm, xc=AB[:, 1, :, 0:D], sq=AB[:, 1, :, D:P])
                    ABT = sb_in(st, "l1c_ABT", [P, 2, 4, P])
                    LK = sb_in(st, "l1c_LK", [P, 2, 4 * P])
                    pT = q["ps"]
                    pM = ps_in(st, "l1c_pM", [P, 2, 512])
                    pL = ps_in(st, "l1c_pL", [P, 512])
                    s_ab = sem("l1c_ab"); s_abf = sem("l1c_abfree"); s_t = sem("l1c_t"); s_tc = sem("l1c_tc")
                    s_m = sem("l1c_m"); s_lk = sem("l1c_lk"); s_l = sem("l1c_l"); s_le = sem("l1c_le")
                    s_ea = sem("l1c_eacopied")
                    PER = 2 * (NORM_STEPS + 1) + 3
                    pX = ps_in(st, "l1c_pX", [P, 512])
                    with nc.Block() as block:
                        @block.sync
                        def _(sp):
                            sp.wait_ge(q["z"], 1)
                            chunks(lambda eng, i, u: sums_sp(eng, i, u, q, D))(sp)

                        @block.vector
                        def _(dve):
                            step = Steps(dve, "l1c_dve")
                            dve.sem_inc(q["fr"], 2)
                            sums_start(dve, step, q)
                            def body(eng, i, u):
                                c = i * 2 + u
                                step.chunk(c, PER, 1)
                                sums_dve(eng, i, u, q)
                                eng.wait_ge(s_abf, c + 1)
                                eng.wait_ge(s_le, 2 * c)
                                norm_dve(eng, step, nm, c, XS[:, bass.ds(c * G, G), :],
                                         lambda xc, r: step(relu_into(eng, AB[:, 0, :, 0:D])(xc, r)), w=c * 2)
                                norm_dve(eng, step, nm2, c, XD[:, bass.ds(c * G, G), :],
                                         lambda xc, r: step(relu_into(eng, AB[:, 1, :, 0:D])(xc, r)), w=c * 2 + 1)
                                eng.wait_ge(q["d"], c + 1)
                                step(eng.tensor_scalar(AB[:, 0, :, D:P], M[:, bass.ds(c * G, G), 0:D], 1.0, None, ALU.mult))
                                step(eng.tensor_tensor(v4(AB[:, 1, :, D:P]), sums_view(q, u, D),
                                                       v4(bc(RC[:, bass.ds(c * G, G)], 2, [P, G, D])), ALU.mult))
                                step(eng.tensor_scalar(M[:, bass.ds(c * G, G), 0:D], AB[:, 0, :, 0:D], 1.0, None, ALU.mult))
                                eng.sem_inc(q["fr"], 1)
                                eng.sem_inc(s_ab, 1)
                                step.end()
                            chunks(body)(dve)

                        @block.tensor
                        def _(pe):
                            def body(eng, i, u):
                                c = i * 2 + u
                                sums_pe(eng, i, u, q, D)
                                eng.wait_ge(s_ab, c + 1)
                                for hf in range(2):
                                    n = c * 2 + hf
                                    for k in range(2):
                                        eng.wait_ge(s_tc, n * 2 + k)
                                        for j in range(4):
                                            last = eng.transpose(pX[:, j * P:(j + 1) * P], AB[:, k, hf * 4 + j, :],
                                                                 ident[:, :])
                                        last.then_inc(s_t, 1)
                                    eng.wait_ge(s_tc, n * 2 + 2)
                                    for k in range(2):
                                        for f in range(3):
                                            m = n * 6 + k * 3 + f
                                            lo, hi = f * P, min(HC, (f + 1) * P)
                                            z = hi - lo
                                            slot = (k * 3 + f) % 2
                                            if k * 3 + f >= 2:
                                                eng.wait_ge(s_lk, m - 1)
                                            to = pM[0:z, slot, :]
                                            rA = ABT[:, 0].rearrange("p j e -> p (j e)")
                                            rB = ABT[:, 1].rearrange("p j e -> p (j e)")
                                            if k == 0:
                                                eng.matmul(to, WA[:, lo:hi], rA, start=True, stop=False)
                                                last = eng.matmul(to, WBr[:, lo:hi], rB[0:D, :], start=False, stop=True)
                                            else:
                                                last = eng.matmul(to, WS[:, lo:hi], rB, start=True, stop=True)
                                            last.then_inc(s_m, 1)
                                            if k * 3 + f >= 1:
                                                dots(eng, n, k * 3 + f - 1)
                                    dots(eng, n, 5)
                                    if hf == 1:
                                        eng.sem_inc(s_abf, 1)

                            def dots(eng, n, kf):
                                k, f = kf // 3, kf % 3
                                z = min(P, HC - f * P)
                                eng.wait_ge(s_lk, n * 6 + kf + 1)
                                if kf == 0:
                                    eng.wait_ge(s_le, n)
                                for j in range(4):
                                    to = pL[:, (k * 4 + j) * H:(k * 4 + j + 1) * H]
                                    if f == 0:
                                        rA, rB = ABT[:, 0, j, :], ABT[:, 1, j, :]
                                        parts = ((rA, lin[:, 0, :]), (rB[0:D], lin[0:D, 1, :])) if k == 0 else \
                                            ((rB, lin[:, 2, :]),)
                                        for n_, (x_, w_) in enumerate(((ones[0:1, :], lin[0:1, 3, :]),) + parts):
                                            eng.matmul(to, x_, w_, start=kf + j + n_ == 0, stop=False,
                                                       skip_group_check=True)
                                    last = eng.matmul(to, LK[0:z, kf % 2, j * P:(j + 1) * P], attC[0:z, f, :],
                                                      start=False, stop=kf == 5 and j == 3, skip_group_check=True)
                                last.then_inc(s_l, 1)

                            eng = pe
                            chunks(body)(pe)

                        @block.scalar
                        def _(act):
                            act.sem_inc(s_abf, 1)
                            def body(eng, i, u):
                                c = i * 2 + u
                                norm_act(eng, nm, w=c * 2)
                                norm_act(eng, nm, w=c * 2 + 1)
                                for hf in range(2):
                                    n = c * 2 + hf
                                    for k in range(2):
                                        eng.wait_ge(s_t, n * 2 + k + 1)
                                        eng.activation(ABT[:, k].rearrange("p j e -> p (j e)"), pX[:, :],
                                                       ACT.Copy).then_inc(s_tc, 1)
                                    for kf in range(6):
                                        f = kf % 3
                                        z = min(P, HC - f * P)
                                        eng.wait_ge(s_m, n * 6 + kf + 1)
                                        if kf >= 2:
                                            eng.wait_ge(s_l, n * 6 + kf - 1)
                                        eng.activation(LK[0:z, kf % 2, :], pM[0:z, kf % 2, :], ACT.Relu,
                                                       bias=mb[0:z, f:f + 1]).then_inc(s_lk, 1)
                                    eng.wait_ge(s_l, n * 6 + 6)
                                    eng.activation(LG[:, :, bass.ds(c * G + hf * 4, 4), :],
                                                   pL[:, 0:8 * H].rearrange("p (k g h) -> p k g h", k=2, h=H),
                                                   ACT.Copy).then_inc(s_le, 1)
                            chunks(body)(act)

            logits()
            if STOP == "logits":
                return

            NR = 25 * H
            NA = NT // 25

            def softmax():
                st = phase()
                with st:
                    t = lambda name, shape, dt=f32: sb_in(st, name, shape, dt)
                    room = M[0:NR, :, :].rearrange("p t d -> p (t d)")
                    part = lambda a, n: room[:, a * NA * P:(a + n) * NA * P].rearrange(
                        "p (n a j) -> p n a j", n=n, j=P)
                    L = part(0, 3)
                    same = part(3, 2)
                    isF0 = part(5, 1)[:, 0]
                    Aall = t("sm_A", [P, 3, NA, P])
                    A = Aall[0:NR]
                    d5 = Aall[:, 2].rearrange("p a j -> p (a j)")[:, 0:NT * H].rearrange("p (t h) -> p t h", h=H)
                    ends = t("sm_ends", [NR, 2, NA])
                    car = t("sm_car", [NR, 2, NA])
                    e5 = t("sm_e5", [H, 2, NT]); c5 = t("sm_c5", [H, 2, NT])
                    m0 = t("sm_m0", [H, NT]); one = t("sm_one", [H, NT]); m1 = t("sm_m1", [H, NT])
                    m1b = t("sm_m1b", [H, NT])
                    u5 = t("sm_u5", [H, NT]); b5 = t("sm_b5", [H, NT])
                    pL = ps_in(st, "sm_pL", [P, 6, 512])
                    kFr = t("sm_kF", [H, NT]); kLr = t("sm_kL", [H, NT])
                    s_k = sem("sm_keys"); s_sp = sem("sm_spill"); s_d = sem("sm_d5"); s_t = sem("sm_t"); s_en = sem("sm_ends"); s_e5 = sem("sm_e5")
                    s_c5 = sem("sm_c5"); s_car = sem("sm_car"); s_o = sem("sm_o"); s_o2 = sem("sm_o2")
                    s_x = sem("sm_x"); s_z = sem("sm_z"); s_al = sem("sm_al"); s_alT = sem("sm_alT")
                    flat = lambda a: a.rearrange("p a j -> p (a j)")
                    with nc.Block() as block:
                        @block.tensor
                        def _(pe):
                            pe.wait_ge(s_d, 1)
                            for n in range(3):
                                of = d5 if n == 2 else LG[:, n]
                                for a in range(NA):
                                    last = pe.transpose(pL[0:NR, 2 * n + a // 4, (a % 4) * P:(a % 4 + 1) * P],
                                                        of[:, 25 * a:25 * (a + 1), :].rearrange("p t h -> p (t h)"),
                                                        ident[:, :])
                            last.then_inc(s_t, 1)
                            pe.wait_ge(s_al, 1)
                            for n in range(2):
                                for a in range(NA):
                                    last = pe.transpose(pL[:, 2 * n + a // 4, (a % 4) * P:(a % 4) * P + NR],
                                                        A[:, n, a, :], ident[0:NR, 0:NR])
                            last.then_inc(s_alT, 1)

                        @block.sync
                        def _(sp):
                            sp.dma_start(Msp, M[:, 0:SPT, :]).then_inc(s_sp, 16)
                            keys = dstP.rearrange("(a t j) -> a t j", a=1, j=P)
                            rows_of = lambda v: v.rearrange("(a p) -> p a", a=NA)
                            heads_of = lambda v: v.rearrange("(t h) -> h t", h=H)
                            with nc.allow_non_contiguous_dma(reason="a few values of each tile"):
                                for to, end in ((kFr, 0), (kLr, P - 1)):
                                    sp.dma_start(to[:, :], keys[:, :, end].broadcast_to([H, NT])).then_inc(s_k, 16)
                                for k in range(2):
                                    sp.wait_ge(s_en, k + 1)
                                    for e_ in range(2):
                                        sp.dma_start(rows_of(SMd[e_]), ends[:, e_, :]).then_inc(s_o, 16)
                                    sp.wait_ge(s_o, 32 * (k + 1))
                                    for e_ in range(2):
                                        sp.dma_start(e5[:, e_, :], heads_of(SMd[e_])).then_inc(s_e5, 16)
                                    sp.wait_ge(s_c5, k + 1)
                                    for e_ in range(2):
                                        sp.dma_start(heads_of(SCd[e_]), c5[:, e_, :]).then_inc(s_o2, 16)
                                    sp.wait_ge(s_o2, 32 * (k + 1))
                                    for e_ in range(2):
                                        sp.dma_start(car[:, e_, :], rows_of(SCd[e_])).then_inc(s_car, 16)
                            sp.wait_ge(s_al, 1)
                            sp.dma_start(M[:, 0:SPT, :], Msp).then_inc(s_sp, 16)
                            sp.wait_ge(s_sp, 32)

                        @block.scalar
                        def _(act):
                            act.wait_ge(s_x, 1)
                            act.activation(A[:, 0:2].rearrange("p n a j -> p (n a j)"),
                                           L[:, 0:2].rearrange("p n a j -> p (n a j)"), ACT.Exp).then_inc(s_z, 1)

                        @block.vector
                        def _(dve):
                            step = Steps(dve, "sm_dve")
                            tt = lambda o, a, b, op: step(dve.tensor_tensor(o, a, b, op))
                            ts = lambda o, a, s1, s2, o1, o2=None: step(
                                dve.tensor_scalar(o, a, s1, s2, o1, o2) if o2 is not None else
                                dve.tensor_scalar(o, a, s1, s2, o1))
                            scan = lambda o, a, b, i0, o1, o2: step(dve.tensor_tensor_scan(o, a, b, i0, o1, o2))
                            dve.wait_ge(s_sp, 16)
                            step(dve.tensor_copy(d5[:, :, :], bc(dstF[:, :], 2, [P, NT, H])))
                            dve.sem_inc(s_d, 1)
                            dve.wait_ge(s_t, 1)
                            for n in range(3):
                                step(dve.tensor_copy(flat(L[:, n]), pL[0:NR, 2 * n:2 * n + 2, :].rearrange("p b j -> p (b j)")))
                            DR = L[:, 2]
                            dve.memset(same[:, 0, :, 0:1], 0.0)
                            dve.memset(same[:, 1, :, P - 1:P], 0.0)
                            tt(same[:, 0, :, 1:P], DR[:, :, 1:P], DR[:, :, 0:P - 1], ALU.is_equal)
                            tt(same[:, 1, :, 0:P - 1], DR[:, :, 1:P], DR[:, :, 0:P - 1], ALU.is_equal)
                            tt(isF0, DR, DR[:, :, 0:1].broadcast_to([NR, NA, P]), ALU.is_equal)
                            step(dve.tensor_copy(ends[:, 0, :], DR[:, :, P - 1]))
                            tt(DR, DR, bc(ends[:, 0, :], 2, [NR, NA, P]), ALU.is_equal)
                            isF = (isF0, DR)
                            dve.wait_ge(s_k, 32)
                            dve.memset(m0[:, 0:1], 0.0)
                            dve.memset(m1[:, 0:1], 0.0)
                            dve.memset(m1b[:, NT - 1:NT], 0.0)
                            tt(m0[:, 1:NT], kFr[0:H, 1:NT], kLr[0:H, 0:NT - 1], ALU.is_equal)
                            tt(one[:, :], kFr[0:H, :], kLr[0:H, :], ALU.is_equal)
                            tt(m1[:, 1:NT], m0[:, 1:NT], one[:, 0:NT - 1], ALU.mult)
                            tt(m1b[:, 0:NT - 1], m0[:, 1:NT], one[:, 1:NT], ALU.mult)

                            def backwards(o, f, mask):
                                ts(o, mask, -1.0, 1.0, ALU.mult, ALU.add)
                                tt(f, o, f, ALU.mult)
                                scan(flat(o)[:, ::-1], flat(mask)[:, ::-1], flat(f)[:, ::-1], 0.0,
                                     ALU.mult, ALU.add)

                            def across(k, op, off):
                                dve.sem_inc(s_en, 1)
                                dve.wait_ge(s_e5, 32 * (k + 1))
                                if k == 1:
                                    dve.wait_ge(s_o2, 32)
                                for e_ in range(2):
                                    step(dve.memset(u5[:, :], off))
                                    a, b = (slice(1, NT), slice(0, NT - 1)) if e_ == 0 else (slice(0, NT - 1), slice(1, NT))
                                    keep = (m1 if e_ == 0 else m1b)
                                    val = e5[:, 1 - e_, b]
                                    if off:
                                        ts(b5[:, a], m0[:, 1:NT], BIG, -BIG, ALU.mult, ALU.add)
                                        tt(u5[:, a], b5[:, a], val, ALU.add)
                                        ts(b5[:, :], keep[:, :], BIG, -BIG, ALU.mult, ALU.add)
                                    else:
                                        tt(u5[:, a], m0[:, 1:NT], val, ALU.mult)
                                        step(dve.tensor_copy(b5[:, :], keep[:, :]))
                                    r = slice(None, None, 1 if e_ == 0 else -1)
                                    scan(c5[:, e_, r], b5[:, r], u5[:, r], off, ALU.add if off else ALU.mult, op)
                                dve.sem_inc(s_c5, 1)
                                dve.wait_ge(s_car, 32 * (k + 1))

                            ts(A[:, 0], same[:, 0], BIG, -BIG, ALU.mult, ALU.add)
                            scan(flat(A[:, 1]), flat(A[:, 0]), flat(L[:, 0]), -BIG, ALU.add, ALU.max)
                            backwards(A[:, 2], A[:, 1], same[:, 1])
                            step(dve.tensor_copy(ends[:, 0, :], A[:, 2, :, 0]))
                            step(dve.tensor_copy(ends[:, 1, :], A[:, 2, :, P - 1]))
                            across(0, ALU.max, -BIG)
                            for e_ in range(2):
                                ts(A[:, 0], isF[e_], BIG, -BIG, ALU.mult, ALU.add)
                                tt(A[:, 0], A[:, 0], bc(car[:, e_, :], 2, [NR, NA, P]), ALU.add)
                                tt(A[:, 2], A[:, 2], A[:, 0], ALU.max)
                            tt(A[:, 2], A[:, 2], L[:, 1], ALU.max)
                            tt(L[:, 0], L[:, 0], A[:, 2], ALU.subtract)
                            tt(L[:, 1], L[:, 1], A[:, 2], ALU.subtract)
                            dve.sem_inc(s_x, 1)
                            dve.wait_ge(s_z, 1)
                            scan(flat(A[:, 2]), flat(same[:, 0]), flat(A[:, 0]), 0.0, ALU.mult, ALU.add)
                            backwards(L[:, 0], A[:, 2], same[:, 1])
                            step(dve.tensor_copy(ends[:, 0, :], L[:, 0, :, 0]))
                            step(dve.tensor_copy(ends[:, 1, :], L[:, 0, :, P - 1]))
                            across(1, ALU.add, 0.0)
                            for e_ in range(2):
                                tt(A[:, 2], isF[e_], bc(car[:, e_, :], 2, [NR, NA, P]), ALU.mult)
                                tt(L[:, 0], L[:, 0], A[:, 2], ALU.add)
                            tt(L[:, 0], L[:, 0], A[:, 1], ALU.add)
                            step(dve.reciprocal(L[:, 1], L[:, 0]))
                            ts(L[:, 1], L[:, 1], 1.0 / H, None, ALU.mult)
                            tt(A[:, 0], A[:, 0], L[:, 1], ALU.mult)
                            tt(A[:, 1], A[:, 1], L[:, 1], ALU.mult)
                            dve.sem_inc(s_al, 1)
                            dve.wait_ge(s_alT, 1)
                            for n in range(2):
                                for b in range(2):
                                    to = LG[:, n, 100 * b:100 * (b + 1), :].rearrange("p (a t) h -> p a (t h)", a=4)
                                    of = pL[:, 2 * n + b, :].rearrange("p (a r) -> p a r", a=4)[:, :, 0:NR]
                                    step(dve.tensor_copy(to, of))
                            tt(LG[:, 1], LG[:, 1], bc(repF[:, :], 2, [P, NT, H]), ALU.mult)

            softmax()
            if STOP == "softmax":
                return

            def weighted():
                st = phase()
                with st:
                    nm = norm_setup(st, "l1e_nm", G)
                    e = ends_setup(st, "l1e_en")
                    hd = sb_in(st, "l1e_hd", [P, G, D])
                    Gs = sb_in(st, "l1e_G", [P, 2, 2, H, D])
                    Gd = sb_in(st, "l1e_Gd", [P, 2, 2, H, D])
                    GT = sb_in(st, "l1e_GT", [P, 2, 3, P])
                    pG = ps_in(st, "l1e_pG", [P, 2, 512])
                    pC = ps_in(st, "l1e_pC", [P, 512])
                    s_hd = sem("l1e_hd"); s_g = sem("l1e_g"); s_gd = sem("l1e_gd")
                    s_gf = sem("l1e_gf"); s_t = sem("l1e_t"); s_te = sem("l1e_te"); s_c = sem("l1e_c")
                    s_ce = sem("l1e_ce")
                    PER = NORM_STEPS + 1
                    with nc.Block() as block:
                        @block.vector
                        def _(dve):
                            step = Steps(dve, "l1e_dve")
                            def body(eng, i, u):
                                c = i * 2 + u
                                step.chunk(c, PER)
                                eng.wait_ge(s_gd, 4 * c)
                                norm_dve(eng, step, nm, c, XD[:, bass.ds(c * G, G), :],
                                         lambda xc, r: step(relu_into(eng, hd[:, :, :])(xc, r)), w=c)
                                eng.sem_inc(s_hd, 1)
                                step.end()
                                for hf in range(4):
                                    n = c * 4 + hf
                                    eng.wait_ge(s_gf, n + 1)
                                    for j in range(2):
                                        t_ = c * G + hf * 2 + j
                                        last = eng.tensor_tensor(
                                            Gs[:, hf % 2, j, :, :], M[:, bass.ds(t_, 1), 0:D].broadcast_to([P, H, D]),
                                            LG[:, 0, bass.ds(t_, 1), :].rearrange("p a h -> p h a").broadcast_to([P, H, D]),
                                            ALU.mult)
                                    last.then_inc(s_g, 1)
                            chunks(body)(dve)

                        @block.gpsimd
                        def _(pool):
                            def body(eng, i, u):
                                c = i * 2 + u
                                eng.wait_ge(s_hd, c + 1)
                                for hf in range(4):
                                    n = c * 4 + hf
                                    eng.wait_ge(s_gf, n + 1)
                                    for j in range(2):
                                        t_ = c * G + hf * 2 + j
                                        last = eng.tensor_tensor(
                                            Gd[:, hf % 2, j, :, :], hd[:, hf * 2 + j:hf * 2 + j + 1, :].broadcast_to([P, H, D]),
                                            LG[:, 1, bass.ds(t_, 1), :].rearrange("p a h -> p h a").broadcast_to([P, H, D]),
                                            ALU.mult)
                                    last.then_inc(s_gd, 1)
                            chunks(body)(pool)

                        @block.tensor
                        def _(pe):
                            pe.sem_inc(s_gf, 2)
                            def body(eng, i, u):
                                c = i * 2 + u
                                for j in range(G):
                                    hf, k = j // 2, c * G + j
                                    if j % 2 == 0:
                                        eng.wait_ge(s_g, c * 4 + hf + 1)
                                        eng.wait_ge(s_gd, c * 4 + hf + 1)
                                    if j >= 2:
                                        eng.wait_ge(s_te, k - 1)
                                    for f in range(3):
                                        z = min(2, H - 2 * f)
                                        to = pG[0:z * D, j % 2, f * P:(f + 1) * P]
                                        for k_, of in enumerate((Gs, Gd)):
                                            last = eng.matmul(
                                                to, of[:, hf % 2, j % 2, 2 * f:2 * f + z, :].rearrange("p h d -> p (h d)"),
                                                ident[:, :], start=k_ == 0, stop=k_ == 1)
                                    last.then_inc(s_t, 1)
                                    if j >= 1:
                                        product(eng, c, j - 1)
                                product(eng, c, G - 1)
                                ends_pe(eng, i, u, e, D)

                            def product(eng, c, j):
                                eng.wait_ge(s_te, c * G + j + 1)
                                if j == 0:
                                    eng.wait_ge(s_ce, c)
                                for f in range(3):
                                    z = min(P, HC - f * P)
                                    last = eng.matmul(pC[:, j * D:(j + 1) * D], GT[0:z, j % 2, f, :], WlS[0:z, f, :],
                                                      start=f == 0, stop=f == 2)
                                    if f == 0 and j % 2 == 0:
                                        last.then_inc(s_gf, 1)
                                if j == G - 1:
                                    last.then_inc(s_c, 1)
                            chunks(body)(pe)

                        @block.scalar
                        def _(act):
                            def body(eng, i, u):
                                c = i * 2 + u
                                ends_act_before(eng, i, u, e)
                                norm_act(eng, nm, w=c)
                                for j in range(G):
                                    k = c * G + j
                                    eng.wait_ge(s_t, k + 1)
                                    eng.activation(GT[:, j % 2, 0:2].rearrange("p f e -> p (f e)"),
                                                   pG[:, j % 2, 0:2 * P], ACT.Copy)
                                    eng.activation(GT[0:D, j % 2, 2, :], pG[0:D, j % 2, 2 * P:3 * P],
                                                   ACT.Copy).then_inc(s_te, 1)
                                eng.wait_ge(s_c, c + 1)
                                eng.activation(M[:, bass.ds(c * G, G), 0:D],
                                               pC[:, :].rearrange("p (g d) -> p g d", d=D), ACT.Copy).then_inc(s_ce, 1)
                                eng.wait_ge(s_ce, c + 1)
                                eng.sem_inc(e["m"], 1)
                                ends_act(eng, i, u, e, D)
                            chunks(body)(act)

                        @block.sync
                        def _(sp):
                            chunks(lambda eng, i, u: ends_sp(eng, i, u, e, D))(sp)
                            ends_sp_done(sp, e)

            weighted()
        carries("l1f", D)

        def tails():
            st = phase()
            with st:
                nm = norm_setup(st, "l1g_nm", G)
                q = tail_setup(st, "l1g_t")
                s = dict(S=sb_in(st, "l1g_S", [P, 2, G, P]),
                         C=sb_in(st, "l1g_C", [P, 2, G, W1]),
                         z=sem("l1g_z"), ld=[sem(f"l1g_ld{u}") for u in range(2)], s=sem("l1g_S"),
                         fr=sem("l1g_fr"))
                h = sb_in(st, "l1g_h", [P, G, D])
                s_x = sem("l1g_x"); s_st = sem("l1g_st")
                PER = 2 * (NORM_STEPS + TAIL_STEPS + 2)
                with nc.Block() as block:
                    @block.sync
                    def _(sp):
                        sp.wait_ge(s["z"], 1)
                        chunks(lambda eng, i, u: sums_sp(eng, i, u, s, D))(sp)

                    @block.vector
                    def _(dve):
                        step = Steps(dve, "l1g_dve")
                        dve.sem_inc(s["fr"], 2)
                        dve.sem_inc(q["done"], 1)
                        sums_start(dve, step, s)
                        def body(eng, i, u):
                            c = i * 2 + u
                            step.chunk(c, PER, 1)
                            sums_dve(eng, i, u, s)
                            for k, X in enumerate((XD, XS)):
                                xin = X[:, bass.ds(c * G, G), :]
                                norm_dve(eng, step, nm, c, xin, lambda xc, r: step(relu_into(eng, h[:, :, :])(xc, r)),
                                         w=c * 2 + k)
                                eng.sem_inc(q["h"], 1)
                                step(tail_dve(eng, step, q, c * 2 + k, xin, xin, 0))
                                if k == 0:
                                    eng.sem_inc(s["fr"], 1)
                                    eng.sem_inc(s_x, 1)
                            step.end()
                        chunks(body)(dve)

                    @block.scalar
                    def _(act):
                        def body(eng, i, u):
                            c = i * 2 + u
                            for k in range(2):
                                norm_act(eng, nm, w=c * 2 + k)
                                tail_act(eng, q, c * 2 + k)
                                if k == 0:
                                    eng.wait_ge(s_x, c + 1)
                                    eng.dma_start(T2[bass.ds(c * G * P, G * P), :].rearrange("(g p) d -> p g d", p=P),
                                                  XD[:, bass.ds(c * G, G), :]).then_inc(s_st, 16)
                        chunks(body)(act)
                        act.wait_ge(s_st, 16 * NCH)

                    @block.tensor
                    def _(pe):
                        def body(eng, i, u):
                            c = i * 2 + u
                            def conv():
                                eng.wait_ge(s["s"], c + 1)
                                for j in range(G):
                                    to = q["py"][:, j * D:(j + 1) * D]
                                    eng.matmul(to, s["S"][:, u, j, :],
                                               M[:, bass.ds(c * G + j, 1), 0:D].rearrange("p a d -> p (a d)"),
                                               start=False, stop=False)
                                    last = eng.matmul(to, s["S"][:, u, j, :], s["C"][:, u, j, 0:D],
                                                      start=False, stop=j == G - 1)
                                return last
                            tail_pe(eng, q, c * 2, h, BDj, extra=conv)
                            tail_pe(eng, q, c * 2 + 1, h, BDc)
                        chunks(body)(pe)

        tails()
        if STOP == "l1":
            return

        srcF, idY, csI, cdI, srcS = source_columns(top, 2)
        move_columns((srcF, idY, csI, cdI, srcS), False)

        def scatter_sums():
            st = phase()
            with st:
                nm = norm_setup(st, "l2a_nm", G)
                S2 = sb_in(st, "l2a_S", [P, 2, G, P])
                m = sb_in(st, "l2a_m", [P, 2, G, D])
                R = sb_in(st, "l2a_R", [P, 2, G, D])
                idx = sb_in(st, "l2a_idx", [P, 2, G], i32)
                pS = ps_in(st, "l2a_pS", [P, 2, 512])
                s_sr = [sem(f"l2a_src{u}") for u in range(2)]; s_sf = sem("l2a_sfree"); s_m = sem("l2a_m")
                s_d = sem("l2a_sums"); s_r = sem("l2a_rows"); s_i = sem("l2a_idx"); s_go = sem("l2a_go")
                s_y = [sem(f"l2a_y{k}") for k in range(NY)]
                with nc.Block() as block:
                    @block.sync
                    def _(sp):
                        def body(eng, i, u):
                            c = i * 2 + u
                            eng.wait_ge(s_sf, c + 1)
                            eng.dma_start(S2[:, u].rearrange("p g j -> p (g j)"),
                                          srcP[bass.ds(c * G * P, G * P)].rearrange("(a n) -> a n", a=1)
                                          .broadcast_to([P, G * P])).then_inc(s_sr[u], 16)
                        chunks(body)(sp)

                    @block.vector
                    def _(dve):
                        step = Steps(dve, "l2a_dve")
                        def body(eng, i, u):
                            c = i * 2 + u
                            step.chunk(c, NORM_STEPS + 3)
                            norm_dve(eng, step, nm, c, XD[:, bass.ds(c * G, G), :],
                                     lambda xc, r: step(relu_into(eng, m[:, u])(xc, r)), w=c)
                            step(eng.tensor_tensor(m[:, u], m[:, u], bc(ewF[:, bass.ds(c * G, G)], 2, [P, G, D]), ALU.mult))
                            eng.wait_ge(s_sr[u], (i + 1) * 16)
                            step(eng.tensor_tensor(S2[:, u], S2[:, u], bc(srcF[:, bass.ds(c * G, G)], 2, [P, G, P]),
                                                   ALU.is_equal))
                            eng.sem_inc(s_m, 1)
                            step.end()
                        chunks(body)(dve)

                    @block.tensor
                    def _(pe):
                        pe.sem_inc(s_sf, 2)
                        def body(eng, i, u):
                            c = i * 2 + u
                            eng.wait_ge(s_m, c + 1)
                            eng.wait_ge(s_go, c)
                            for j in range(G):
                                last = eng.matmul(pS[:, u, j * D:(j + 1) * D], S2[:, u, j, :], m[:, u, j, :],
                                                  start=True, stop=True)
                            last.then_inc(s_d, 1)
                            eng.wait_ge(s_d, c + 1)
                            eng.sem_inc(s_sf, 1)
                        chunks(body)(pe)

                    @block.scalar
                    def _(act):
                        def body(eng, i, u):
                            c = i * 2 + u
                            norm_act(eng, nm, w=c)
                            eng.wait_ge(s_d, c + 1)
                            for k in range(NY):
                                eng.wait_ge(s_y[k], i * 64)
                            eng.activation(R[:, u], pS[:, u, :].rearrange("p (g d) -> p g d", d=D),
                                           ACT.Copy).then_inc(s_go, 1)
                        chunks(body)(act)

                    @block.gpsimd
                    def _(pool):
                        def body(eng, i, u):
                            c = i * 2 + u
                            for k in range(NY):
                                eng.wait_ge(s_y[k], i * 64)
                            eng.tensor_copy(idx[:, u, :], idY[:, bass.ds(c * G, G)]).then_inc(s_i, 1)
                            eng.wait_ge(s_i, c + 1)
                            eng.wait_ge(s_go, c + 1)
                            for j in range(G):
                                k = j % NY
                                eng.wait_ge(s_y[k], c * 32 + j // NY * 16)
                                eng.sem_inc(s_r, 1)
                                eng.indirect_dma_start(
                                    out=Yk[k], out_offset=bass.IndirectOffsetOnAxis(ap=idx[:, u, j:j + 1], axis=0),
                                    in_=R[:, u, j, :], in_offset=None, compute_op=ALU.add).then_inc(s_y[k], 16)
                        chunks(body)(pool)
                        for k in range(NY):
                            pool.wait_ge(s_y[k], 32 * NCH)

        scatter_sums()

        def combine():
            with phase(), nc.Block() as block:
                s_a = sem("cb_add"); s_o = sem("cb_out")
                part = M[:, :, :].rearrange("p t d -> p (t d)")[:, 0:YR // P * D]

                @block.gpsimd
                def _(pool):
                    for k in range(NY):
                        of = Yk[k].rearrange("(p r) d -> p (r d)", p=P)
                        if k == 0:
                            pool.dma_start(part, of, max_dma_last_dim=8192).then_inc(s_a, 16)
                        else:
                            pool.dma_start(part, of, accum_op=ALU.add, max_dma_last_dim=8192).then_inc(s_a, 16)
                        pool.wait_ge(s_a, 16 * (k + 1))
                    pool.dma_start(Y.rearrange("(p r) d -> p (r d)", p=P), part).then_inc(s_o, 16)
                    pool.wait_ge(s_o, 16)

        combine()

        def add_rows():
            st = phase()
            with st:
                gm = gather_setup(st, "l2g_m", D); gs = gather_setup(st, "l2g_s", D)
                gd = gather_setup(st, "l2g_d", D)
                zr = sb_in(st, "l2g_zero", [P, G, D])
                s_x = sem("l2g_x"); s_z = sem("l2g_z")
                with nc.Block() as block:
                    @block.gpsimd
                    def _(pool):
                        last_row = pool.to_reg(NT * P - 1)
                        pool.memset(zr[:, :, :], 0.0).then_inc(s_z, 1)
                        pool.wait_ge(s_z, 1)
                        def body(eng, i, u):
                            gather_chunk(eng, i, u, gm, T2, riI, last_row, old=XS)
                            gather_chunk(eng, i, u, gs, Y, csI, last_row, old=zr)
                            gather_chunk(eng, i, u, gd, Y, cdI, last_row, old=zr)
                        chunks(body)(pool)

                    @block.vector
                    def _(dve):
                        for g in (gm, gs, gd):
                            dve.sem_inc(g["free"], 2)
                        def body(eng, i, u):
                            c = i * 2 + u
                            xs, xd = XS[:, bass.ds(c * G, G), :], XD[:, bass.ds(c * G, G), :]
                            for g in (gm, gs, gd):
                                eng.wait_ge(g["sems"][u], (i + 1) * (16 * G))
                            eng.tensor_tensor(xs, gm["ring"][:, u], gs["ring"][:, u], ALU.add)
                            eng.tensor_tensor(xd, xd, gd["ring"][:, u], ALU.add).then_inc(s_x, 1)
                            eng.wait_ge(s_x, c + 1)
                            for g in (gm, gs, gd):
                                eng.sem_inc(g["free"], 1)
                        chunks(body)(dve)

        add_rows()

        def degrees():
            with phase(), nc.Block() as block:
                s_a, s_b = sem("dg_a"), sem("dg_b")

                @block.scalar
                def _(act):
                    act.activation(RC[:, :], RC[:, :], ACT.Sqrt).then_inc(s_a, 1)
                    act.activation(OD[:, :], OD[:, :], ACT.Sqrt).then_inc(s_a, 1)

                @block.vector
                def _(dve):
                    dve.wait_ge(s_a, 2)
                    dve.reciprocal(OD[:, :], OD[:, :]).then_inc(s_b, 1)

        degrees()

        def scale_out(eng, step, c, to, xc, r):
            step(relu_into(eng, to)(xc, r))
            step(eng.tensor_tensor(to, to, bc(OD[:, bass.ds(c * G, G)], 2, [P, G, D]), ALU.mult))

        norms_and_ends("l3a", scale_out, 1, w=D, lone=True)
        carries("l3b", D)

        def last_layer():
            st = phase()
            with st:
                q = sums_setup(st, "l3c_s")
                a = sb_in(st, "l3c_a", [P, G, D])
                aT = sb_in(st, "l3c_aT", [P, 4 * P])
                R = sb_in(st, "l3c_R", [P, 2, G, D])
                idx = sb_in(st, "l3c_idx", [P, 2, G], i32)
                pT = ps_in(st, "l3c_pT", [P, 512]); pY = ps_in(st, "l3c_pY", [P, 512])
                s_a = sem("l3c_a"); s_t = sem("l3c_t"); s_tc = sem("l3c_tc"); s_y = sem("l3c_y")
                s_r = sem("l3c_r"); s_i = sem("l3c_i"); s_go = sem("l3c_go"); s_sc = [sem(f"l3c_sc{u}") for u in range(2)]
                with nc.Block() as block:
                    @block.sync
                    def _(sp):
                        sp.wait_ge(q["z"], 1)
                        chunks(lambda eng, i, u: sums_sp(eng, i, u, q, D))(sp)

                    @block.vector
                    def _(dve):
                        step = Steps(dve, "l3c_dve")
                        dve.sem_inc(q["fr"], 2)
                        sums_start(dve, step, q)
                        def body(eng, i, u):
                            c = i * 2 + u
                            step.chunk(c, 3, 1)
                            sums_dve(eng, i, u, q)
                            eng.wait_ge(q["d"], c + 1)
                            step(eng.tensor_tensor(v4(a[:, :, :]), sums_view(q, u, D),
                                                   v4(bc(RC[:, bass.ds(c * G, G)], 2, [P, G, D])), ALU.mult))
                            eng.sem_inc(q["fr"], 1)
                            eng.sem_inc(s_a, 1)
                            eng.wait_ge(s_y, c + 1)
                            eng.wait_ge(s_sc[u], i * (16 * G))
                            step(eng.tensor_scalar(R[:, u], pY[:, :].rearrange("p (g d) -> p g d", d=D), 0.0, None, ALU.max))
                            step(eng.tensor_tensor(R[:, u], R[:, u], XD[:, bass.ds(c * G, G), :], ALU.add))
                            eng.sem_inc(s_r, 1)
                            step.end()
                        chunks(body)(dve)

                    @block.scalar
                    def _(act):
                        def body(eng, i, u):
                            c = i * 2 + u
                            eng.wait_ge(s_t, c + 1)
                            eng.activation(aT[:, :], pT[:, :], ACT.Copy).then_inc(s_tc, 1)
                        chunks(body)(act)

                    @block.tensor
                    def _(pe):
                        def body(eng, i, u):
                            c = i * 2 + u
                            sums_pe(eng, i, u, q, D)
                            eng.wait_ge(s_a, c + 1)
                            for j in range(4):
                                last = eng.transpose(pT[:, j * P:(j + 1) * P],
                                                     a[:, 2 * j:2 * j + 2, :].rearrange("p a d -> p (a d)"), ident[:, :])
                            last.then_inc(s_t, 1)
                            eng.wait_ge(s_tc, c + 1)
                            eng.wait_ge(s_r, c)
                            eng.matmul(pY[:, :], ones[0:1, :], bias8(3),
                                       start=True, stop=False)
                            for j in range(4):
                                last = eng.matmul(pY[:, j * P:(j + 1) * P], aT[:, j * P:(j + 1) * P], BD3[:, :],
                                                  start=False, stop=j == 3)
                            last.then_inc(s_y, 1)
                        chunks(body)(pe)

                    @block.gpsimd
                    def _(pool):
                        last_row = pool.to_reg(N - 1)
                        def body(eng, i, u):
                            c = i * 2 + u
                            eng.wait_ge(s_sc[u], i * (16 * G))
                            eng.tensor_copy(idx[:, u, :], dstS[:, bass.ds(c * G, G)]).then_inc(s_i, 1)
                            eng.wait_ge(s_i, c + 1)
                            eng.wait_ge(s_r, c + 1)
                            eng.sem_inc(s_go, 1)
                            for j in range(G):
                                eng.indirect_dma_start(
                                    out=out, out_offset=bass.IndirectOffsetOnAxis(ap=idx[:, u, j:j + 1], axis=0),
                                    in_=R[:, u, j, :], in_offset=None, bounds_check=last_row,
                                    oob_is_err=False).then_inc(s_sc[u], 16)
                        chunks(body)(pool)
                        pool.wait_ge(s_sc[0], 16 * G * (NCH // 2 + 1))
                        pool.wait_ge(s_sc[1], 16 * G * (NCH // 2))

        last_layer()


def kernel(**inputs):
    import numpy as _np
    import concourse.bacc as _bacc
    from concourse import mybir as _mybir
    from concourse.bass_utils import run_bass_kernel_spmd as _run

    nc = _bacc.Bacc("TRN2", target_bir_lowering=False, num_devices=1)
    arrays, args = {}, []
    for name in _INS:
        a = _np.ascontiguousarray(inputs[name])
        arrays[f"in_{name}_dram"] = a
        args.append(nc.dram_tensor(f"in_{name}_dram", a.shape, _mybir.dt.from_np(a.dtype), kind="ExternalInput").ap())
    shape = inputs["x"].shape
    args.append(nc.dram_tensor("out_0_dram", shape, _mybir.dt.float32, kind="ExternalOutput").ap())
    gnn_program(nc, *args)
    r = _run(nc, [arrays], core_ids=[0])
    return r.results[0]["out_0_dram"]
```

```python
import concourse.bass as bass
from concourse import mybir
from contextlib import ExitStack

_INS = ["x", "src", "dst", "edge_attr_64", "edge_weight", "L1_gnn_Wl", "L1_gnn_bl", "L1_gnn_Wr", "L1_gnn_br",
        "L1_gnn_We", "L1_gnn_att", "L1_gnn_conv_bias", "L1_gnn_ln_g", "L1_gnn_ln_b", "L1_gnn_ln1_g",
        "L1_gnn_ln1_b", "L1_gnn_fc_w", "L1_gnn_fc_b", "L1_gnn_fc1_w", "L1_gnn_fc1_b", "L3_gnn_W", "L3_gnn_b"]


def gnn_program(nc, x, src, dst, edge_attr, edge_weight, Wl, bl, Wr, br, We, att, conv_bias,
                ln_g, ln_b, ln1_g, ln1_b, fc_w, fc_b, fc1_w, fc1_b, W3, b3, out, STOP=None):
    f32, i32, f16, bf16 = mybir.dt.float32, mybir.dt.int32, mybir.dt.float16, mybir.dt.bfloat16
    ALU = mybir.AluOpType
    ACT = mybir.ActivationFunctionType
    AX = mybir.AxisListType

    N, D = x.shape
    E = src.shape[0]
    H = att.shape[0]
    HC = H * D
    P = 128
    G = 8
    NT = 200
    NCH = NT // G
    HALF = NT // 2
    NP = 125
    NN = N // NP
    PAD = 65535
    FAR = 1 << 20
    BIG = 1.0e30
    EPS = 1e-5
    W1 = D + 1
    RW = D + 4
    full_rows, rest = E // P, E % P
    assert NP * NN == N and NT * P >= E and NT == NCH * G and D == 64 and P == 2 * D

    dstP = nc.dram_tensor("dstP", (NT * P,), f32, kind="Internal").ap()
    srcP = nc.dram_tensor("srcP", (NT * P,), f32, kind="Internal").ap()
    NY = 4
    YR = NT * P + P
    Yk = [nc.dram_tensor(f"Y{k}", (YR, D), f32, kind="Internal").ap() for k in range(NY)]
    Y = nc.dram_tensor("Y", (YR, D), f32, kind="Internal").ap()
    XT = nc.dram_tensor("XT", (N, RW), f32, kind="Internal").ap()
    T1 = nc.dram_tensor("T1", (NT * P, D), f32, kind="Internal").ap()
    T2 = nc.dram_tensor("T2", (NT * P, D), f32, kind="Internal").ap()
    FLd = nc.dram_tensor("FLd", (2, NT, W1), f32, kind="Internal").ap()
    CAd = nc.dram_tensor("CAd", (2, NT, W1), f32, kind="Internal").ap()
    SPT = -(-6 * (NT // 25) * P // W1)
    Msp = nc.dram_tensor("Msp", (P, SPT, W1), f32, kind="Internal").ap()
    SMd = nc.dram_tensor("SMd", (2, NT * H), f32, kind="Internal").ap()
    SCd = nc.dram_tensor("SCd", (2, NT * H), f32, kind="Internal").ap()

    SFd = nc.dram_tensor("SFd", (3, P, NT), f32, kind="Internal").ap()
    SId = nc.dram_tensor("SId", (5, P, NT), i32, kind="Internal").ap()

    top = ExitStack()

    def sb_in(stack, name, shape, dt=f32):
        return stack.enter_context(nc.sbuf_tensor(name, shape, dt))

    def ps_in(stack, name, shape, dt=f32):
        return stack.enter_context(nc.psum_tensor(name, shape, dt))

    def sem(name):
        s = nc.alloc_semaphore(name)
        phase_sems.append(s)
        return s

    phase_sems = []

    def phase():
        phase_sems.clear()
        stack = ExitStack()

        def end():
            nc.clear_and_free_semaphores(list(phase_sems))
            nc.all_engine_barrier()
        stack.callback(end)
        return stack

    def bc(ap, dim, shape):
        return ap.unsqueeze(dim).broadcast_to(shape)

    class Steps:

        def __init__(self, eng, name):
            self.eng, self.sem, self.base, self.k, self.before = eng, sem(name), 0, 0, None

        def __call__(self, ins):
            ins.then_inc(self.sem, 1)
            self.k += 1
            self.eng.wait_ge(self.sem, self.base + self.k)

        def chunk(self, c, per, before=0):
            self.base, self.k, self.per = c * per + before, 0, per

        def end(self):
            assert self.k == self.per, self.k

        def turn(self, w, per, begins):
            if begins:
                if self.before is None:
                    self.before = self.k
                self.base, self.k = self.before + (w - 2) * per, 0

    def chunks(body):
        def run(eng):
            with eng.Fori(0, NCH // 2) as i:
                body(eng, i, 0)
                body(eng, i, 1)
            body(eng, NCH // 2, 0)
        return run

    def chunks_ahead(one, rest):
        def run(eng):
            one(eng, 0, 0)
            with eng.Fori(0, NCH // 2) as i:
                one(eng, i, 1)
                rest(eng, i, 0)
                one(eng, i + 1, 0)
                rest(eng, i, 1)
            rest(eng, NCH // 2, 0)
        return run

    with top:
        sb = lambda name, shape, dt=f32: sb_in(top, name, shape, dt)
        XS = sb("XS", [P, NT, D])
        XD = sb("XD", [P, NT, D])
        M = sb("M", [P, NT, W1])
        ident = sb("ident", [P, P])
        dstF = sb("dstF", [P, NT])
        repF = sb("repF", [P, NT])
        riI = sb("riI", [P, NT], i32)
        RC = sb("RC", [P, NT])
        RCM = sb("RCM", [P, NT])
        SFL = sb("SFL", [P, NT, 2])
        BLF = sb("BLF", [HALF, 2, NT])
        BFL = sb("BFL", [HALF, 2, NT])
        eps = sb("eps", [P, 1])
        ones = sb("ones", [1, P])
        BDc = sb("BDc", [P, P])
        BDj = sb("BDj", [P, P])
        BD2 = sb("BD2", [P, P])
        g1B = sb("g1B", [P, D])
        BD3 = sb("BD3", [P, P])
        biasR = sb("biasR", [3, 3, D], bf16)
        ones3 = sb("ones3", [3, P], bf16)
        cD = sb("cD", [P, 3, D])
        WA = sb("WA", [P, HC])
        WBr = sb("WBr", [D, HC])
        WS = sb("WS", [P, HC])
        WlS = sb("WlS", [P, 3, D])
        attC = sb("attC", [P, 3, H])
        mb = sb("mb", [P, 3])
        def source_columns(stack, n):
            srcF = sb_in(stack, f"srcF{n}", [P, NT])
            idY = sb_in(stack, f"idY{n}", [P, NT], i32)
            csI = sb_in(stack, f"csI{n}", [P, NT], i32)
            cdI = sb_in(stack, f"cdI{n}", [P, NT], i32)
            srcS = sb_in(stack, f"srcS{n}", [P, NT], i32)
            ewF = sb_in(stack, f"ewF{n}", [P, NT])
            dstS = sb_in(stack, f"dstS{n}", [P, NT], i32)
            OD = sb_in(stack, f"OD{n}", [P, NT])
            return srcF, ewF, OD, idY, csI, cdI, srcS, dstS

        def move_columns(columns, out_of_chip):
            with phase(), nc.Block() as block:
                s_m = sem("mv_out" if out_of_chip else "mv_back")

                @block.sync
                def _(sp):
                    for n, col in enumerate(columns):
                        kept = SFd[n] if n < 3 else SId[n - 3]
                        to, of = (kept, col[:, :]) if out_of_chip else (col[:, :], kept)
                        sp.dma_start(to, of).then_inc(s_m, 16)
                    sp.wait_ge(s_m, 16 * len(columns))

        columns_st = ExitStack()
        columns = source_columns(columns_st, 1)
        srcF, ewF, OD, idY, csI, cdI, srcS, dstS = columns
        early = ExitStack()
        srcG = sb_in(early, "srcG", [P, NT], i32)
        dstG = sb_in(early, "dstG", [P, NT], i32)
        RI = sb_in(early, "RI", [P, NT])
        CS = sb_in(early, "CS", [P, NT])
        CD = sb_in(early, "CD", [P, NT])
        tab_st = ExitStack()
        TAB = sb_in(tab_st, "TAB", [P, 3, NN])

        def bias8(n):
            return biasR[0:3, n, :].unsqueeze(1).broadcast_to([3, G, D])

        def load_rows(eng, to, of, count, s):
            rows, last = count // P, count % P
            eng.dma_start(to[0:HALF, 0, :], of[0:HALF * P].rearrange("(p j) -> p j", j=P)).then_inc(s, 16)
            eng.dma_start(to[0:rows - HALF, 1, :],
                          of[HALF * P:rows * P].rearrange("(p j) -> p j", j=P)).then_inc(s, 16)
            eng.dma_start(to[rows - HALF:rows - HALF + 1, 1, 0:last],
                          of[rows * P:count].rearrange("(p j) -> p j", p=1)).then_inc(s, 16)

        def borrowed():
            flat = XS[:, :, :].rearrange("p t d -> p (t d)")
            used = [0]

            def room(shape):
                n = 1
                for v in shape[1:]:
                    n *= v
                ap = flat[0:shape[0], used[0]:used[0] + n]
                used[0] += n
                assert used[0] <= NT * D
                names = "abc"[:len(shape) - 1]
                return ap if len(shape) == 2 else ap.rearrange(
                    f"p ({' '.join(names)}) -> p {' '.join(names)}", **dict(zip(names[1:], shape[2:])))
            return room

        def setup():
            st = phase()
            with st:
                t = lambda name, shape, dt=f32: sb_in(st, name, shape, dt)
                rI = t("rI", [HALF, 3, 2, P], i32)
                room = borrowed()
                rF = room([HALF, 5, 2, P])
                kb = room([HALF, 2, 2, P])
                kFr = room([P, NT])
                kLr = room([P, NT])
                bd = room([P, 3, NT])
                wl = room([D, H, D]); wr = room([D, H, D])
                fw = room([D, P]); fwT = room([P, D]); f1 = room([P, D])
                fbc = room([P, 1]); gcol = room([D, 1]); bcol = room([D, 1])
                w = room([D, 6, D]); wst = room([D, 4, 1])
                w3 = room([D, D])
                rows = room([1, 8, D]); blr = room([1, H, D]); rst = room([1, 4])
                bcolsl = room([P, 3]); bcolsr = room([P, 3])
                g1b = room([P, D])
                b3b = room([P, D])
                b1b = room([P, D])
                bsum = room([1, 3, D]); bback = room([1, 3, D])
                bpart = t("bpart", [1, 3, 3, D], bf16)
                s_bp = sem("su_biasparts")
                pI = ps_in(st, "pI", [P, 4, 512])
                pK = ps_in(st, "pK", [P, 2, 512])
                pW = ps_in(st, "pW", [P, 2, 512])
                s_zero = sem("su_zero"); s_in = sem("su_in"); s_w = sem("su_w")
                s_fl = sem("su_floats"); s_id = sem("su_ident"); s_tp = sem("su_transposed")
                s_kb = sem("su_keys"); s_kr = sem("su_keyrows"); s_b = sem("su_masks"); s_out = sem("su_out")
                s_w1 = sem("su_w1"); s_w2 = sem("su_w2"); s_w3 = sem("su_w3"); s_w4 = sem("su_w4")
                with nc.Block() as block:
                    @block.sync
                    def _(sp):
                        sp.wait_ge(s_zero, 1)
                        load_rows(sp, rI[:, 0], src, E, s_in)
                        load_rows(sp, rI[:, 1], dst, E, s_in)
                        load_rows(sp, rI[:, 2], dst[1:E], E - 1, s_in)
                        load_rows(sp, rF[:, 3], edge_weight, E, s_in)
                        sp.wait_ge(s_fl, 1)
                        sp.dma_start(dstP.rearrange("(c p j) -> p c j", c=2, j=P), rF[:, 1]).then_inc(s_out, 16)
                        sp.dma_start(srcP.rearrange("(c p j) -> p c j", c=2, j=P), rF[:, 0]).then_inc(s_out, 16)
                        sp.wait_ge(s_bp, 1)
                        for k in range(3):
                            sp.dma_start(biasR[k:k + 1, :, :], bpart[:, k, :, :]).then_inc(s_out, 16)
                        sp.wait_ge(s_out, 80)

                    @block.scalar
                    def _(act):
                        def ld(to, of):
                            act.dma_start(to, of).then_inc(s_w, 16)
                        row = lambda v: v.rearrange("(a n) -> a n", a=1)
                        col = lambda v: v.rearrange("(n a) -> n a", a=1)
                        act.wait_ge(s_zero, 1)
                        ld(wl[:, :, :], Wl.rearrange("k (h c) -> k h c", h=H))
                        ld(wr[:, :, :], Wr.rearrange("k (h c) -> k h c", h=H))
                        ld(WA[0:D, :], Wl); ld(WA[D:P, :], We); ld(WBr[:, :], Wr)
                        ld(WS[D:P, :], We)
                        ld(fw[:, :], fc_w); ld(f1[:, :], fc1_w); ld(w3[:, :], W3)
                        ld(fbc[:, :], col(fc_b)); ld(gcol[:, :], col(ln_g)); ld(bcol[:, :], col(ln_b))
                        ld(blr[:, :, :], bl.rearrange("(a h c) -> a h c", a=1, h=H))
                        ld(rows[:, 0, :], row(conv_bias)); ld(rows[:, 1, :], row(fc1_b))
                        ld(rows[:, 2, :], row(ln1_g)); ld(rows[:, 3, :], row(b3))
                        for h in range(H):
                            lo = D * (h % 2)
                            ld(attC[lo:lo + D, h // 2, h:h + 1], att[h:h + 1, :].rearrange("a c -> c a"))
                            ld(bcolsl[lo:lo + D, h // 2:h // 2 + 1], col(bl[h * D:(h + 1) * D]))
                            ld(bcolsr[lo:lo + D, h // 2:h // 2 + 1], col(br[h * D:(h + 1) * D]))
                            ld(WlS[lo:lo + D, h // 2, :], Wl[:, h * D:(h + 1) * D])
                        ld(g1b[:, :], row(ln1_g).broadcast_to([P, D]))
                        ld(b1b[:, :], row(ln1_b).broadcast_to([P, D]))
                        ld(b3b[:, :], row(b3).broadcast_to([P, D]))
                    NLOAD = 20 + 4 * H

                    @block.gpsimd
                    def _(pool):
                        pool.memset(ident[:, :], 0.0).then_inc(s_id, 1)
                        pool.wait_ge(s_id, 1)
                        pool.affine_select(out=ident[:, :], in_=ident[:, :], compare_op=ALU.not_equal, fill=1.0,
                                           base=0, pattern=[[-1, P]], channel_multiplier=1).then_inc(s_id, 1)
                        pool.wait_ge(s_b, 1)
                        for c in range(2):
                            pool.affine_select(out=BLF[:, c, :], in_=BLF[:, c, :], compare_op=ALU.is_gt, fill=0.0,
                                               base=-c * HALF, pattern=[[1, NT]], channel_multiplier=-1)
                            pool.affine_select(out=BFL[:, c, :], in_=BFL[:, c, :], compare_op=ALU.is_gt, fill=0.0,
                                               base=c * HALF, pattern=[[-1, NT]], channel_multiplier=1)

                    @block.vector
                    def _(dve):
                        step = Steps(dve, "su_dve")
                        dve.memset(rI[:, 0:2], PAD)
                        dve.memset(rI[:, 2], -1)
                        dve.memset(rF[:, 3], 0.0)
                        dve.memset(attC[:, :, :], 0.0)
                        dve.memset(mb[:, :], 0.0)
                        dve.memset(bcolsl[:, :], 0.0)
                        dve.memset(bcolsr[:, :], 0.0)
                        dve.memset(WlS[:, :, :], 0.0)
                        dve.memset(eps[:, :], EPS)
                        dve.memset(ones[:, :], 1.0)
                        dve.memset(ones3[:, :], 1.0)
                        for b_ in (BDc, BDj, BD2, BD3):
                            dve.memset(b_[:, :], 0.0)
                        step(dve.memset(rF[:, 4], 0.0))
                        dve.sem_inc(s_zero, 1)
                        dve.wait_ge(s_in, 16 * 12)
                        step(dve.tensor_copy(rF[:, 0:3].rearrange("p a c j -> p (a c j)"),
                                             rI[:, :].rearrange("p a c j -> p (a c j)")))
                        dve.sem_inc(s_fl, 1)
                        for k, end in enumerate((0, P - 1)):
                            for c in range(2):
                                dve.tensor_copy(kb[:, k, c, :],
                                                rF[:, 1, c, end:end + 1].broadcast_to([HALF, P]))
                        step(dve.tensor_tensor(rF[:, 4].rearrange("p c j -> p (c j)"),
                                               rF[:, 1].rearrange("p c j -> p (c j)"),
                                               rF[:, 2].rearrange("p c j -> p (c j)"), ALU.not_equal))
                        dve.sem_inc(s_kb, 1)
                        dve.wait_ge(s_tp, 1)
                        for n, to in enumerate((srcF, dstF, ewF, repF)):
                            dve.tensor_copy(to[:, :], pI[:, n, 0:NT])
                        dve.tensor_copy(kFr[:, :], pK[:, 0, 0:NT])
                        step(dve.tensor_copy(kLr[:, :], pK[:, 1, 0:NT]))
                        for c in range(2):
                            dve.tensor_scalar(BLF[:, c, :], kFr[0:HALF, :], rF[:, 1, c, P - 1:P], None, ALU.is_equal)
                            dve.tensor_scalar(BFL[:, c, :], kLr[0:HALF, :], rF[:, 1, c, 0:1], None, ALU.is_equal)
                        dve.tensor_tensor(SFL[:, :, 0], dstF[:, :], kFr[:, :], ALU.is_equal)
                        step(dve.tensor_tensor(SFL[:, :, 1], dstF[:, :], kLr[:, :], ALU.is_equal))
                        dve.sem_inc(s_b, 1)
                        for f, g in ((srcF, srcG), (dstF, dstG)):
                            step(dve.tensor_scalar(bd[:, 0, :], f[:, :], float(N), None, ALU.is_lt))
                            step(dve.tensor_tensor(bd[:, 1, :], bd[:, 0, :], f[:, :], ALU.mult))
                            step(dve.tensor_copy(g[:, :], bd[:, 1, :]))
                        step(dve.tensor_scalar(bd[:, 0, :], repF[:, :], -float(FAR), float(FAR), ALU.mult, ALU.add))
                        step(dve.tensor_tensor(bd[:, 1, :], bd[:, 0, :], dstF[:, :], ALU.add))
                        step(dve.tensor_copy(dstS[:, :], bd[:, 1, :]))
                        dve.wait_ge(s_w, 16 * NLOAD)
                        dve.wait_ge(s_id, 2)
                        I64 = ident[0:D, 0:D]

                        def centre(ap, acc):
                            step(dve.tensor_reduce(acc, ap, AX.X, ALU.add))
                            step(dve.tensor_scalar(acc, acc, -1.0 / D, None, ALU.mult))
                            step(dve.tensor_scalar(ap, ap, acc, None, ALU.add))

                        def mean_heads(to, of):
                            step(dve.tensor_tensor(to, of[:, 0, :], of[:, 1, :], ALU.add))
                            for h in range(2, H):
                                step(dve.tensor_tensor(to, to, of[:, h, :], ALU.add))
                            step(dve.tensor_scalar(to, to, 1.0 / H, None, ALU.mult))

                        def diagonal(bd_, ap):
                            dve.tensor_copy(bd_[0:D, 0:D], ap)
                            step(dve.tensor_copy(bd_[D:P, D:P], ap))

                        mean_heads(w[:, 0, :], wl)
                        step(dve.tensor_tensor(w[:, 0, :], w[:, 0, :], I64, ALU.add))
                        centre(w[:, 0, :], wst[:, 0, :])
                        diagonal(BDc, w[:, 0, :])
                        step(dve.tensor_copy(w[:, 1, :], I64))
                        centre(w[:, 1, :], wst[:, 1, :])
                        diagonal(BDj, w[:, 1, :])
                        diagonal(BD3, w3[:, :])
                        mean_heads(rows[:, 4, :], blr)
                        step(dve.tensor_tensor(rows[:, 4, :], rows[:, 4, :], rows[:, 0, :], ALU.add))
                        centre(rows[:, 4, :], rst[:, 0:1])
                        for k in range(3):
                            centre(WlS[:, k, :], bd[:, 2, k:k + 1])
                        step(dve.tensor_tensor(WS[0:D, :], wl[:, :, :].rearrange("k h c -> k (h c)"),
                                               wr[:, :, :].rearrange("k h c -> k (h c)"), ALU.add))
                        step(dve.tensor_tensor(mb[:, :], bcolsl[:, :], bcolsr[:, :], ALU.add))
                        dve.tensor_copy(cD[:, 0, :], b1b[:, :])
                        step(dve.tensor_scalar(cD[:, 2, :], b3b[:, :], 0.0, None, ALU.max))
                        step(dve.tensor_tensor(cD[:, 1, :], cD[:, 2, :], b1b[:, :], ALU.add))
                        dve.wait_ge(s_w1, 1)
                        step(dve.tensor_copy(fwT[:, :], pW[:, 0, 0:D]))
                        dve.sem_inc(s_w2, 1)
                        dve.wait_ge(s_w1, 2)
                        step(dve.tensor_tensor(w[:, 2, :], pW[0:D, 0, D:P], I64, ALU.add))
                        dve.sem_inc(s_w2, 1)
                        dve.wait_ge(s_w1, 3)
                        step(dve.tensor_tensor(rows[:, 5, :], pW[0:1, 1, 0:D], rows[:, 1, :], ALU.add))
                        centre(rows[:, 5, :], rst[:, 1:2])
                        centre(w[:, 2, :], wst[:, 2, :])
                        step(dve.tensor_scalar(w[:, 3, :], w[:, 2, :], gcol[:, :], None, ALU.mult))
                        diagonal(BD2, w[:, 3, :])
                        step(dve.tensor_copy(g1B[:, :], g1b[:, :]))
                        for n, r in enumerate((4, 5, 3)):
                            step(dve.tensor_copy(bsum[:, n, :], rows[:, r, :]))
                        for k in range(3):
                            step(dve.tensor_copy(bpart[:, k, :, :], bsum[:, :, :]))
                            step(dve.tensor_copy(bback[:, :, :], bpart[:, k, :, :]))
                            step(dve.tensor_tensor(bsum[:, :, :], bsum[:, :, :], bback[:, :, :], ALU.subtract))
                        dve.sem_inc(s_bp, 1)

                    @block.tensor
                    def _(pe):
                        pe.wait_ge(s_id, 2)
                        pe.wait_ge(s_kb, 1)
                        for n, r in enumerate((0, 1, 3, 4)):
                            for c in range(2):
                                pe.transpose(pI[:, n, c * HALF:(c + 1) * HALF], rF[:, r, c, :],
                                             ident[0:HALF, 0:HALF])
                        for k in range(2):
                            for c in range(2):
                                last = pe.matmul(pK[:, k, c * HALF:(c + 1) * HALF], kb[:, k, c, :],
                                                 ident[0:HALF, 0:HALF], start=True, stop=True)
                        last.then_inc(s_tp, 1)
                        pe.wait_ge(s_w, 16 * NLOAD)
                        pe.transpose(pW[:, 0, 0:D], fw[:, :], ident[0:D, 0:D]).then_inc(s_w1, 1)
                        pe.wait_ge(s_w2, 1)
                        pe.matmul(pW[0:D, 0, D:P], fwT[:, :], f1[:, :], start=True, stop=True).then_inc(s_w1, 1)
                        pe.wait_ge(s_w2, 2)
                        pe.matmul(pW[0:1, 1, 0:D], fbc[:, :], f1[:, :], start=True, stop=False)
                        pe.matmul(pW[0:1, 1, 0:D], bcol[:, :], w[:, 2, :], start=False, stop=True).then_inc(s_w1, 1)

        setup()

        def gather_setup(st, name, width, slots=2):
            return dict(ring=sb_in(st, name + "_ring", [P, slots, G, width]),
                        idx=sb_in(st, name + "_idx", [P, slots, G], i32),
                        sems=[sem(f"{name}_rows{u}") for u in range(slots)], free=sem(name + "_free"),
                        pool=sem(name + "_pool"), go=sem(name + "_go"), width=width)

        def gather_chunk(pool, i, u, g, table, index, bound, old=None):
            c = i * 2 + u
            per = 2 if old is not None else 1
            pool.wait_ge(g["free"], c + 1)
            pool.wait_ge(g["sems"][u], i * (16 * G))
            pool.tensor_copy(g["idx"][:, u, :], index[:, bass.ds(c * G, G)]).then_inc(g["pool"], 1)
            if old is not None:
                was = old[:, bass.ds(c * G, G), :] if old.shape[1] == NT else old[:, :, :]
                pool.tensor_copy(g["ring"][:, u, :, :], was).then_inc(g["pool"], 1)
            pool.wait_ge(g["pool"], c * per + per)
            pool.sem_inc(g["go"], 1)
            for j in range(G):
                pool.indirect_dma_start(
                    out=g["ring"][:, u, j, :], out_offset=None, in_=table,
                    in_offset=bass.IndirectOffsetOnAxis(ap=g["idx"][:, u, j:j + 1], axis=0),
                    bounds_check=bound, oob_is_err=False).then_inc(g["sems"][u], 16)

        def tables():
            st = phase()
            with st:
                t = lambda name, shape, dt=f32: sb_in(st, name, shape, dt)
                iN = t("iN", [P, NN], i32); loI = t("loI", [P, NN], f16)
                iH = t("iH", [P, P], i32); hiI = t("hiI", [P, P], f16)
                iT = t("iT", [P, NT], i32); iP = t("iP", [P, NT], i32)
                room = borrowed()
                tnum = room([P, NT]); pnum = room([P, NT])
                hi32 = t("hi32", [P, NT], i32)
                hi = room([P, 2, NT]); lo = room([P, 2, NT]); tmp = room([P, NT])
                U = 2
                ohl = t("ohl", [P, 2, U, 2, NN], f16)
                ohh = t("ohh", [P, 2, U, 3, P], f16)
                pT = ps_in(st, "pT", [P, 3, 512])
                lower = t("lower", [P, NP]); total = t("total", [P, 1]); offs = t("offs", [P, 1])
                has = room([P, 2, NN])
                pO = ps_in(st, "pO", [P, 512])
                s_lo = sem("tb_lower"); s_tot = sem("tb_total"); s_of = sem("tb_offsets")
                s_z = sem("tb_zero"); s_y = sem("tb_yzero")
                s_i = sem("tb_iota"); s_oh = sem("tb_onehots"); s_fr = sem("tb_free"); s_t = sem("tb_tables")
                TURNS = NT // U // 2
                with nc.Block() as block:
                    @block.gpsimd
                    def _(pool):
                        pool.iota(iN[:, :], [[1, NN]], channel_multiplier=0)
                        pool.iota(iH[:, :], [[1, P]], channel_multiplier=0)
                        pool.iota(iT[:, :], [[1, NT]], channel_multiplier=0)
                        pool.iota(iP[:, :], [[0, NT]], base=1, channel_multiplier=1).then_inc(s_i, 1)
                        pool.memset(lower[:, :], 1.0).then_inc(s_lo, 1)
                        pool.wait_ge(s_lo, 1)
                        pool.affine_select(out=lower[:, :], in_=lower[:, :], compare_op=ALU.is_gt, fill=0.0,
                                           base=0, pattern=[[1, NP]], channel_multiplier=-1).then_inc(s_lo, 1)

                    @block.sync
                    def _(sp):
                        sp.wait_ge(s_z, 1)
                        zeros = M[:, :, :].rearrange("p t d -> p (t d)")[:, 0:YR // P * D]
                        for k in range(NY):
                            sp.dma_start(Yk[k].rearrange("(p r) d -> p (r d)", p=P), zeros).then_inc(s_y, 16)
                        sp.wait_ge(s_y, 16 * NY)

                    @block.vector
                    def _(dve):
                        step = Steps(dve, "tb_dve")
                        step(dve.memset(M[:, :, :], 0.0))
                        dve.sem_inc(s_z, 1)
                        dve.wait_ge(s_i, 1)
                        dve.tensor_copy(loI[:, :], iN[:, :])
                        dve.tensor_copy(hiI[:, :], iH[:, :])
                        dve.tensor_copy(tnum[:, :], iT[:, :])
                        step(dve.tensor_copy(pnum[:, :], iP[:, :]))
                        for k, f in enumerate((srcF, dstF)):
                            step(dve.tensor_scalar(tmp[:, :], f[:, :], (1.0 - NN) / 2, 1.0 / NN, ALU.add, ALU.mult))
                            step(dve.tensor_copy(hi32[:, :], tmp[:, :]))
                            step(dve.tensor_copy(hi[:, k, :], hi32[:, :]))
                            step(dve.tensor_scalar(tmp[:, :], hi[:, k, :], -float(NN), None, ALU.mult))
                            step(dve.tensor_tensor(lo[:, k, :], tmp[:, :], f[:, :], ALU.add))
                        step(dve.tensor_tensor(tnum[:, :], tnum[:, :], repF[:, :], ALU.mult))
                        step(dve.tensor_tensor(pnum[:, :], pnum[:, :], repF[:, :], ALU.mult))

                        def body(i, u):
                            c = i * 2 + u
                            dve.wait_ge(s_fr, c + 1)
                            for j in range(U):
                                t_ = c * U + j
                                for k in range(2):
                                    dve.tensor_scalar(ohl[:, u, j, k, :], loI[:, :], lo[:, k, bass.ds(t_, 1)],
                                                      None, ALU.is_equal)
                                dve.tensor_scalar(ohh[:, u, j, 0, :], hiI[:, :], hi[:, 0, bass.ds(t_, 1)],
                                                  None, ALU.is_equal)
                                dve.tensor_scalar(ohh[:, u, j, 1, :], hiI[:, :], hi[:, 1, bass.ds(t_, 1)],
                                                  tnum[:, bass.ds(t_, 1)], ALU.is_equal, ALU.mult)
                                last = dve.tensor_scalar(ohh[:, u, j, 2, :], hiI[:, :], hi[:, 1, bass.ds(t_, 1)],
                                                         pnum[:, bass.ds(t_, 1)], ALU.is_equal, ALU.mult)
                            last.then_inc(s_oh, 1)
                        with dve.Fori(0, TURNS) as i:
                            body(i, 0)
                            body(i, 1)
                        dve.wait_ge(s_t, 1)
                        dve.tensor_copy(TAB[:, 1, :], pT[:, 0, 0:NN])
                        step(dve.tensor_scalar(TAB[:, 2, :], pT[:, 1, 0:NN], float(P), None, ALU.mult))
                        step(dve.tensor_tensor(TAB[:, 0, :], pT[:, 2, 0:NN], TAB[:, 2, :], ALU.add))
                        step(dve.tensor_scalar(has[:, 0, :], TAB[:, 1, :], 0.0, None, ALU.is_gt))
                        step(dve.memset(has[:, 1, :], 1.0))
                        step(dve.tensor_tensor_scan(TAB[:, 2, :], has[:, 1, :], has[:, 0, :], 0.0, ALU.mult, ALU.add))
                        step(dve.tensor_copy(total[:, :], TAB[:, 2, NN - 1:NN]))
                        dve.sem_inc(s_tot, 1)
                        dve.wait_ge(s_of, 1)
                        step(dve.tensor_copy(offs[0:NP, :], pO[0:NP, 0:1]))
                        step(dve.tensor_scalar(TAB[0:NP, 2, :], TAB[0:NP, 2, :], offs[0:NP, :], -1.0, ALU.add, ALU.add))
                        step(dve.tensor_scalar(has[:, 1, :], has[:, 0, :], -float(FAR), float(FAR), ALU.mult, ALU.add))
                        step(dve.tensor_tensor(TAB[:, 2, :], TAB[:, 2, :], has[:, 1, :], ALU.add))

                    @block.tensor
                    def _(pe):
                        pe.sem_inc(s_fr, 2)
                        def body(i, u, first=False, stop=False):
                            c = i * 2 + u
                            pe.wait_ge(s_oh, c + 1)
                            for j in range(U):
                                for n, (a, b) in enumerate(((0, 0), (1, 1), (2, 1))):
                                    last = pe.matmul(pT[:, n, 0:NN], ohh[:, u, j, a, :], ohl[:, u, j, b, :],
                                                     start=first and j == 0, stop=stop and j == U - 1)
                            last.then_inc(s_fr, 1)
                            return last
                        body(0, 0, first=True)
                        body(0, 1)
                        with pe.Fori(1, TURNS - 1) as i:
                            body(i, 0)
                            body(i, 1)
                        body(TURNS - 1, 0)
                        body(TURNS - 1, 1, stop=True)
                        pe.wait_ge(s_fr, 2 * TURNS + 2)
                        pe.sem_inc(s_t, 1)
                        pe.wait_ge(s_lo, 2)
                        pe.wait_ge(s_tot, 1)
                        pe.matmul(pO[0:NP, 0:1], lower[0:NP, :], total[0:NP, :], start=True, stop=True).then_inc(s_of, 1)

        tables()

        NB = NN // (2 * G)
        assert NB == NCH
        x_v = x.rearrange("(p n) d -> p n d", p=NP)
        out_v = out.rearrange("(p n) d -> p n d", p=NP)
        XT_v = XT.rearrange("(p n) d -> p n d", p=NP)
        CUT = 112

        def node_dma(eng, to, of, s):
            eng.dma_start(to[0:CUT], of[0:CUT]).then_inc(s, 16)
            eng.dma_start(to[CUT:NP], of[CUT:NP]).then_inc(s, 16)

        def widen():
            st = phase()
            with st:
                W = sb_in(st, "wd_W", [P, 2, 2 * G, RW])
                s_l = [sem(f"wd_load{u}") for u in range(2)]; s_s = [sem(f"wd_store{u}") for u in range(2)]
                s_z = sem("wd_zero"); s_c = sem("wd_cols")
                with nc.Block() as block:
                    @block.vector
                    def _(dve):
                        dve.memset(W[:, :, :, D + 3:RW], 0.0).then_inc(s_z, 1)
                        def body(eng, i, u):
                            c = i * 2 + u
                            eng.wait_ge(s_s[u], i * 32)
                            for k in range(3):
                                last = eng.tensor_scalar(W[:, u, :, D + k], TAB[:, k, bass.ds(c * 2 * G, 2 * G)],
                                                         1.0, None, ALU.mult)
                            last.then_inc(s_c, 1)
                        chunks(body)(dve)

                    @block.sync
                    def _(sp):
                        def body(eng, i, u):
                            c = i * 2 + u
                            eng.wait_ge(s_s[u], i * 32)
                            node_dma(eng, W[0:NP, u, :, 0:D], x_v[:, bass.ds(c * 2 * G, 2 * G), :], s_l[u])
                        chunks(body)(sp)

                    @block.scalar
                    def _(act):
                        act.wait_ge(s_z, 1)
                        def body(eng, i, u):
                            c = i * 2 + u
                            eng.wait_ge(s_c, c + 1)
                            eng.wait_ge(s_l[u], (i + 1) * 32)
                            node_dma(eng, XT_v[:, bass.ds(c * 2 * G, 2 * G), :], W[0:NP, u, :, :], s_s[u])
                        chunks(body)(act)
                        act.wait_ge(s_s[0], 32 * (NCH // 2 + 1))
                        act.wait_ge(s_s[1], 32 * (NCH // 2))

        widen()
        tab_st.close()

        def norm_setup(st, name, tiles, xc=None, sq=None):
            return dict(s=sb_in(st, name + "_s", [P, 4, tiles]),
                        xc=sb_in(st, name + "_xc", [P, tiles, D]) if xc is None else xc,
                        sq=sb_in(st, name + "_sq", [P, tiles, D]) if sq is None else sq, v=sem(name + "_var"), sd=sem(name + "_sd"))

        NORM_STEPS = 5

        def norm_dve(dve, step, n, c, xin, emit, p=P, tiles=G, w=0):
            s, xc, sq = n["s"], n["xc"], n["sq"]
            step(dve.tensor_reduce(s[0:p, 0, :], xin, AX.X, ALU.add))
            step(dve.tensor_scalar(s[0:p, 1, :], s[0:p, 0, :], -1.0 / D, None, ALU.mult))
            step(dve.tensor_tensor(xc[0:p], xin, bc(s[0:p, 1, :], 2, [p, tiles, D]), ALU.add))
            step(dve.tensor_tensor(sq[0:p], xc[0:p], xc[0:p], ALU.mult))
            dve.tensor_reduce(s[0:p, 2, :], sq[0:p], AX.X, ALU.add).then_inc(n["v"], 1)
            dve.wait_ge(n["sd"], w + 1)
            step(dve.reciprocal(s[0:p, 0, :], s[0:p, 3, :]))
            emit(xc[0:p], bc(s[0:p, 0, :], 2, [p, tiles, D]))

        def norm_act(act, n, p=P, w=0):
            act.wait_ge(n["v"], w + 1)
            act.activation(n["s"][0:p, 3, :], n["s"][0:p, 2, :], ACT.Sqrt, bias=eps[0:p, 0:1],
                           scale=1.0 / D).then_inc(n["sd"], 1)

        def relu_into(dve, to):
            return lambda xc, r: dve.scalar_tensor_tensor(to, xc, 0.0, r, ALU.max, ALU.mult)

        def tail_setup(st, name, get=None):
            get = get or (lambda k, shape: sb_in(st, f"{name}_{k}", shape)[:])
            q = {k: get(k, [P, G, D]) for k in ("xc", "sq0", "h", "sq1", "n", "sq2", "t")}
            q.update({k: get(k, [P, 4, P]) for k in ("hT", "nT")})
            q["XB"] = get("XB", [P, 2, G, D])
            q.update({k: sb_in(st, f"{name}_{k}", [P, 4, G]) for k in ("s0", "s1", "s2")})
            q.update({k: ps_in(st, f"{name}_{k}", [P, 512]) for k in ("ph", "pn", "py")})
            q["pz"] = ps_in(st, name + "_pz", [P, 2, 512])
            q.update({k: sem(f"{name}_{k}") for k in (
                "centred", "squared0", "var0", "dev0", "h_ready", "h_transposed", "hT_ready", "y_ready",
                "squared1", "var1", "dev1", "n_ready", "n_transposed", "nT_ready", "z_ready",
                "squared2", "var2", "dev2", "z_read")})
            return q

        def turns(turn):
            def run(eng):
                turn(eng, 0, 0, 0, True, False, False)
                turn(eng, 0, 0, 1, True, True, False)
                with eng.Fori(0, NCH // 2) as i:
                    for v in range(2):
                        for k in range(2):
                            turn(eng, i + v, 1 - v, k, True, True, True)
                turn(eng, NCH // 2, 1, 0, False, True, True)
                turn(eng, NCH // 2, 1, 1, False, False, True)
            return run

        def tail_pe(pe, q, w, k, flags, first, p=P, extra=None):
            one, two, _ = flags
            tr = lambda to, of: [pe.transpose(to[:, j * P:j * P + p],
                                              of[0:p, 2 * j:2 * j + 2, :].rearrange("p a d -> p (a d)"),
                                              ident[0:p, 0:p]) for j in range(4)][-1]
            if two:
                pe.wait_ge(q["n_ready"], w)
                tr(q["pn"], q["n"]).then_inc(q["n_transposed"], 1)
            if one:
                pe.wait_ge(q["h_ready"], w + 1)
                tr(q["ph"], q["h"]).then_inc(q["h_transposed"], 1)
            if two:
                pe.wait_ge(q["nT_ready"], w)
                pe.wait_ge(q["z_read"], w)
                to = q["pz"][:, 1 - k, :]
                pe.matmul(to[0:p, :], ones3[:, 0:p], bias8(1), start=True, stop=False)
                for j in range(4):
                    last = pe.matmul(to[0:p, j * P:(j + 1) * P], q["nT"][:, j, 0:p], BD2[:, :],
                                     start=False, stop=j == 3)
                last.then_inc(q["z_ready"], 1)
            if one:
                pe.wait_ge(q["hT_ready"], w + 1)
                pe.matmul(q["py"][0:p, :], ones3[:, 0:p], bias8(0), start=True, stop=False)
                for j in range(4):
                    last = pe.matmul(q["py"][0:p, j * P:(j + 1) * P], q["hT"][:, j, 0:p], first[:, :],
                                     start=False, stop=extra is None and j == 3)
                if extra is not None:
                    last = extra()
                last.then_inc(q["y_ready"], 1)

        def tail_act(act, q, w, k, flags, p=P):
            one, two, three = flags
            g3 = lambda a: a[0:p, :].rearrange("p (g d) -> p g d", d=D)
            c3 = lambda a: a[:, :].rearrange("q (j p) -> q j p", p=P)[:, :, 0:p]

            def root(s, n, at):
                act.wait_ge(q["var" + n], at)
                act.activation(s[0:p, 3, :], s[0:p, 2, :], ACT.Sqrt, bias=eps[0:p, 0:1],
                               scale=1.0 / D).then_inc(q["dev" + n], 1)
            if one:
                act.wait_ge(q["centred"], w + 1)
                act.activation(q["sq0"][0:p], q["xc"][0:p], ACT.Square).then_inc(q["squared0"], 1)
            if two:
                root(q["s1"], "1", w)
            if three:
                root(q["s2"], "2", w - 1)
            if one:
                root(q["s0"], "0", w + 1)
            if two:
                act.wait_ge(q["n_transposed"], w)
                act.activation(q["nT"][:, :, 0:p], c3(q["pn"]), ACT.Copy).then_inc(q["nT_ready"], 1)
            if one:
                act.wait_ge(q["h_transposed"], w + 1)
                act.activation(q["hT"][:, :, 0:p], c3(q["ph"]), ACT.Copy).then_inc(q["hT_ready"], 1)
            if two:
                act.wait_ge(q["z_ready"], w)
                act.activation(q["sq2"][0:p], g3(q["pz"][:, 1 - k, :]), ACT.Square).then_inc(q["squared2"], 1)
            if one:
                act.wait_ge(q["y_ready"], w + 1)
                act.activation(q["sq1"][0:p], g3(q["py"]), ACT.Square).then_inc(q["squared1"], 1)

        TAIL_STEPS = 9

        def tail_dve(dve, step, q, w, k, flags, xin, to, const, p=P):
            one, two, three = flags
            g3 = lambda a: a[0:p, :].rearrange("p (g d) -> p g d", d=D)
            s0, s1, s2 = q["s0"], q["s1"], q["s2"]
            by = lambda s, n: bc(s[0:p, n, :], 2, [p, G, D])
            if one:
                step(dve.tensor_reduce(s0[0:p, 0, :], xin, AX.X, ALU.add))
                step(dve.tensor_scalar(s0[0:p, 1, :], s0[0:p, 0, :], -1.0 / D, None, ALU.mult))
                dve.tensor_tensor(q["xc"][0:p], xin, by(s0, 1), ALU.add).then_inc(q["centred"], 1)
            if two:
                dve.wait_ge(q["squared1"], w)
                dve.tensor_reduce(s1[0:p, 2, :], q["sq1"][0:p], AX.X, ALU.add).then_inc(q["var1"], 1)
            if three:
                dve.wait_ge(q["squared2"], w - 1)
                dve.tensor_reduce(s2[0:p, 2, :], q["sq2"][0:p], AX.X, ALU.add).then_inc(q["var2"], 1)
            if one:
                dve.wait_ge(q["squared0"], w + 1)
                dve.tensor_reduce(s0[0:p, 2, :], q["sq0"][0:p], AX.X, ALU.add).then_inc(q["var0"], 1)
            if two:
                dve.wait_ge(q["dev1"], w)
                step(dve.reciprocal(s1[0:p, 0, :], s1[0:p, 3, :]))
                dve.tensor_tensor(q["n"][0:p], g3(q["py"]), by(s1, 0), ALU.mult).then_inc(q["n_ready"], 1)
            if one:
                dve.wait_ge(q["dev0"], w + 1)
                step(dve.reciprocal(s0[0:p, 0, :], s0[0:p, 3, :]))
                dve.scalar_tensor_tensor(q["h"][0:p], q["xc"][0:p], 0.0, by(s0, 0), ALU.max, ALU.mult)\
                    .then_inc(q["h_ready"], 1)
            if three:
                dve.wait_ge(q["dev2"], w - 1)
                step(dve.reciprocal(s2[0:p, 0, :], s2[0:p, 3, :]))
                step(dve.tensor_tensor(q["t"][0:p], g3(q["pz"][:, k, :]), by(s2, 0), ALU.mult))
                dve.sem_inc(q["z_read"], 1)
                step(dve.tensor_tensor(q["t"][0:p], q["t"][0:p], bc(g1B[0:p, :], 1, [p, G, D]), ALU.mult))
                step(dve.tensor_tensor(to, q["t"][0:p], q["XB"][0:p, k], ALU.add))
            if one:
                step(dve.tensor_tensor(q["XB"][0:p, k], xin, bc(cD[0:p, const, :], 1, [p, G, D]), ALU.add))

        def dense():
            st = phase()
            with st:
                g1 = gather_setup(st, "g1", RW)
                g0 = gather_setup(st, "g0", RW)
                flat = M[:, :, :].rearrange("p t d -> p (t d)")
                XR = flat[:, 0:8 * G * D].rearrange("p (a u g d) -> p a u g d", a=2, u=2, d=D)
                X, R = XR[:, 0], XR[:, 1]
                used = [8 * G * D]

                def get(key, shape):
                    n = 1
                    for v in shape[1:]:
                        n *= v
                    used[0] += n
                    ap = flat[:, used[0] - n:used[0]]
                    names = "abc"[:len(shape) - 1]
                    return ap.rearrange(f"p ({' '.join(names)}) -> p {' '.join(names)}",
                                        **dict(zip(names[1:], shape[2:])))
                q = tail_setup(st, "dn", get)
                s_l = [sem(f"dn_load{u}") for u in range(2)]; s_st = [sem(f"dn_store{u}") for u in range(2)]
                s_x = sem("dn_xfree"); s_r = sem("dn_result")
                with nc.Block() as block:
                    @block.gpsimd
                    def _(pool):
                        last_row = pool.to_reg(N - 1)
                        def body(eng, i, u):
                            gather_chunk(eng, i, u, g1, XT, srcG, last_row)
                            gather_chunk(eng, i, u, g0, XT, dstG, last_row)
                        chunks(body)(pool)

                    @block.sync
                    def _(sp):
                        nodes = lambda v, c: v[:, bass.ds(c * 2 * G, 2 * G), :]
                        for c in range(2):
                            node_dma(sp, X[0:NP, c], nodes(x_v, c), s_l[c])
                        def body(c, u, load=True):
                            if load:
                                sp.wait_ge(s_x, c - 1)
                                node_dma(sp, X[0:NP, u], nodes(x_v, c), s_l[u])
                            sp.wait_ge(s_r, c - 1)
                            node_dma(sp, nodes(out_v, c - 2), R[0:NP, u], s_st[u])
                        with sp.Fori(0, NCH // 2 - 1) as i:
                            for u in range(2):
                                body(i * 2 + 2 + u, u)
                        body(NCH - 1, 0)
                        body(NCH, 1, load=False)
                        body(NCH + 1, 0, load=False)
                        sp.wait_ge(s_st[0], 32 * (NCH // 2 + 2))
                        sp.wait_ge(s_st[1], 32 * (NCH // 2 + 1))

                    @block.vector
                    def _(dve):
                        step = Steps(dve, "dn_dve")
                        dve.sem_inc(q["z_read"], 2)
                        for u in range(2):
                            dve.sem_inc(s_st[u], 32)
                        def turn(eng, i, u, k, *flags):
                            w = (i * 2 + u) * 2 + k
                            step.turn(w, TAIL_STEPS, flags[2] and (flags[0] or k == 0))
                            if flags[0] and k == 0:
                                eng.wait_ge(s_l[u], (i + 1) * 32)
                            if flags[2] and k == 0:
                                eng.wait_ge(s_st[1 - u], (i + u) * 32)
                            tail_dve(eng, step, q, w, k, flags, X[0:NP, u, k * G:(k + 1) * G, :],
                                     R[0:NP, 1 - u, k * G:(k + 1) * G, :], 1, p=NP)
                            if k == 1:
                                if flags[0]:
                                    eng.sem_inc(s_x, 1)
                                if flags[2]:
                                    eng.sem_inc(s_r, 1)
                        turns(turn)(dve)

                    @block.scalar
                    def _(act):
                        act.sem_inc(g1["free"], 2)
                        act.sem_inc(g0["free"], 2)
                        def turn(eng, i, u, k, *flags):
                            c = i * 2 + u
                            tail_act(eng, q, c * 2 + k, k, flags, p=NP)
                            if flags[0]:
                                g = (g1, g0)[k]
                                eng.wait_ge(g["sems"][u], (i + 1) * (16 * G))
                                ring = g["ring"][:, u]
                                t_ = bass.ds(c * G, G)
                                if k == 0:
                                    eng.activation(XS[:, t_, :], ring[:, :, 0:D], ACT.Copy)
                                    eng.activation(RI[:, t_], ring[:, :, D], ACT.Copy)
                                    eng.activation(OD[:, t_], ring[:, :, D + 1], ACT.Copy)
                                    eng.activation(CS[:, t_], ring[:, :, D + 2], ACT.Copy).then_inc(g["free"], 1)
                                else:
                                    eng.activation(XD[:, t_, :], ring[:, :, 0:D], ACT.Copy)
                                    eng.activation(CD[:, t_], ring[:, :, D + 2], ACT.Copy).then_inc(g["free"], 1)
                        turns(turn)(act)

                    @block.tensor
                    def _(pe):
                        turns(lambda eng, i, u, k, *flags: tail_pe(eng, q, (i * 2 + u) * 2 + k, k, flags, BDc, p=NP))(pe)

        dense()
        if STOP == "dense":
            return

        def ends_setup(st, name):
            return dict(fl=sb_in(st, name + "_sfl", [P, 2, G, 2]), ev=sb_in(st, name + "_ev", [2, 2, G * W1]),
                        ps=ps_in(st, name + "_ps", [P, 2, 2, 512]), m=sem(name + "_m"), cp=sem(name + "_cp"), go=sem(name + "_go"),
                        d=sem(name + "_sums"), e=sem(name + "_evac"), st=[sem(f"{name}_st{u}") for u in range(2)])

        def ends_pe(pe, i, u, q, w=W1):
            c = i * 2 + u
            pe.wait_ge(q["m"], c + 1)
            pe.wait_ge(q["cp"], c + 1)
            pe.sem_inc(q["go"], 1)
            for j in range(G):
                last = pe.matmul(q["ps"][0:2, u, j // 4, (j % 4) * w:(j % 4 + 1) * w], q["fl"][:, u, j, :],
                                 M[:, bass.ds(c * G + j, 1), 0:w].rearrange("p a d -> p (a d)"),
                                 start=True, stop=True)
            last.then_inc(q["d"], 1)

        def ends_act_before(act, i, u, q):
            c = i * 2 + u
            act.activation(q["fl"][:, u], SFL[:, bass.ds(c * G, G), :], ACT.Copy).then_inc(q["cp"], 1)

        def ends_act(act, i, u, q, w=W1):
            c = i * 2 + u
            act.wait_ge(q["d"], c + 1)
            act.wait_ge(q["st"][u], i * 16)
            act.activation(q["ev"][:, u, 0:G * w].rearrange("k (b n) -> k b n", b=2), q["ps"][0:2, u, :, 0:4 * w], ACT.Copy).then_inc(q["e"], 1)

        def ends_sp(sp, i, u, q, w=W1):
            c = i * 2 + u
            sp.wait_ge(q["e"], c + 1)
            sp.dma_start(FLd[:, bass.ds(c * G, G), 0:w],
                         q["ev"][:, u, 0:G * w].rearrange("k (g d) -> k g d", d=w)).then_inc(q["st"][u], 16)

        def ends_sp_done(sp, q):
            sp.wait_ge(q["st"][0], 16 * (NCH // 2 + 1))
            sp.wait_ge(q["st"][1], 16 * (NCH // 2))

        def carries(name, w=W1):
            st = phase()
            with st:
                fl = sb_in(st, name + "_fl", [HALF, 2, 2, w])
                ca = sb_in(st, name + "_ca", [HALF, 2, 2, w])
                ps = ps_in(st, name + "_ps", [P, 2, 512])
                s_l, s_m, s_e, s_o = sem(name + "_l"), sem(name + "_m"), sem(name + "_e"), sem(name + "_o")
                with nc.Block() as block:
                    @block.sync
                    def _(sp):
                        for k in range(2):
                            sp.dma_start(fl[:, k], FLd[k, :, 0:w].rearrange("(c p) d -> p c d", c=2)).then_inc(s_l, 16)
                        sp.wait_ge(s_e, 1)
                        for k in range(2):
                            sp.dma_start(CAd[k, :, 0:w].rearrange("(c p) d -> p c d", c=2), ca[:, k]).then_inc(s_o, 16)
                        sp.wait_ge(s_o, 32)

                    @block.tensor
                    def _(pe):
                        pe.wait_ge(s_l, 32)
                        for k, (masks, end) in enumerate(((BLF, 1), (BFL, 0))):
                            for c in range(2):
                                for cc in range(2):
                                    last = pe.matmul(ps[0:HALF, k, c * w:(c + 1) * w],
                                                     masks[:, cc, c * HALF:(c + 1) * HALF], fl[:, end, cc, :],
                                                     start=cc == 0, stop=cc == 1)
                        last.then_inc(s_m, 1)

                    @block.vector
                    def _(dve):
                        dve.wait_ge(s_m, 1)
                        dve.tensor_copy(ca[:, :, :, :], ps[0:HALF, :, 0:2 * w].rearrange("p k (c d) -> p k c d", d=w))\
                            .then_inc(s_e, 1)

        def sums_setup(st, name):
            return dict(S=sb_in(st, name + "_S", [P, 2, G, P]),
                        C=sb_in(st, name + "_C", [P, 2, G, W1]), ps=ps_in(st, name + "_ps", [P, 2, 2, 512]),
                        z=sem(name + "_z"), ld=[sem(f"{name}_ld{u}") for u in range(2)], s=sem(name + "_S"),
                        d=sem(name + "_d"), fr=sem(name + "_fr"))

        def sums_sp(sp, i, u, q, w=W1, carry=True):
            c = i * 2 + u
            sp.wait_ge(q["fr"], c + 1)
            sp.dma_start(q["S"][:, u].rearrange("p g j -> p (g j)"),
                         dstP[bass.ds(c * G * P, G * P)].rearrange("(a n) -> a n", a=1).broadcast_to([P, G * P]))\
                .then_inc(q["ld"][u], 16)
            if carry:
                for k, row in enumerate((0, P - 1)):
                    sp.dma_start(q["C"][row:row + 1, u, :, 0:w],
                                 CAd[k:k + 1, bass.ds(c * G, G), 0:w]).then_inc(q["ld"][u], 16)

        def sums_start(dve, step, q):
            step(dve.memset(q["C"][:, :, :, :], 0.0))
            dve.sem_inc(q["z"], 1)

        def sums_dve(dve, i, u, q, carry=True):
            c = i * 2 + u
            dve.wait_ge(q["ld"][u], (i + 1) * (48 if carry else 16))
            dve.tensor_tensor(q["S"][:, u], q["S"][:, u], bc(dstF[:, bass.ds(c * G, G)], 2, [P, G, P]),
                              ALU.is_equal).then_inc(q["s"], 1)

        def sums_pe(pe, i, u, q, w=W1):
            c = i * 2 + u
            pe.wait_ge(q["s"], c + 1)
            for j in range(G):
                to = q["ps"][:, u, j // 4, (j % 4) * w:(j % 4 + 1) * w]
                pe.matmul(to, q["S"][:, u, j, :], M[:, bass.ds(c * G + j, 1), 0:w].rearrange("p a d -> p (a d)"),
                          start=True, stop=False)
                last = pe.matmul(to, q["S"][:, u, j, :], q["C"][:, u, j, 0:w], start=False, stop=True)
            last.then_inc(q["d"], 1)

        def sums_view(q, u, w=W1, a=0, b=D):
            return q["ps"][:, u, :, 0:4 * w].rearrange("p k (g d) -> p k g d", d=w)[:, :, :, a:b]

        def v4(ap):
            return ap.rearrange("p (k g) d -> p k g d", k=2)

        def norms_and_ends(name, emit_for, per, before=None, w=W1):
            st = phase()
            with st:
                nm = norm_setup(st, name + "_nm", G)
                q = ends_setup(st, name + "_en")
                with nc.Block() as block:
                    @block.vector
                    def _(dve):
                        step = Steps(dve, name + "_dve")
                        if before is not None:
                            before(dve, step)
                        base = step.k
                        def body(eng, i, u):
                            c = i * 2 + u
                            step.chunk(c, NORM_STEPS + per + 1, base)
                            to = M[:, bass.ds(c * G, G), 0:D]
                            norm_dve(eng, step, nm, c, XS[:, bass.ds(c * G, G), :],
                                     lambda xc, r: emit_for(eng, step, c, to, xc, r), w=c)
                            eng.sem_inc(q["m"], 1)
                            step.end()
                        chunks(body)(dve)

                    @block.scalar
                    def _(act):
                        def body(eng, i, u):
                            c = i * 2 + u
                            ends_act_before(eng, i, u, q)
                            norm_act(eng, nm, w=c)
                            ends_act(eng, i, u, q, w)
                        chunks(body)(act)

                    @block.tensor
                    def _(pe):
                        chunks(lambda eng, i, u: ends_pe(eng, i, u, q, w))(pe)

                    @block.sync
                    def _(sp):
                        chunks(lambda eng, i, u: ends_sp(eng, i, u, q, w))(sp)
                        ends_sp_done(sp, q)

        def after_gather(dve, step):
            step(dve.tensor_scalar(RC[:, :], RI[:, :], 0.0, None, ALU.is_equal))
            step(dve.tensor_scalar(RC[:, :], RC[:, :], float(FAR), -1.0, ALU.mult, ALU.add))
            step(dve.tensor_tensor(RI[:, :], RI[:, :], RC[:, :], ALU.add))
            step(dve.tensor_copy(riI[:, :], RI[:, :]))
            step(dve.tensor_copy(csI[:, :], CS[:, :]))
            step(dve.tensor_copy(cdI[:, :], CD[:, :]))
            step(dve.tensor_scalar(RC[:, :], RI[:, :], float(NT * P), float(FAR), ALU.is_lt, ALU.mult))
            step(dve.tensor_tensor(RC[:, :], RC[:, :], srcF[:, :], ALU.add))
            step(dve.tensor_copy(srcS[:, :], RC[:, :]))
            step(dve.tensor_scalar(OD[:, :], OD[:, :], 1.0, None, ALU.max))

        def plain(eng, step, c, to, xc, r):
            step(relu_into(eng, to)(xc, r))

        with phase(), nc.Block() as block:
            @block.vector
            def _(dve):
                step = Steps(dve, "ri_dve")
                after_gather(dve, step)
                step(dve.memset(M[:, :, D:W1], 1.0))
        early.close()
        norms_and_ends("l0a", plain, 0)
        carries("l0b")

        def means_and_squares():
            st = phase()
            with st:
                q = sums_setup(st, "l0c_s")
                e = ends_setup(st, "l0c_e")
                mean = sb_in(st, "l0c_mean", [P, G, D])
                d = sb_in(st, "l0c_d", [P, 2, G, D])
                cnt = sb_in(st, "l0c_cnt", [P, 2, G])
                s_d = sem("l0c_dev"); s_df = sem("l0c_devfree")
                PER = 7
                with nc.Block() as block:
                    @block.sync
                    def _(sp):
                        sp.wait_ge(q["z"], 1)
                        sums_sp(sp, 0, 0, q)
                        sums_sp(sp, 0, 1, q)
                        with sp.Fori(0, NCH // 2 - 1) as i:
                            for u in range(2):
                                sums_sp(sp, i + 1, u, q)
                                ends_sp(sp, i, u, e, D)
                        sums_sp(sp, NCH // 2, 0, q)
                        ends_sp(sp, NCH // 2 - 1, 0, e, D)
                        ends_sp(sp, NCH // 2 - 1, 1, e, D)
                        ends_sp(sp, NCH // 2, 0, e, D)
                        ends_sp_done(sp, e)

                    @block.vector
                    def _(dve):
                        step = Steps(dve, "l0c_dve")
                        dve.sem_inc(q["fr"], 2)
                        dve.sem_inc(s_df, 2)
                        sums_start(dve, step, q)
                        def body(eng, i, u):
                            c = i * 2 + u
                            step.chunk(c, PER, 1)
                            eng.wait_ge(q["d"], c + 1)
                            cc = sums_view(q, u, W1, D, W1)
                            t2 = lambda a: a[:, bass.ds(c * G, G)]
                            step(eng.tensor_copy(v4(cnt[:, u, :].unsqueeze(2)), cc))
                            step(eng.reciprocal(t2(RC), cnt[:, u, :]))
                            step(eng.tensor_scalar(cnt[:, u, :], cnt[:, u, :], 1.0, None, ALU.is_gt))
                            step(eng.tensor_tensor(t2(RCM), t2(RC), cnt[:, u, :], ALU.mult))
                            step(eng.tensor_tensor(v4(mean[:, :, :]), sums_view(q, u),
                                                   v4(bc(t2(RC), 2, [P, G, D])), ALU.mult))
                            eng.sem_inc(q["fr"], 1)
                            eng.wait_ge(s_df, c + 1)
                            step(eng.tensor_tensor(d[:, u], M[:, bass.ds(c * G, G), 0:D], mean[:, :, :], ALU.subtract))
                            step(eng.tensor_tensor(M[:, bass.ds(c * G, G), 0:D], d[:, u], d[:, u], ALU.mult))
                            eng.sem_inc(s_df, 1)
                            eng.sem_inc(e["m"], 1)
                            step.end()
                        chunks_ahead(lambda eng, i, u: sums_dve(eng, i, u, q), body)(dve)

                    @block.scalar
                    def _(act):
                        def body(eng, i, u):
                            ends_act_before(eng, i, u, e)
                            ends_act(eng, i, u, e, D)
                        chunks(body)(act)

                    @block.tensor
                    def _(pe):
                        chunks_ahead(lambda eng, i, u: sums_pe(eng, i, u, q),
                                     lambda eng, i, u: ends_pe(eng, i, u, e, D))(pe)

        means_and_squares()
        carries("l0d", D)

        def update(name, table, emit, per, act_fn=None, w=D):
            st = phase()
            with st:
                q = sums_setup(st, name + "_s")
                t = sb_in(st, name + "_t", [P, 2, G, D])
                s_x = sem(name + "_xd"); s_a = sem(name + "_a"); s_b = sem(name + "_b")
                s_st = sem(name + "_st")
                with nc.Block() as block:
                    @block.sync
                    def _(sp):
                        sp.wait_ge(q["z"], 1)
                        chunks(lambda eng, i, u: sums_sp(eng, i, u, q, w))(sp)

                    @block.vector
                    def _(dve):
                        step = Steps(dve, name + "_dve")
                        dve.sem_inc(q["fr"], 2)
                        sums_start(dve, step, q)
                        def body(eng, i, u):
                            c = i * 2 + u
                            step.chunk(c, per, 1)
                            eng.wait_ge(q["d"], c + 1)
                            emit(eng, step, i, u, q, t, s_a, s_b)
                            step.end()
                            eng.sem_inc(s_x, 1)
                        chunks_ahead(lambda eng, i, u: sums_dve(eng, i, u, q), body)(dve)

                    @block.tensor
                    def _(pe):
                        chunks(lambda eng, i, u: sums_pe(eng, i, u, q, w))(pe)

                    @block.scalar
                    def _(act):
                        def body(eng, i, u):
                            c = i * 2 + u
                            if act_fn is not None:
                                act_fn(eng, i, u, t, s_a, s_b)
                            eng.wait_ge(s_x, c + 1)
                            eng.dma_start(table[bass.ds(c * G * P, G * P), :].rearrange("(g p) d -> p g d", p=P),
                                          XD[:, bass.ds(c * G, G), :]).then_inc(s_st, 16)
                        chunks(body)(act)
                        act.wait_ge(s_st, 16 * NCH)

        def deviation(eng, step, i, u, q, t, s_a, s_b):
            c = i * 2 + u
            xd = XD[:, bass.ds(c * G, G), :]
            eng.tensor_tensor(v4(t[:, u]), sums_view(q, u, D), v4(bc(RCM[:, bass.ds(c * G, G)], 2, [P, G, D])),
                              ALU.mult).then_inc(s_a, 1)
            eng.wait_ge(s_b, c + 1)
            eng.sem_inc(q["fr"], 1)
            step(eng.tensor_tensor(xd, xd, t[:, u], ALU.add))

        def deviation_root(act, i, u, t, s_a, s_b):
            c = i * 2 + u
            act.wait_ge(s_a, c + 1)
            act.activation(t[:, u], t[:, u], ACT.Sqrt).then_inc(s_b, 1)

        update("l0e", T1, deviation, 1, deviation_root)
        if STOP == "l0":
            return

        def attributes():
            st = phase()
            with st:
                q = ends_setup(st, "l1a_en")
                g = gather_setup(st, "l1a_g", D)
                s_e = sem("l1a_ea"); s_z = sem("l1a_z"); s_x = sem("l1a_x"); s_io = sem("l1a_iota")
                S2 = sb_in(st, "l1a_S2", [P, 2, G, P])
                jI = sb_in(st, "l1a_jI", [P, P], i32); jF = sb_in(st, "l1a_jF", [P, P])
                pI_ = sb_in(st, "l1a_pI", [P, 1], i32); pF = sb_in(st, "l1a_pF", [P, 2])
                lastR = sb_in(st, "l1a_last", [P, NT]); tmp = sb_in(st, "l1a_tmp", [P, NT])
                s_sr = [sem(f"l1a_src{u}") for u in range(2)]; s_sf = sem("l1a_srcfree")
                with nc.Block() as block:
                    @block.gpsimd
                    def _(pool):
                        pool.iota(jI[:, :], [[1, P]], channel_multiplier=0)
                        pool.iota(pI_[:, :], [[1, 1]], channel_multiplier=1).then_inc(s_io, 1)
                        last_row = pool.to_reg(NT * P - 1)
                        chunks(lambda eng, i, u: gather_chunk(eng, i, u, g, T1, riI, last_row, old=XS))(pool)

                    @block.vector
                    def _(dve):
                        dve.memset(M[:, full_rows:NT, 0:D], 0.0).then_inc(s_z, 1)
                        dve.wait_ge(s_e, 32)
                        dve.sem_inc(q["m"], NCH)
                        step = Steps(dve, "l1a_dve")
                        dve.sem_inc(s_sf, 2)
                        dve.wait_ge(s_io, 1)
                        dve.tensor_copy(jF[:, :], jI[:, :])
                        step(dve.tensor_copy(pF[:, 0:1], pI_[:, :]))
                        def body(eng, i, u):
                            c = i * 2 + u
                            step.chunk(c, 3, 1)
                            eng.wait_ge(s_sr[u], (i + 1) * 16)
                            step(eng.tensor_tensor(S2[:, u], S2[:, u], bc(srcF[:, bass.ds(c * G, G)], 2, [P, G, P]),
                                                   ALU.is_equal))
                            step(eng.tensor_tensor(S2[:, u], S2[:, u], bc(jF[:, :], 1, [P, G, P]), ALU.mult))
                            step(eng.tensor_reduce(lastR[:, bass.ds(c * G, G)], S2[:, u], AX.X, ALU.max))
                            eng.sem_inc(s_sf, 1)
                            step.end()
                        chunks(body)(dve)
                        step.base, step.k = 3 * NCH + 1, 0
                        step(dve.tensor_scalar(lastR[:, :], lastR[:, :], pF[:, 0:1], None, ALU.is_equal))
                        step(dve.tensor_scalar(tmp[:, :], srcF[:, :], float(N), None, ALU.is_lt))
                        step(dve.tensor_tensor(lastR[:, :], lastR[:, :], tmp[:, :], ALU.mult))
                        step(dve.tensor_scalar(pF[:, 1:2], pF[:, 0:1], float(NT * P), None, ALU.add))
                        step(dve.tensor_copy(tmp[:, :], csI[:, :]))
                        step(dve.tensor_scalar(tmp[:, :], tmp[:, :], pF[:, 1:2], None, ALU.subtract))
                        step(dve.tensor_tensor(tmp[:, :], tmp[:, :], lastR[:, :], ALU.mult))
                        step(dve.tensor_scalar(tmp[:, :], tmp[:, :], pF[:, 1:2], None, ALU.add))
                        step(dve.tensor_copy(idY[:, :], tmp[:, :]))
                        step(dve.tensor_scalar(lastR[:, :], lastR[:, :], -float(FAR), float(FAR), ALU.mult, ALU.add))
                        step(dve.tensor_copy(tmp[:, :], srcS[:, :]))
                        step(dve.tensor_tensor(tmp[:, :], tmp[:, :], lastR[:, :], ALU.add))
                        step(dve.tensor_copy(srcS[:, :], tmp[:, :]))

                    @block.scalar
                    def _(act):
                        act.sem_inc(g["free"], 2)
                        def body(eng, i, u):
                            c = i * 2 + u
                            ends_act_before(eng, i, u, q)
                            ends_act(eng, i, u, q, D)
                            eng.wait_ge(g["sems"][u], (i + 1) * (16 * G))
                            eng.activation(XS[:, bass.ds(c * G, G), :], g["ring"][:, u], ACT.Copy)\
                                .then_inc(g["free"], 1)
                        chunks(body)(act)

                    @block.tensor
                    def _(pe):
                        chunks(lambda eng, i, u: ends_pe(eng, i, u, q, D))(pe)

                    @block.sync
                    def _(sp):
                        sp.dma_start(M[:, 0:full_rows, 0:D],
                                     edge_attr[0:full_rows * P, :].rearrange("(t p) d -> p t d", p=P)).then_inc(s_e, 16)
                        sp.wait_ge(s_z, 1)
                        sp.dma_start(M[0:rest, full_rows, 0:D], edge_attr[full_rows * P:E, :]).then_inc(s_e, 16)
                        def body(eng, i, u):
                            c = i * 2 + u
                            eng.wait_ge(s_sf, c + 1)
                            eng.dma_start(S2[:, u].rearrange("p g j -> p (g j)"),
                                          srcP[bass.ds(c * G * P, G * P)].rearrange("(a n) -> a n", a=1)
                                          .broadcast_to([P, G * P])).then_inc(s_sr[u], 16)
                            ends_sp(eng, i, u, q, D)
                        chunks(body)(sp)
                        ends_sp_done(sp, q)

        attributes()
        move_columns(columns, True)
        columns_st.close()
        carries("l1b", D)

        alive = ExitStack()
        with alive:
            LG = sb_in(alive, "LG", [P, 2, NT, H])

            def logits():
                st = phase()
                with st:
                    B4 = G // 2
                    TN = 2 * NCH
                    S = sb_in(st, "l1c_S", [P, 2, B4, P])
                    C = sb_in(st, "l1c_C", [P, 2, B4, D])
                    AB = sb_in(st, "l1c_AB", [P, 2, 2, B4, P])
                    ABT = sb_in(st, "l1c_ABT", [P, 2, 2, B4, P])
                    LK = sb_in(st, "l1c_LK", [P, 3, B4 * P])
                    sq = sb_in(st, "l1c_sq", [P, 2 * B4, D])
                    s4 = sb_in(st, "l1c_s4", [P, 4, 2 * B4])
                    pS = ps_in(st, "l1c_pS", [P, 2, 512])
                    pX = ps_in(st, "l1c_pX", [P, 2, 512])
                    pM = ps_in(st, "l1c_pM", [P, 2, 512])
                    pL = ps_in(st, "l1c_pL", [P, 2, 512])
                    s_z = sem("l1c_zeroed"); s_fr = sem("l1c_sfree"); s_ld = [sem(f"l1c_ld{u}") for u in range(2)]
                    s_S = sem("l1c_S"); s_d = sem("l1c_sums"); s_v = sem("l1c_var"); s_sd = sem("l1c_dev")
                    s_ab = sem("l1c_ab"); s_t = sem("l1c_t"); s_tc = sem("l1c_tc")
                    s_m = sem("l1c_m"); s_sum = sem("l1c_m_biased"); s_lk = sem("l1c_lk")
                    s_l = sem("l1c_l"); s_le = sem("l1c_le")
                    PER = 11

                    def pairs(body):
                        def run(eng):
                            with eng.Fori(0, TN // 2) as i:
                                for u in range(2):
                                    body(eng, i * 2 + u, i, u)
                        return run

                    def pairs_ahead(turn):
                        def run(eng):
                            with eng.Fori(0, TN // 2 - 1) as i:
                                for u in range(2):
                                    turn(eng, i * 2 + u, u, True, True, i)
                            turn(eng, TN - 2, 0, True, False, TN // 2 - 1)
                            turn(eng, TN - 1, 1, False, False, TN // 2 - 1)
                        return run

                    with nc.Block() as block:
                        @block.sync
                        def _(sp):
                            sp.wait_ge(s_z, 1)
                            def body(eng, n, i, u):
                                eng.wait_ge(s_fr, n + 1)
                                eng.dma_start(S[:, u].rearrange("p g j -> p (g j)"),
                                              dstP[bass.ds(n * B4 * P, B4 * P)].rearrange("(a n) -> a n", a=1)
                                              .broadcast_to([P, B4 * P])).then_inc(s_ld[u], 16)
                                for k, row in enumerate((0, P - 1)):
                                    eng.dma_start(C[row:row + 1, u, :, :],
                                                  CAd[k:k + 1, bass.ds(n * B4, B4), 0:D]).then_inc(s_ld[u], 16)
                            pairs(body)(sp)

                        @block.vector
                        def _(dve):
                            step = Steps(dve, "l1c_dve")
                            dve.sem_inc(s_fr, 2)
                            step(dve.memset(C[:, :, :, :], 0.0))
                            dve.sem_inc(s_z, 1)
                            def operands(eng, part, n, i, u):
                                t_ = bass.ds(n * B4, B4)
                                ab = AB[:, u].rearrange("p k j e -> p (k j) e")[:, :, 0:D]
                                if part == 0:
                                    eng.wait_ge(s_ld[u], i * 48 + 48)
                                    eng.tensor_tensor(S[:, u], S[:, u], bc(dstF[:, t_], 2, [P, B4, P]),
                                                      ALU.is_equal).then_inc(s_S, 1)
                                    for k, X in enumerate((XS, XD)):
                                        step(eng.tensor_reduce(s4[:, 0, k * B4:(k + 1) * B4], X[:, t_, :], AX.X, ALU.add))
                                if part == 1:
                                    eng.wait_ge(s_tc, n * 2 + 2)
                                    step(eng.tensor_scalar(s4[:, 1, :], s4[:, 0, :], -1.0 / D, None, ALU.mult))
                                    for k, X in enumerate((XS, XD)):
                                        step(eng.tensor_tensor(AB[:, u, k, :, 0:D], X[:, t_, :],
                                                               bc(s4[:, 1, k * B4:(k + 1) * B4], 2, [P, B4, D]), ALU.add))
                                if part == 2:
                                    step(eng.tensor_tensor(sq[:, :, :], ab, ab, ALU.mult))
                                    eng.tensor_reduce(s4[:, 2, :], sq[:, :, :], AX.X, ALU.add).then_inc(s_v, 1)
                                if part == 3:
                                    step(eng.tensor_scalar(AB[:, u, 0, :, D:P], M[:, t_, 0:D], 1.0, None, ALU.mult))
                                if part == 4:
                                    eng.wait_ge(s_d, n + 1)
                                    eng.sem_inc(s_fr, 1)
                                    step(eng.tensor_tensor(AB[:, u, 1, :, D:P],
                                                           pS[:, u, 0:B4 * D].rearrange("p (g d) -> p g d", d=D),
                                                           bc(RC[:, t_], 2, [P, B4, D]), ALU.mult))
                                    eng.wait_ge(s_sd, n + 1)
                                    step(eng.reciprocal(s4[:, 0, :], s4[:, 3, :]))
                                if part == 5:
                                    step(eng.scalar_tensor_tensor(ab, ab, 0.0, bc(s4[:, 0, :], 2, [P, 2 * B4, D]),
                                                                  ALU.max, ALU.mult))
                                    eng.sem_inc(s_ab, 1)
                                    step(eng.tensor_scalar(M[:, t_, 0:D], AB[:, u, 0, :, 0:D], 1.0, None, ALU.mult))

                            def turn(eng, n, u, next_, second, i):
                                if second:
                                    step.chunk(n + 2, PER, 1)
                                for kf in range(6):
                                    z = min(P, HC - kf % 3 * P)
                                    m = LK[0:z, kf % 3, :]
                                    eng.wait_ge(s_sum, n * 6 + kf + 1)
                                    eng.scalar_tensor_tensor(m, m, 0.2, m, ALU.mult, ALU.max).then_inc(s_lk, 1)
                                    if second:
                                        operands(eng, kf, n + 2, i + 1, u)
                                if second:
                                    step.end()
                            for n in range(2):
                                for part in range(6):
                                    operands(dve, part, n, 0, n)
                            pairs_ahead(turn)(dve)

                        @block.tensor
                        def _(pe):
                            def sums(eng, n, u):
                                eng.wait_ge(s_S, n + 1)
                                for j in range(B4):
                                    to = pS[:, u, j * D:(j + 1) * D]
                                    eng.matmul(to, S[:, u, j, :],
                                               M[:, bass.ds(n * B4 + j, 1), 0:D].rearrange("p a d -> p (a d)"),
                                               start=True, stop=False)
                                    last = eng.matmul(to, S[:, u, j, :], C[:, u, j, :], start=False, stop=True)
                                last.then_inc(s_d, 1)

                            def transposes(eng, n, u):
                                eng.wait_ge(s_ab, n + 1)
                                for k in range(2):
                                    eng.wait_ge(s_tc, n * 2 + 3 + k)
                                    for j in range(B4):
                                        last = eng.transpose(pX[:, k, j * P:(j + 1) * P], AB[:, u, k, j, :],
                                                             ident[:, :])
                                    last.then_inc(s_t, 1)

                            def product(eng, n, u, kf):
                                k, f = kf // 3, kf % 3
                                lo, hi = f * P, min(HC, (f + 1) * P)
                                if kf == 0:
                                    eng.wait_ge(s_tc, n * 2 + 6)
                                if kf >= 2:
                                    eng.wait_ge(s_sum, n * 6 + kf - 1)
                                to = pM[0:hi - lo, kf % 2, :]
                                rA = ABT[:, u, 0].rearrange("p j e -> p (j e)")
                                rB = ABT[:, u, 1].rearrange("p j e -> p (j e)")
                                if k == 0:
                                    eng.matmul(to, WA[:, lo:hi], rA, start=True, stop=False)
                                    last = eng.matmul(to, WBr[:, lo:hi], rB[0:D, :], start=False, stop=True)
                                else:
                                    last = eng.matmul(to, WS[:, lo:hi], rB, start=True, stop=True)
                                last.then_inc(s_m, 1)

                            def dots(eng, n, u, kf):
                                k, f = kf // 3, kf % 3
                                z = min(P, HC - f * P)
                                eng.wait_ge(s_lk, n * 6 + kf + 1)
                                if kf == 0:
                                    eng.wait_ge(s_le, n + 1)
                                for j in range(B4):
                                    to = pL[:, u, (k * B4 + j) * H:(k * B4 + j + 1) * H]
                                    last = eng.matmul(to, LK[0:z, f, j * P:(j + 1) * P], attC[0:z, f, :],
                                                      start=kf + j == 0, stop=kf == 5 and j == B4 - 1,
                                                      skip_group_check=True)
                                last.then_inc(s_l, 1)

                            def turn(eng, n, u, next_, second, i):
                                for kf in range(6):
                                    if kf == 3:
                                        if next_:
                                            transposes(eng, n + 1, 1 - u)
                                        if second:
                                            sums(eng, n + 2, u)
                                    product(eng, n, u, kf)
                                    if kf >= 2:
                                        dots(eng, n, u, kf - 2)
                                dots(eng, n, u, 4)
                                dots(eng, n, u, 5)
                            sums(pe, 0, 0)
                            sums(pe, 1, 1)
                            transposes(pe, 0, 0)
                            pairs_ahead(turn)(pe)

                        @block.scalar
                        def _(act):
                            act.sem_inc(s_tc, 4)
                            act.sem_inc(s_le, 2)

                            def root(eng, n):
                                eng.wait_ge(s_v, n + 1)
                                eng.activation(s4[:, 3, :], s4[:, 2, :], ACT.Sqrt, bias=eps[:, 0:1],
                                               scale=1.0 / D).then_inc(s_sd, 1)

                            def copies(eng, n, u):
                                for k in range(2):
                                    eng.wait_ge(s_t, n * 2 + k + 1)
                                    eng.activation(ABT[:, u, k].rearrange("p j e -> p (j e)"), pX[:, k, :],
                                                   ACT.Copy).then_inc(s_tc, 1)

                            def turn(eng, n, u, next_, second, i):
                                for kf in range(6):
                                    if kf == 3 and next_:
                                        copies(eng, n + 1, 1 - u)
                                    f = kf % 3
                                    z = min(P, HC - f * P)
                                    eng.wait_ge(s_m, n * 6 + kf + 1)
                                    if kf >= 3:
                                        eng.wait_ge(s_l, n * 6 + kf - 2)
                                    eng.activation(LK[0:z, f, :], pM[0:z, kf % 2, :], ACT.Identity,
                                                   bias=mb[0:z, f:f + 1]).then_inc(s_sum, 1)
                                    if kf == 3 and second:
                                        root(eng, n + 2)
                                eng.wait_ge(s_l, n * 6 + 6)
                                eng.activation(LG[:, :, bass.ds(n * B4, B4), :],
                                               pL[:, u, 0:2 * B4 * H].rearrange("p (k g h) -> p k g h", k=2, h=H),
                                               ACT.Copy).then_inc(s_le, 1)

                            root(act, 0)
                            root(act, 1)
                            copies(act, 0, 0)
                            pairs_ahead(turn)(act)

            logits()
            if STOP == "logits":
                return

            NR = 25 * H
            NA = NT // 25

            def softmax():
                st = phase()
                with st:
                    t = lambda name, shape, dt=f32: sb_in(st, name, shape, dt)
                    room = M[0:NR, :, :].rearrange("p t d -> p (t d)")
                    part = lambda a, n: room[:, a * NA * P:(a + n) * NA * P].rearrange(
                        "p (n a j) -> p n a j", n=n, j=P)
                    L = part(0, 3)
                    same = part(3, 2)
                    isF0 = part(5, 1)[:, 0]
                    Aall = t("sm_A", [P, 3, NA, P])
                    A = Aall[0:NR]
                    d5 = Aall[:, 2].rearrange("p a j -> p (a j)")[:, 0:NT * H].rearrange("p (t h) -> p t h", h=H)
                    ends = t("sm_ends", [NR, 2, NA])
                    car = t("sm_car", [NR, 2, NA])
                    e5 = t("sm_e5", [H, 2, NT]); c5 = t("sm_c5", [H, 2, NT])
                    m0 = t("sm_m0", [H, NT]); one = t("sm_one", [H, NT]); m1 = t("sm_m1", [H, NT])
                    m1b = t("sm_m1b", [H, NT])
                    u5 = t("sm_u5", [H, NT]); b5 = t("sm_b5", [H, NT])
                    pL = ps_in(st, "sm_pL", [P, 6, 512])
                    kFr = t("sm_kF", [H, NT]); kLr = t("sm_kL", [H, NT])
                    s_k = sem("sm_keys"); s_sp = sem("sm_spill"); s_d = sem("sm_d5"); s_t = sem("sm_t"); s_en = sem("sm_ends"); s_e5 = sem("sm_e5")
                    s_c5 = sem("sm_c5"); s_car = sem("sm_car"); s_o = sem("sm_o"); s_o2 = sem("sm_o2")
                    s_x = sem("sm_x"); s_z = sem("sm_z"); s_al = sem("sm_al"); s_alT = sem("sm_alT")
                    flat = lambda a: a.rearrange("p a j -> p (a j)")
                    with nc.Block() as block:
                        @block.tensor
                        def _(pe):
                            pe.wait_ge(s_d, 1)
                            for n in range(3):
                                of = d5 if n == 2 else LG[:, n]
                                for a in range(NA):
                                    last = pe.transpose(pL[0:NR, 2 * n + a // 4, (a % 4) * P:(a % 4 + 1) * P],
                                                        of[:, 25 * a:25 * (a + 1), :].rearrange("p t h -> p (t h)"),
                                                        ident[:, :])
                            last.then_inc(s_t, 1)
                            pe.wait_ge(s_al, 1)
                            for n in range(2):
                                for a in range(NA):
                                    last = pe.transpose(pL[:, 2 * n + a // 4, (a % 4) * P:(a % 4) * P + NR],
                                                        A[:, n, a, :], ident[0:NR, 0:NR])
                            last.then_inc(s_alT, 1)

                        @block.sync
                        def _(sp):
                            sp.dma_start(Msp, M[:, 0:SPT, :]).then_inc(s_sp, 16)
                            keys = dstP.rearrange("(a t j) -> a t j", a=1, j=P)
                            rows_of = lambda v: v.rearrange("(a p) -> p a", a=NA)
                            heads_of = lambda v: v.rearrange("(t h) -> h t", h=H)
                            with nc.allow_non_contiguous_dma(reason="a few values of each tile"):
                                for to, end in ((kFr, 0), (kLr, P - 1)):
                                    sp.dma_start(to[:, :], keys[:, :, end].broadcast_to([H, NT])).then_inc(s_k, 16)
                                for k in range(2):
                                    sp.wait_ge(s_en, k + 1)
                                    for e_ in range(2):
                                        sp.dma_start(rows_of(SMd[e_]), ends[:, e_, :]).then_inc(s_o, 16)
                                    sp.wait_ge(s_o, 32 * (k + 1))
                                    for e_ in range(2):
                                        sp.dma_start(e5[:, e_, :], heads_of(SMd[e_])).then_inc(s_e5, 16)
                                    sp.wait_ge(s_c5, k + 1)
                                    for e_ in range(2):
                                        sp.dma_start(heads_of(SCd[e_]), c5[:, e_, :]).then_inc(s_o2, 16)
                                    sp.wait_ge(s_o2, 32 * (k + 1))
                                    for e_ in range(2):
                                        sp.dma_start(car[:, e_, :], rows_of(SCd[e_])).then_inc(s_car, 16)
                            sp.wait_ge(s_al, 1)
                            sp.dma_start(M[:, 0:SPT, :], Msp).then_inc(s_sp, 16)
                            sp.wait_ge(s_sp, 32)

                        @block.scalar
                        def _(act):
                            act.wait_ge(s_x, 1)
                            act.activation(A[:, 0:2].rearrange("p n a j -> p (n a j)"),
                                           L[:, 0:2].rearrange("p n a j -> p (n a j)"), ACT.Exp).then_inc(s_z, 1)

                        @block.vector
                        def _(dve):
                            step = Steps(dve, "sm_dve")
                            tt = lambda o, a, b, op: step(dve.tensor_tensor(o, a, b, op))
                            ts = lambda o, a, s1, s2, o1, o2=None: step(
                                dve.tensor_scalar(o, a, s1, s2, o1, o2) if o2 is not None else
                                dve.tensor_scalar(o, a, s1, s2, o1))
                            scan = lambda o, a, b, i0, o1, o2: step(dve.tensor_tensor_scan(o, a, b, i0, o1, o2))
                            dve.wait_ge(s_sp, 16)
                            step(dve.tensor_copy(d5[:, :, :], bc(dstF[:, :], 2, [P, NT, H])))
                            dve.sem_inc(s_d, 1)
                            dve.wait_ge(s_t, 1)
                            for n in range(3):
                                step(dve.tensor_copy(flat(L[:, n]), pL[0:NR, 2 * n:2 * n + 2, :].rearrange("p b j -> p (b j)")))
                            DR = L[:, 2]
                            dve.memset(same[:, 0, :, 0:1], 0.0)
                            dve.memset(same[:, 1, :, P - 1:P], 0.0)
                            tt(same[:, 0, :, 1:P], DR[:, :, 1:P], DR[:, :, 0:P - 1], ALU.is_equal)
                            tt(same[:, 1, :, 0:P - 1], DR[:, :, 1:P], DR[:, :, 0:P - 1], ALU.is_equal)
                            tt(isF0, DR, DR[:, :, 0:1].broadcast_to([NR, NA, P]), ALU.is_equal)
                            step(dve.tensor_copy(ends[:, 0, :], DR[:, :, P - 1]))
                            tt(DR, DR, bc(ends[:, 0, :], 2, [NR, NA, P]), ALU.is_equal)
                            isF = (isF0, DR)
                            dve.wait_ge(s_k, 32)
                            dve.memset(m0[:, 0:1], 0.0)
                            dve.memset(m1[:, 0:1], 0.0)
                            dve.memset(m1b[:, NT - 1:NT], 0.0)
                            tt(m0[:, 1:NT], kFr[0:H, 1:NT], kLr[0:H, 0:NT - 1], ALU.is_equal)
                            tt(one[:, :], kFr[0:H, :], kLr[0:H, :], ALU.is_equal)
                            tt(m1[:, 1:NT], m0[:, 1:NT], one[:, 0:NT - 1], ALU.mult)
                            tt(m1b[:, 0:NT - 1], m0[:, 1:NT], one[:, 1:NT], ALU.mult)

                            def backwards(o, f, mask):
                                ts(o, mask, -1.0, 1.0, ALU.mult, ALU.add)
                                tt(f, o, f, ALU.mult)
                                scan(flat(o)[:, ::-1], flat(mask)[:, ::-1], flat(f)[:, ::-1], 0.0,
                                     ALU.mult, ALU.add)

                            def across(k, op, off):
                                dve.sem_inc(s_en, 1)
                                dve.wait_ge(s_e5, 32 * (k + 1))
                                if k == 1:
                                    dve.wait_ge(s_o2, 32)
                                for e_ in range(2):
                                    step(dve.memset(u5[:, :], off))
                                    a, b = (slice(1, NT), slice(0, NT - 1)) if e_ == 0 else (slice(0, NT - 1), slice(1, NT))
                                    keep = (m1 if e_ == 0 else m1b)
                                    val = e5[:, 1 - e_, b]
                                    if off:
                                        ts(b5[:, a], m0[:, 1:NT], BIG, -BIG, ALU.mult, ALU.add)
                                        tt(u5[:, a], b5[:, a], val, ALU.add)
                                        ts(b5[:, :], keep[:, :], BIG, -BIG, ALU.mult, ALU.add)
                                    else:
                                        tt(u5[:, a], m0[:, 1:NT], val, ALU.mult)
                                        step(dve.tensor_copy(b5[:, :], keep[:, :]))
                                    r = slice(None, None, 1 if e_ == 0 else -1)
                                    scan(c5[:, e_, r], b5[:, r], u5[:, r], off, ALU.add if off else ALU.mult, op)
                                dve.sem_inc(s_c5, 1)
                                dve.wait_ge(s_car, 32 * (k + 1))

                            ts(A[:, 0], same[:, 0], BIG, -BIG, ALU.mult, ALU.add)
                            scan(flat(A[:, 1]), flat(A[:, 0]), flat(L[:, 0]), -BIG, ALU.add, ALU.max)
                            backwards(A[:, 2], A[:, 1], same[:, 1])
                            step(dve.tensor_copy(ends[:, 0, :], A[:, 2, :, 0]))
                            step(dve.tensor_copy(ends[:, 1, :], A[:, 2, :, P - 1]))
                            across(0, ALU.max, -BIG)
                            for e_ in range(2):
                                ts(A[:, 0], isF[e_], BIG, -BIG, ALU.mult, ALU.add)
                                tt(A[:, 0], A[:, 0], bc(car[:, e_, :], 2, [NR, NA, P]), ALU.add)
                                tt(A[:, 2], A[:, 2], A[:, 0], ALU.max)
                            tt(A[:, 2], A[:, 2], L[:, 1], ALU.max)
                            tt(L[:, 0], L[:, 0], A[:, 2], ALU.subtract)
                            tt(L[:, 1], L[:, 1], A[:, 2], ALU.subtract)
                            dve.sem_inc(s_x, 1)
                            dve.wait_ge(s_z, 1)
                            scan(flat(A[:, 2]), flat(same[:, 0]), flat(A[:, 0]), 0.0, ALU.mult, ALU.add)
                            backwards(L[:, 0], A[:, 2], same[:, 1])
                            step(dve.tensor_copy(ends[:, 0, :], L[:, 0, :, 0]))
                            step(dve.tensor_copy(ends[:, 1, :], L[:, 0, :, P - 1]))
                            across(1, ALU.add, 0.0)
                            for e_ in range(2):
                                tt(A[:, 2], isF[e_], bc(car[:, e_, :], 2, [NR, NA, P]), ALU.mult)
                                tt(L[:, 0], L[:, 0], A[:, 2], ALU.add)
                            tt(L[:, 0], L[:, 0], A[:, 1], ALU.add)
                            step(dve.reciprocal(L[:, 1], L[:, 0]))
                            ts(L[:, 1], L[:, 1], 1.0 / H, None, ALU.mult)
                            tt(A[:, 0], A[:, 0], L[:, 1], ALU.mult)
                            tt(A[:, 1], A[:, 1], L[:, 1], ALU.mult)
                            dve.sem_inc(s_al, 1)
                            dve.wait_ge(s_alT, 1)
                            for n in range(2):
                                for b in range(2):
                                    to = LG[:, n, 100 * b:100 * (b + 1), :].rearrange("p (a t) h -> p a (t h)", a=4)
                                    of = pL[:, 2 * n + b, :].rearrange("p (a r) -> p a r", a=4)[:, :, 0:NR]
                                    step(dve.tensor_copy(to, of))
                            tt(LG[:, 1], LG[:, 1], bc(repF[:, :], 2, [P, NT, H]), ALU.mult)

            softmax()
            if STOP == "softmax":
                return

            def weighted():
                st = phase()
                with st:
                    nm = norm_setup(st, "l1e_nm", G)
                    e = ends_setup(st, "l1e_en")
                    hd = sb_in(st, "l1e_hd", [P, G, D])
                    Gs = sb_in(st, "l1e_G", [P, 2, 2, H, D])
                    Gd = sb_in(st, "l1e_Gd", [P, 2, 2, H, D])
                    GT = sb_in(st, "l1e_GT", [P, 2, 3, P])
                    pG = ps_in(st, "l1e_pG", [P, 2, 512])
                    pC = ps_in(st, "l1e_pC", [P, 512])
                    s_hd = sem("l1e_hd"); s_g = sem("l1e_g"); s_gd = sem("l1e_gd")
                    s_gf = sem("l1e_gf"); s_t = sem("l1e_t"); s_te = sem("l1e_te"); s_c = sem("l1e_c")
                    s_ce = sem("l1e_ce")
                    PER = NORM_STEPS + 1
                    with nc.Block() as block:
                        @block.vector
                        def _(dve):
                            step = Steps(dve, "l1e_dve")
                            def body(eng, i, u):
                                c = i * 2 + u
                                step.chunk(c, PER)
                                eng.wait_ge(s_gd, 4 * c)
                                norm_dve(eng, step, nm, c, XD[:, bass.ds(c * G, G), :],
                                         lambda xc, r: step(relu_into(eng, hd[:, :, :])(xc, r)), w=c)
                                eng.sem_inc(s_hd, 1)
                                step.end()
                                for hf in range(4):
                                    n = c * 4 + hf
                                    eng.wait_ge(s_gf, n + 1)
                                    for j in range(2):
                                        t_ = c * G + hf * 2 + j
                                        last = eng.tensor_tensor(
                                            Gs[:, hf % 2, j, :, :], M[:, bass.ds(t_, 1), 0:D].broadcast_to([P, H, D]),
                                            LG[:, 0, bass.ds(t_, 1), :].rearrange("p a h -> p h a").broadcast_to([P, H, D]),
                                            ALU.mult)
                                    last.then_inc(s_g, 1)
                            chunks(body)(dve)

                        @block.gpsimd
                        def _(pool):
                            def body(eng, i, u):
                                c = i * 2 + u
                                eng.wait_ge(s_hd, c + 1)
                                for hf in range(4):
                                    n = c * 4 + hf
                                    eng.wait_ge(s_gf, n + 1)
                                    for j in range(2):
                                        t_ = c * G + hf * 2 + j
                                        last = eng.tensor_tensor(
                                            Gd[:, hf % 2, j, :, :], hd[:, hf * 2 + j:hf * 2 + j + 1, :].broadcast_to([P, H, D]),
                                            LG[:, 1, bass.ds(t_, 1), :].rearrange("p a h -> p h a").broadcast_to([P, H, D]),
                                            ALU.mult)
                                    last.then_inc(s_gd, 1)
                            chunks(body)(pool)

                        @block.tensor
                        def _(pe):
                            pe.sem_inc(s_gf, 2)
                            def body(eng, i, u):
                                c = i * 2 + u
                                for j in range(G):
                                    hf, k = j // 2, c * G + j
                                    if j % 2 == 0:
                                        eng.wait_ge(s_g, c * 4 + hf + 1)
                                        eng.wait_ge(s_gd, c * 4 + hf + 1)
                                    if j >= 2:
                                        eng.wait_ge(s_te, k - 1)
                                    for f in range(3):
                                        z = min(2, H - 2 * f)
                                        to = pG[0:z * D, j % 2, f * P:(f + 1) * P]
                                        for k_, of in enumerate((Gs, Gd)):
                                            last = eng.matmul(
                                                to, of[:, hf % 2, j % 2, 2 * f:2 * f + z, :].rearrange("p h d -> p (h d)"),
                                                ident[:, :], start=k_ == 0, stop=k_ == 1)
                                    last.then_inc(s_t, 1)
                                    if j >= 1:
                                        product(eng, c, j - 1)
                                product(eng, c, G - 1)
                                ends_pe(eng, i, u, e, D)

                            def product(eng, c, j):
                                eng.wait_ge(s_te, c * G + j + 1)
                                if j == 0:
                                    eng.wait_ge(s_ce, c)
                                for f in range(3):
                                    z = min(P, HC - f * P)
                                    last = eng.matmul(pC[:, j * D:(j + 1) * D], GT[0:z, j % 2, f, :], WlS[0:z, f, :],
                                                      start=f == 0, stop=f == 2)
                                    if f == 0 and j % 2 == 0:
                                        last.then_inc(s_gf, 1)
                                if j == G - 1:
                                    last.then_inc(s_c, 1)
                            chunks(body)(pe)

                        @block.scalar
                        def _(act):
                            def body(eng, i, u):
                                c = i * 2 + u
                                ends_act_before(eng, i, u, e)
                                norm_act(eng, nm, w=c)
                                for j in range(G):
                                    k = c * G + j
                                    eng.wait_ge(s_t, k + 1)
                                    eng.activation(GT[:, j % 2, 0:2].rearrange("p f e -> p (f e)"),
                                                   pG[:, j % 2, 0:2 * P], ACT.Copy)
                                    eng.activation(GT[0:D, j % 2, 2, :], pG[0:D, j % 2, 2 * P:3 * P],
                                                   ACT.Copy).then_inc(s_te, 1)
                                eng.wait_ge(s_c, c + 1)
                                eng.activation(M[:, bass.ds(c * G, G), 0:D],
                                               pC[:, :].rearrange("p (g d) -> p g d", d=D), ACT.Copy).then_inc(s_ce, 1)
                                eng.wait_ge(s_ce, c + 1)
                                eng.sem_inc(e["m"], 1)
                                ends_act(eng, i, u, e, D)
                            chunks(body)(act)

                        @block.sync
                        def _(sp):
                            chunks(lambda eng, i, u: ends_sp(eng, i, u, e, D))(sp)
                            ends_sp_done(sp, e)

            weighted()
        carries("l1f", D)

        def tails():
            st = phase()
            with st:
                q = tail_setup(st, "l1g_t")
                s = dict(S=sb_in(st, "l1g_S", [P, 2, G, P]),
                         C=sb_in(st, "l1g_C", [P, 2, G, W1]),
                         z=sem("l1g_z"), ld=[sem(f"l1g_ld{u}") for u in range(2)], s=sem("l1g_S"),
                         fr=sem("l1g_fr"))
                s_x = sem("l1g_x"); s_st = sem("l1g_st")
                with nc.Block() as block:
                    @block.sync
                    def _(sp):
                        sp.wait_ge(s["z"], 1)
                        chunks(lambda eng, i, u: sums_sp(eng, i, u, s, D))(sp)

                    @block.vector
                    def _(dve):
                        step = Steps(dve, "l1g_dve")
                        dve.sem_inc(s["fr"], 2)
                        dve.sem_inc(q["z_read"], 2)
                        sums_start(dve, step, s)
                        def turn(eng, i, u, k, *flags):
                            w = (i * 2 + u) * 2 + k
                            step.turn(w, TAIL_STEPS, flags[2] and (flags[0] or k == 0))
                            if flags[0] and k == 0:
                                sums_dve(eng, i, u, s)
                            X = (XD, XS)[k]
                            tail_dve(eng, step, q, w, k, flags,
                                     X[:, bass.ds((i * 2 + u) * G, G), :] if flags[0] else None,
                                     X[:, bass.ds((i * 2 + u) * G - G, G), :] if flags[2] else None, 0)
                            if k == 1 and flags[1] and flags[0]:
                                eng.sem_inc(s["fr"], 1)
                            if k == 0 and flags[2]:
                                eng.sem_inc(s_x, 1)
                        turns(turn)(dve)

                    @block.scalar
                    def _(act):
                        def turn(eng, i, u, k, *flags):
                            c = i * 2 + u
                            tail_act(eng, q, c * 2 + k, k, flags)
                            if k == 1 and flags[2]:
                                eng.wait_ge(s_x, c)
                                eng.dma_start(T2[bass.ds(c * G * P - G * P, G * P), :].rearrange("(g p) d -> p g d", p=P),
                                              XD[:, bass.ds(c * G - G, G), :]).then_inc(s_st, 16)
                        turns(turn)(act)
                        act.wait_ge(s_st, 16 * NCH)

                    @block.tensor
                    def _(pe):
                        def turn(eng, i, u, k, *flags):
                            c = i * 2 + u
                            def conv():
                                eng.wait_ge(s["s"], c + 1)
                                for j in range(G):
                                    to = q["py"][:, j * D:(j + 1) * D]
                                    eng.matmul(to, s["S"][:, u, j, :],
                                               M[:, bass.ds(c * G + j, 1), 0:D].rearrange("p a d -> p (a d)"),
                                               start=False, stop=False)
                                    last = eng.matmul(to, s["S"][:, u, j, :], s["C"][:, u, j, 0:D],
                                                      start=False, stop=j == G - 1)
                                return last
                            tail_pe(eng, q, c * 2 + k, k, flags, (BDj, BDc)[k], extra=None if k else conv)
                        turns(turn)(pe)

        tails()
        if STOP == "l1":
            return

        columns = source_columns(top, 2)
        srcF, ewF, OD, idY, csI, cdI, srcS, dstS = columns
        move_columns(columns, False)

        def scatter_sums():
            st = phase()
            with st:
                nm = norm_setup(st, "l2a_nm", G)
                S2 = sb_in(st, "l2a_S", [P, 2, G, P])
                m = sb_in(st, "l2a_m", [P, 2, G, D])
                R = sb_in(st, "l2a_R", [P, 2, G, D])
                idx = sb_in(st, "l2a_idx", [P, 2, G], i32)
                pS = ps_in(st, "l2a_pS", [P, 2, 512])
                s_sr = [sem(f"l2a_src{u}") for u in range(2)]; s_sf = sem("l2a_sfree"); s_m = sem("l2a_m")
                s_d = sem("l2a_sums"); s_r = sem("l2a_rows"); s_i = sem("l2a_idx"); s_go = sem("l2a_go")
                s_y = [sem(f"l2a_y{k}") for k in range(NY)]
                with nc.Block() as block:
                    @block.sync
                    def _(sp):
                        def body(eng, i, u):
                            c = i * 2 + u
                            eng.wait_ge(s_sf, c + 1)
                            eng.dma_start(S2[:, u].rearrange("p g j -> p (g j)"),
                                          srcP[bass.ds(c * G * P, G * P)].rearrange("(a n) -> a n", a=1)
                                          .broadcast_to([P, G * P])).then_inc(s_sr[u], 16)
                        chunks(body)(sp)

                    @block.vector
                    def _(dve):
                        step = Steps(dve, "l2a_dve")
                        def body(eng, i, u):
                            c = i * 2 + u
                            step.chunk(c, NORM_STEPS + 3)
                            norm_dve(eng, step, nm, c, XD[:, bass.ds(c * G, G), :],
                                     lambda xc, r: step(relu_into(eng, m[:, u])(xc, r)), w=c)
                            step(eng.tensor_tensor(m[:, u], m[:, u], bc(ewF[:, bass.ds(c * G, G)], 2, [P, G, D]), ALU.mult))
                            eng.wait_ge(s_sr[u], (i + 1) * 16)
                            step(eng.tensor_tensor(S2[:, u], S2[:, u], bc(srcF[:, bass.ds(c * G, G)], 2, [P, G, P]),
                                                   ALU.is_equal))
                            eng.sem_inc(s_m, 1)
                            step.end()
                        chunks(body)(dve)

                    @block.tensor
                    def _(pe):
                        pe.sem_inc(s_sf, 2)
                        def body(eng, i, u):
                            c = i * 2 + u
                            eng.wait_ge(s_m, c + 1)
                            eng.wait_ge(s_go, c)
                            for j in range(G):
                                last = eng.matmul(pS[:, u, j * D:(j + 1) * D], S2[:, u, j, :], m[:, u, j, :],
                                                  start=True, stop=True)
                            last.then_inc(s_d, 1)
                            eng.wait_ge(s_d, c + 1)
                            eng.sem_inc(s_sf, 1)
                        chunks(body)(pe)

                    @block.scalar
                    def _(act):
                        def body(eng, i, u):
                            c = i * 2 + u
                            norm_act(eng, nm, w=c)
                            eng.wait_ge(s_d, c + 1)
                            for k in range(NY):
                                eng.wait_ge(s_y[k], i * 64)
                            eng.activation(R[:, u], pS[:, u, :].rearrange("p (g d) -> p g d", d=D),
                                           ACT.Copy).then_inc(s_go, 1)
                        chunks(body)(act)

                    @block.gpsimd
                    def _(pool):
                        def body(eng, i, u):
                            c = i * 2 + u
                            for k in range(NY):
                                eng.wait_ge(s_y[k], i * 64)
                            eng.tensor_copy(idx[:, u, :], idY[:, bass.ds(c * G, G)]).then_inc(s_i, 1)
                            eng.wait_ge(s_i, c + 1)
                            eng.wait_ge(s_go, c + 1)
                            for j in range(G):
                                k = j % NY
                                eng.wait_ge(s_y[k], c * 32 + j // NY * 16)
                                eng.sem_inc(s_r, 1)
                                eng.indirect_dma_start(
                                    out=Yk[k], out_offset=bass.IndirectOffsetOnAxis(ap=idx[:, u, j:j + 1], axis=0),
                                    in_=R[:, u, j, :], in_offset=None, compute_op=ALU.add).then_inc(s_y[k], 16)
                        chunks(body)(pool)
                        for k in range(NY):
                            pool.wait_ge(s_y[k], 32 * NCH)

        scatter_sums()

        def combine():
            with phase(), nc.Block() as block:
                s_a = sem("cb_add"); s_o = sem("cb_out")
                part = M[:, :, :].rearrange("p t d -> p (t d)")[:, 0:YR // P * D]

                @block.gpsimd
                def _(pool):
                    for k in range(NY):
                        of = Yk[k].rearrange("(p r) d -> p (r d)", p=P)
                        if k == 0:
                            pool.dma_start(part, of, max_dma_last_dim=8192).then_inc(s_a, 16)
                        else:
                            pool.dma_start(part, of, accum_op=ALU.add, max_dma_last_dim=8192).then_inc(s_a, 16)
                        pool.wait_ge(s_a, 16 * (k + 1))
                    pool.dma_start(Y.rearrange("(p r) d -> p (r d)", p=P), part).then_inc(s_o, 16)
                    pool.wait_ge(s_o, 16)

        combine()

        def degrees():
            with phase(), nc.Block() as block:
                s_a, s_b = sem("dg_a"), sem("dg_b")

                @block.scalar
                def _(act):
                    act.activation(RC[:, :], RC[:, :], ACT.Sqrt).then_inc(s_a, 1)
                    act.activation(OD[:, :], OD[:, :], ACT.Sqrt).then_inc(s_a, 1)

                @block.vector
                def _(dve):
                    dve.wait_ge(s_a, 2)
                    dve.reciprocal(OD[:, :], OD[:, :]).then_inc(s_b, 1)

        degrees()

        def add_rows():
            st = phase()
            with st:
                rings = [sb_in(st, f"l3a_ring{n}", [P, 2, G, D]) for n in range(3)]
                idx = sb_in(st, "l3a_idx", [P, 2, 4, G], i32)
                R = sb_in(st, "l3a_R", [P, 2, G, D])
                nm = norm_setup(st, "l3a_nm", G)
                q = ends_setup(st, "l3a_en")
                s_rows = [sem(f"l3a_rows{u}") for u in range(2)]; s_fill = sem("l3a_filled")
                s_free = sem("l3a_free"); s_i = sem("l3a_idx"); s_go = sem("l3a_go"); s_r = sem("l3a_r")
                s_sc = sem("l3a_written"); s_x = sem("l3a_x"); s_z = sem("l3a_z")
                zero = sb_in(st, "l3a_zero", [P, D])
                s_rf = sem("l3a_rfree")
                with nc.Block() as block:
                    @block.gpsimd
                    def _(pool):
                        last_row = pool.to_reg(NT * P - 1)
                        last_node = pool.to_reg(N - 1)

                        def turn(c, u, gather=True, write=True):
                            t_, tw = bass.ds(c * G, G), bass.ds(c * G - 2 * G, G)
                            if gather:
                                pool.wait_ge(s_fill, c + 1)
                                for n, of in enumerate((riI, csI, cdI)):
                                    pool.tensor_copy(idx[:, u, n, :], of[:, t_])
                            if write:
                                pool.wait_ge(s_r, c - 1)
                                last = pool.tensor_copy(idx[:, u, 3, :], srcS[:, tw])
                            else:
                                last = pool.tensor_copy(idx[:, u, 3, :], srcS[:, t_])
                            last.then_inc(s_i, 1)
                            pool.wait_ge(s_i, c + 1)
                            for j in range(G):
                                if gather:
                                    pool.sem_inc(s_go, 1)
                                    for n, of in enumerate((T2, Y, Y)):
                                        pool.indirect_dma_start(
                                            out=rings[n][:, u, j, :], out_offset=None, in_=of,
                                            in_offset=bass.IndirectOffsetOnAxis(ap=idx[:, u, n, j:j + 1], axis=0),
                                            bounds_check=last_row, oob_is_err=False).then_inc(s_rows[u], 16)
                                if write:
                                    if j or not isinstance(c, int) or c > 2:
                                        pool.wait_ge(s_sc, c * (16 * G) + (16 * j - 32 * G))
                                        if j == 0:
                                            pool.sem_inc(s_rf, 1)
                                    pool.sem_inc(s_go, 1)
                                    pool.indirect_dma_start(
                                        out=out, out_offset=bass.IndirectOffsetOnAxis(ap=idx[:, u, 3, j:j + 1], axis=0),
                                        in_=R[:, u, j, :], in_offset=None, bounds_check=last_node,
                                        oob_is_err=False).then_inc(s_sc, 16)
                        turn(0, 0, write=False)
                        turn(1, 1, write=False)
                        turn(2, 0)
                        turn(3, 1)
                        with pool.Fori(2, NCH // 2) as i:
                            for u in range(2):
                                turn(i * 2 + u, u)
                        turn(NCH - 1, 0)
                        turn(NCH, 1, gather=False)
                        turn(NCH + 1, 0, gather=False)
                        pool.wait_ge(s_sc, 16 * G * NCH)

                    @block.vector
                    def _(dve):
                        step = Steps(dve, "l3a_dve")
                        dve.sem_inc(s_rf, 2)
                        dve.sem_inc(s_free, 2)
                        dve.memset(zero[:, :], 0.0).then_inc(s_z, 1)
                        def body(eng, i, u):
                            c = i * 2 + u
                            t_ = bass.ds(c * G, G)
                            step.chunk(c, NORM_STEPS + 4)
                            eng.wait_ge(s_rows[u], (i + 1) * (48 * G))
                            eng.tensor_tensor(XD[:, t_, :], XD[:, t_, :], rings[2][:, u], ALU.add)
                            step(eng.tensor_tensor(XS[:, t_, :], rings[0][:, u], rings[1][:, u], ALU.add))
                            eng.sem_inc(s_free, 1)
                            eng.wait_ge(s_rf, c + 1)
                            step(eng.tensor_tensor(R[:, u], XS[:, t_, :], bc(cD[:, 2, :], 1, [P, G, D]), ALU.add))
                            eng.sem_inc(s_r, 1)
                            to = M[:, t_, 0:D]
                            norm_dve(eng, step, nm, c, XS[:, t_, :],
                                     lambda xc, r: step(relu_into(eng, to)(xc, r)), w=c)
                            step(eng.tensor_tensor(to, to, bc(OD[:, t_], 2, [P, G, D]), ALU.mult))
                            eng.sem_inc(q["m"], 1)
                            step.end()
                        chunks(body)(dve)

                    @block.scalar
                    def _(act):
                        act.wait_ge(s_z, 1)
                        def fill(eng, i, u):
                            c = i * 2 + u
                            eng.wait_ge(s_free, c + 1)
                            eng.activation(rings[0][:, u], XS[:, bass.ds(c * G, G), :], ACT.Copy)
                            for n in (1, 2):
                                last = eng.activation(rings[n][:, u], bc(zero[:, :], 1, [P, G, D]), ACT.Copy)
                            last.then_inc(s_fill, 1)
                        def rest(eng, i, u):
                            ends_act_before(eng, i, u, q)
                            norm_act(eng, nm, w=i * 2 + u)
                            ends_act(eng, i, u, q, D)
                        chunks_ahead(fill, rest)(act)

                    @block.tensor
                    def _(pe):
                        chunks(lambda eng, i, u: ends_pe(eng, i, u, q, D))(pe)

                    @block.sync
                    def _(sp):
                        chunks(lambda eng, i, u: ends_sp(eng, i, u, q, D))(sp)
                        ends_sp_done(sp, q)

        add_rows()
        carries("l3b", D)

        def last_layer():
            st = phase()
            with st:
                q = sums_setup(st, "l3c_s")
                a = sb_in(st, "l3c_a", [P, G, D])
                aT = sb_in(st, "l3c_aT", [P, 4 * P])
                R = sb_in(st, "l3c_R", [P, 2, G, D])
                idx = sb_in(st, "l3c_idx", [P, 2, G], i32)
                pT = ps_in(st, "l3c_pT", [P, 512]); pY = ps_in(st, "l3c_pY", [P, 2, 512])
                s_a = sem("l3c_a"); s_t = sem("l3c_t"); s_tc = sem("l3c_tc"); s_y = sem("l3c_y"); s_re = sem("l3c_relu")
                s_r = sem("l3c_r"); s_i = sem("l3c_i"); s_go = sem("l3c_go"); s_sc = [sem(f"l3c_sc{u}") for u in range(2)]
                with nc.Block() as block:
                    @block.sync
                    def _(sp):
                        sp.wait_ge(q["z"], 1)
                        chunks(lambda eng, i, u: sums_sp(eng, i, u, q, D))(sp)

                    @block.vector
                    def _(dve):
                        step = Steps(dve, "l3c_dve")
                        dve.sem_inc(q["fr"], 2)
                        sums_start(dve, step, q)
                        def mean(eng, i, u):
                            c = i * 2 + u
                            step.chunk(c, 1, 1)
                            eng.wait_ge(q["d"], c + 1)
                            if not isinstance(c, int) or c:
                                eng.wait_ge(s_t, c)
                            step(eng.tensor_tensor(v4(a[:, :, :]), sums_view(q, u, D),
                                                   v4(bc(RC[:, bass.ds(c * G, G)], 2, [P, G, D])), ALU.mult))
                            eng.sem_inc(q["fr"], 1)
                            eng.sem_inc(s_a, 1)

                        def result(eng, i, u):
                            c = i * 2 + u
                            eng.wait_ge(s_y, c + 1)
                            if not isinstance(i, int) or i:
                                eng.wait_ge(s_sc[u], i * (16 * G))
                            eng.tensor_scalar(R[:, u], pY[:, u, :].rearrange("p (g d) -> p g d", d=D), 0.0, None,
                                              ALU.max).then_inc(s_re, 1)
                            eng.wait_ge(s_re, c + 1)
                            eng.tensor_tensor(R[:, u], R[:, u], XD[:, bass.ds(c * G, G), :], ALU.add).then_inc(s_r, 1)
                        sums_dve(dve, 0, 0, q)
                        sums_dve(dve, 0, 1, q)
                        mean(dve, 0, 0)
                        def turn(i, u):
                            sums_dve(dve, i + 1, u, q)
                            mean(dve, i + u, 1 - u)
                            result(dve, i, u)
                        turn(0, 0)
                        turn(0, 1)
                        with dve.Fori(1, NCH // 2 - 1) as i:
                            turn(i, 0)
                            turn(i, 1)
                        sums_dve(dve, NCH // 2, 0, q)
                        mean(dve, NCH // 2 - 1, 1)
                        result(dve, NCH // 2 - 1, 0)
                        mean(dve, NCH // 2, 0)
                        result(dve, NCH // 2 - 1, 1)
                        result(dve, NCH // 2, 0)

                    @block.scalar
                    def _(act):
                        def body(eng, i, u):
                            c = i * 2 + u
                            eng.wait_ge(s_t, c + 1)
                            eng.activation(aT[:, :], pT[:, :], ACT.Copy).then_inc(s_tc, 1)
                        chunks(body)(act)

                    @block.tensor
                    def _(pe):
                        def body(eng, i, u):
                            c = i * 2 + u
                            eng.wait_ge(s_a, c + 1)
                            for j in range(4):
                                last = eng.transpose(pT[:, j * P:(j + 1) * P],
                                                     a[:, 2 * j:2 * j + 2, :].rearrange("p a d -> p (a d)"), ident[:, :])
                            last.then_inc(s_t, 1)
                            eng.wait_ge(s_tc, c + 1)
                            eng.wait_ge(s_r, c + 1)
                            eng.matmul(pY[:, u, :], ones3[:, :], bias8(2),
                                       start=True, stop=False)
                            for j in range(4):
                                last = eng.matmul(pY[:, u, j * P:(j + 1) * P], aT[:, j * P:(j + 1) * P], BD3[:, :],
                                                  start=False, stop=j == 3)
                            last.then_inc(s_y, 1)
                        pe.sem_inc(s_r, 2)
                        chunks_ahead(lambda eng, i, u: sums_pe(eng, i, u, q, D), body)(pe)

                    @block.gpsimd
                    def _(pool):
                        last_row = pool.to_reg(N - 1)
                        def body(eng, i, u):
                            c = i * 2 + u
                            if not isinstance(i, int) or i:
                                eng.wait_ge(s_sc[u], i * (16 * G))
                            eng.tensor_copy(idx[:, u, :], dstS[:, bass.ds(c * G, G)]).then_inc(s_i, 1)
                            eng.wait_ge(s_i, c + 1)
                            eng.wait_ge(s_r, c + 3)
                            eng.sem_inc(s_go, 1)
                            for j in range(G):
                                eng.indirect_dma_start(
                                    out=out, out_offset=bass.IndirectOffsetOnAxis(ap=idx[:, u, j:j + 1], axis=0),
                                    in_=R[:, u, j, :], in_offset=None, bounds_check=last_row,
                                    oob_is_err=False).then_inc(s_sc[u], 16)
                        body(pool, 0, 0)
                        body(pool, 0, 1)
                        with pool.Fori(1, NCH // 2) as i:
                            body(pool, i, 0)
                            body(pool, i, 1)
                        body(pool, NCH // 2, 0)
                        pool.wait_ge(s_sc[0], 16 * G * (NCH // 2 + 1))
                        pool.wait_ge(s_sc[1], 16 * G * (NCH // 2))

        last_layer()


def kernel(**inputs):
    import numpy as _np
    import concourse.bacc as _bacc
    from concourse import mybir as _mybir
    from concourse.bass_utils import run_bass_kernel_spmd as _run

    nc = _bacc.Bacc("TRN2", target_bir_lowering=False, num_devices=1)
    arrays, args = {}, []
    for name in _INS:
        a = _np.ascontiguousarray(inputs[name])
        arrays[f"in_{name}_dram"] = a
        args.append(nc.dram_tensor(f"in_{name}_dram", a.shape, _mybir.dt.from_np(a.dtype), kind="ExternalInput").ap())
    shape = inputs["x"].shape
    args.append(nc.dram_tensor("out_0_dram", shape, _mybir.dt.float32, kind="ExternalOutput").ap())
    gnn_program(nc, *args)
    r = _run(nc, [arrays], core_ids=[0])
    return r.results[0]["out_0_dram"]
```

```python
import concourse.bass as bass
from concourse import mybir
from contextlib import ExitStack

_INS = ["x", "src", "dst", "edge_attr_64", "edge_weight", "L1_gnn_Wl", "L1_gnn_bl", "L1_gnn_Wr", "L1_gnn_br",
        "L1_gnn_We", "L1_gnn_att", "L1_gnn_conv_bias", "L1_gnn_ln_g", "L1_gnn_ln_b", "L1_gnn_ln1_g",
        "L1_gnn_ln1_b", "L1_gnn_fc_w", "L1_gnn_fc_b", "L1_gnn_fc1_w", "L1_gnn_fc1_b", "L3_gnn_W", "L3_gnn_b"]


def gnn_program(nc, x, src, dst, edge_attr, edge_weight, Wl, bl, Wr, br, We, att, conv_bias,
                ln_g, ln_b, ln1_g, ln1_b, fc_w, fc_b, fc1_w, fc1_b, W3, b3, out):
    f32, i32, f16, bf16 = mybir.dt.float32, mybir.dt.int32, mybir.dt.float16, mybir.dt.bfloat16
    ALU = mybir.AluOpType
    ACT = mybir.ActivationFunctionType
    AX = mybir.AxisListType

    N, D = x.shape
    E = src.shape[0]
    H = att.shape[0]
    HC = H * D
    P = 128
    G = 8
    NT = 200
    NCH = NT // G
    HALF = NT // 2
    NP = 125
    NN = N // NP
    PAD = 65535
    FAR = 1 << 20
    BIG = 1.0e30
    EPS = 1e-5
    W1 = D + 1
    RW = D + 4
    full_rows, rest = E // P, E % P
    assert NP * NN == N and NT * P >= E and NT == NCH * G and D == 64 and P == 2 * D

    dstP = nc.dram_tensor("dstP", (NT * P,), f32, kind="Internal").ap()
    srcP = nc.dram_tensor("srcP", (NT * P,), f32, kind="Internal").ap()
    NY = 4
    YR = NT * P + P
    Yk = [nc.dram_tensor(f"Y{k}", (YR, D), f32, kind="Internal").ap() for k in range(NY)]
    TY = nc.dram_tensor("TY", (NT * P + YR, D), f32, kind="Internal").ap()
    XT = nc.dram_tensor("XT", (N, RW), f32, kind="Internal").ap()
    T1 = nc.dram_tensor("T1", (NT * P, D), f32, kind="Internal").ap()
    FLd = nc.dram_tensor("FLd", (2, NT, W1), f32, kind="Internal").ap()
    CAd = nc.dram_tensor("CAd", (2, NT, W1), f32, kind="Internal").ap()
    SPT = -(-6 * (NT // 25) * P // W1)
    Msp = nc.dram_tensor("Msp", (P, SPT, W1), f32, kind="Internal").ap()
    SMd = nc.dram_tensor("SMd", (2, NT * H), f32, kind="Internal").ap()
    SCd = nc.dram_tensor("SCd", (2, NT * H), f32, kind="Internal").ap()

    SFd = nc.dram_tensor("SFd", (3, P, NT), f32, kind="Internal").ap()
    SId = nc.dram_tensor("SId", (5, P, NT), i32, kind="Internal").ap()

    top = ExitStack()

    def sb_in(stack, name, shape, dt=f32):
        return stack.enter_context(nc.sbuf_tensor(name, shape, dt))

    def ps_in(stack, name, shape, dt=f32):
        return stack.enter_context(nc.psum_tensor(name, shape, dt))

    def sem(name):
        s = nc.alloc_semaphore(name)
        phase_sems.append(s)
        return s

    phase_sems = []

    def phase():
        phase_sems.clear()
        stack = ExitStack()

        def end():
            nc.clear_and_free_semaphores(list(phase_sems))
            nc.all_engine_barrier()
        stack.callback(end)
        return stack

    def bc(ap, dim, shape):
        return ap.unsqueeze(dim).broadcast_to(shape)

    class Steps:

        def __init__(self, eng, name):
            self.eng, self.sem, self.base, self.k, self.before = eng, sem(name), 0, 0, None

        def __call__(self, ins):
            ins.then_inc(self.sem, 1)
            self.k += 1
            self.eng.wait_ge(self.sem, self.base + self.k)

        def chunk(self, c, per, before=0):
            self.base, self.k, self.per = c * per + before, 0, per

        def end(self):
            assert self.k == self.per, self.k

        def turn(self, w, per, begins):
            if begins:
                if self.before is None:
                    self.before = self.k
                self.base, self.k = self.before + (w - 2) * per, 0

    def chunks(body):
        def run(eng):
            body(eng, 0, 0)
            body(eng, 0, 1)
            with eng.Fori(1, NCH // 2) as i:
                body(eng, i, 0)
                body(eng, i, 1)
            body(eng, NCH // 2, 0)
        return run

    def chunks_ahead(one, rest):
        def run(eng):
            def two(i):
                one(eng, i, 1)
                rest(eng, i, 0)
                one(eng, i + 1, 0)
                rest(eng, i, 1)
            one(eng, 0, 0)
            two(0)
            with eng.Fori(1, NCH // 2) as i:
                two(i)
            rest(eng, NCH // 2, 0)
        return run

    def wait_past(eng, s, value):
        if not isinstance(value, int) or value > 0:
            eng.wait_ge(s, value)

    with top:
        sb = lambda name, shape, dt=f32: sb_in(top, name, shape, dt)
        XS = sb("XS", [P, NT, D])
        XD = sb("XD", [P, NT, D])
        M = sb("M", [P, NT, W1])
        ident = sb("ident", [P, P])
        dstF = sb("dstF", [P, NT])
        repF = sb("repF", [P, NT])
        riI = sb("riI", [P, NT], i32)
        RC = sb("RC", [P, NT])
        RCM = sb("RCM", [P, NT])
        SFL = sb("SFL", [P, NT, 2])
        BLF = sb("BLF", [HALF, 2, NT])
        BFL = sb("BFL", [HALF, 2, NT])
        eps = sb("eps", [P, 1])
        ones = sb("ones", [1, P])
        BDc = sb("BDc", [P, P])
        BDj = sb("BDj", [P, P])
        BD2 = sb("BD2", [P, P])
        g1B = sb("g1B", [P, D])
        BD3 = sb("BD3", [P, P])
        biasR = sb("biasR", [3, 3, D], bf16)
        ones3 = sb("ones3", [3, P], bf16)
        cD = sb("cD", [P, 3, D])
        WA = sb("WA", [P, HC])
        WBr = sb("WBr", [D, HC])
        WS = sb("WS", [P, HC])
        WlS = sb("WlS", [P, 3, D])
        attC = sb("attC", [P, 3, H])
        mb = sb("mb", [P, 3])
        def source_columns(stack, n):
            srcF = sb_in(stack, f"srcF{n}", [P, NT])
            idY = sb_in(stack, f"idY{n}", [P, NT], i32)
            csI = sb_in(stack, f"csI{n}", [P, NT], i32)
            cdI = sb_in(stack, f"cdI{n}", [P, NT], i32)
            srcS = sb_in(stack, f"srcS{n}", [P, NT], i32)
            ewF = sb_in(stack, f"ewF{n}", [P, NT])
            dstS = sb_in(stack, f"dstS{n}", [P, NT], i32)
            OD = sb_in(stack, f"OD{n}", [P, NT])
            return srcF, ewF, OD, idY, csI, cdI, srcS, dstS

        def move_columns(columns, out_of_chip):
            with phase(), nc.Block() as block:
                s_m = sem("mv_out" if out_of_chip else "mv_back")

                @block.sync
                def _(sp):
                    for n, col in enumerate(columns):
                        kept = SFd[n] if n < 3 else SId[n - 3]
                        to, of = (kept, col[:, :]) if out_of_chip else (col[:, :], kept)
                        sp.dma_start(to, of).then_inc(s_m, 16)
                    sp.wait_ge(s_m, 16 * len(columns))

        columns_st = ExitStack()
        columns = source_columns(columns_st, 1)
        srcF, ewF, OD, idY, csI, cdI, srcS, dstS = columns
        early = ExitStack()
        srcG = sb_in(early, "srcG", [P, NT], i32)
        dstG = sb_in(early, "dstG", [P, NT], i32)
        RI = sb_in(early, "RI", [P, NT])
        CS = sb_in(early, "CS", [P, NT])
        CD = sb_in(early, "CD", [P, NT])
        tab_st = ExitStack()
        TAB = sb_in(tab_st, "TAB", [P, 3, NN])

        def bias8(n):
            return biasR[0:3, n, :].unsqueeze(1).broadcast_to([3, G, D])

        def load_rows(eng, to, of, count, s):
            rows, last = count // P, count % P
            eng.dma_start(to[0:HALF, 0, :], of[0:HALF * P].rearrange("(p j) -> p j", j=P)).then_inc(s, 16)
            eng.dma_start(to[0:rows - HALF, 1, :],
                          of[HALF * P:rows * P].rearrange("(p j) -> p j", j=P)).then_inc(s, 16)
            eng.dma_start(to[rows - HALF:rows - HALF + 1, 1, 0:last],
                          of[rows * P:count].rearrange("(p j) -> p j", p=1)).then_inc(s, 16)

        def borrowed():
            flat = XS[:, :, :].rearrange("p t d -> p (t d)")
            used = [0]

            def room(shape):
                n = 1
                for v in shape[1:]:
                    n *= v
                ap = flat[0:shape[0], used[0]:used[0] + n]
                used[0] += n
                assert used[0] <= NT * D
                names = "abc"[:len(shape) - 1]
                return ap if len(shape) == 2 else ap.rearrange(
                    f"p ({' '.join(names)}) -> p {' '.join(names)}", **dict(zip(names[1:], shape[2:])))
            return room

        def setup():
            st = phase()
            with st:
                t = lambda name, shape, dt=f32: sb_in(st, name, shape, dt)
                rI = t("rI", [HALF, 3, 2, P], i32)
                room = borrowed()
                rF = room([HALF, 5, 2, P])
                kb = room([HALF, 2, 2, P])
                kFr = room([P, NT])
                kLr = room([P, NT])
                bd = room([P, 3, NT])
                wl = room([D, H, D]); wr = room([D, H, D])
                fw = room([D, P]); fwT = room([P, D]); f1 = room([P, D])
                fbc = room([P, 1]); gcol = room([D, 1]); bcol = room([D, 1])
                w = room([D, 6, D]); wst = room([D, 4, 1])
                w3 = room([D, D])
                rows = room([1, 8, D]); blr = room([1, H, D]); rst = room([1, 4])
                bcolsl = room([P, 3]); bcolsr = room([P, 3])
                g1b = room([P, D])
                b3b = room([P, D])
                b1b = room([P, D])
                bsum = room([1, 3, D]); bback = room([1, 3, D])
                bpart = t("bpart", [1, 3, 3, D], bf16)
                s_bp = sem("su_biasparts")
                pI = ps_in(st, "pI", [P, 4, 512])
                pK = ps_in(st, "pK", [P, 2, 512])
                pW = ps_in(st, "pW", [P, 2, 512])
                s_zero = sem("su_zero"); s_in = sem("su_in"); s_w = sem("su_w")
                s_fl = sem("su_floats"); s_id = sem("su_ident"); s_tp = sem("su_transposed")
                s_kb = sem("su_keys"); s_b = sem("su_masks"); s_out = sem("su_out")
                s_w1 = sem("su_w1"); s_w2 = sem("su_w2");
                with nc.Block() as block:
                    @block.sync
                    def _(sp):
                        sp.wait_ge(s_zero, 1)
                        load_rows(sp, rI[:, 0], src, E, s_in)
                        load_rows(sp, rI[:, 1], dst, E, s_in)
                        load_rows(sp, rI[:, 2], dst[1:E], E - 1, s_in)
                        load_rows(sp, rF[:, 3], edge_weight, E, s_in)
                        sp.wait_ge(s_fl, 1)
                        sp.dma_start(dstP.rearrange("(c p j) -> p c j", c=2, j=P), rF[:, 1]).then_inc(s_out, 16)
                        sp.dma_start(srcP.rearrange("(c p j) -> p c j", c=2, j=P), rF[:, 0]).then_inc(s_out, 16)
                        sp.wait_ge(s_bp, 1)
                        for k in range(3):
                            sp.dma_start(biasR[k:k + 1, :, :], bpart[:, k, :, :]).then_inc(s_out, 16)
                        sp.wait_ge(s_out, 80)

                    @block.scalar
                    def _(act):
                        def ld(to, of):
                            act.dma_start(to, of).then_inc(s_w, 16)
                        row = lambda v: v.rearrange("(a n) -> a n", a=1)
                        col = lambda v: v.rearrange("(n a) -> n a", a=1)
                        act.wait_ge(s_zero, 1)
                        ld(wl[:, :, :], Wl.rearrange("k (h c) -> k h c", h=H))
                        ld(wr[:, :, :], Wr.rearrange("k (h c) -> k h c", h=H))
                        ld(WA[0:D, :], Wl); ld(WA[D:P, :], We); ld(WBr[:, :], Wr)
                        ld(WS[D:P, :], We)
                        ld(fw[:, :], fc_w); ld(f1[:, :], fc1_w); ld(w3[:, :], W3)
                        ld(fbc[:, :], col(fc_b)); ld(gcol[:, :], col(ln_g)); ld(bcol[:, :], col(ln_b))
                        ld(blr[:, :, :], bl.rearrange("(a h c) -> a h c", a=1, h=H))
                        ld(rows[:, 0, :], row(conv_bias)); ld(rows[:, 1, :], row(fc1_b))
                        ld(rows[:, 2, :], row(ln1_g)); ld(rows[:, 3, :], row(b3))
                        for h in range(H):
                            lo = D * (h % 2)
                            ld(attC[lo:lo + D, h // 2, h:h + 1], att[h:h + 1, :].rearrange("a c -> c a"))
                            ld(bcolsl[lo:lo + D, h // 2:h // 2 + 1], col(bl[h * D:(h + 1) * D]))
                            ld(bcolsr[lo:lo + D, h // 2:h // 2 + 1], col(br[h * D:(h + 1) * D]))
                            ld(WlS[lo:lo + D, h // 2, :], Wl[:, h * D:(h + 1) * D])
                        ld(g1b[:, :], row(ln1_g).broadcast_to([P, D]))
                        ld(b1b[:, :], row(ln1_b).broadcast_to([P, D]))
                        ld(b3b[:, :], row(b3).broadcast_to([P, D]))
                    NLOAD = 20 + 4 * H

                    @block.gpsimd
                    def _(pool):
                        pool.memset(ident[:, :], 0.0).then_inc(s_id, 1)
                        pool.wait_ge(s_id, 1)
                        pool.affine_select(out=ident[:, :], in_=ident[:, :], compare_op=ALU.not_equal, fill=1.0,
                                           base=0, pattern=[[-1, P]], channel_multiplier=1).then_inc(s_id, 1)
                        pool.wait_ge(s_b, 1)
                        for c in range(2):
                            pool.affine_select(out=BLF[:, c, :], in_=BLF[:, c, :], compare_op=ALU.is_gt, fill=0.0,
                                               base=-c * HALF, pattern=[[1, NT]], channel_multiplier=-1)
                            pool.affine_select(out=BFL[:, c, :], in_=BFL[:, c, :], compare_op=ALU.is_gt, fill=0.0,
                                               base=c * HALF, pattern=[[-1, NT]], channel_multiplier=1)

                    @block.vector
                    def _(dve):
                        step = Steps(dve, "su_dve")
                        dve.memset(rI[:, 0:2], PAD)
                        dve.memset(rI[:, 2], -1)
                        dve.memset(rF[:, 3], 0.0)
                        dve.memset(attC[:, :, :], 0.0)
                        dve.memset(mb[:, :], 0.0)
                        dve.memset(bcolsl[:, :], 0.0)
                        dve.memset(bcolsr[:, :], 0.0)
                        dve.memset(WlS[:, :, :], 0.0)
                        dve.memset(eps[:, :], EPS)
                        dve.memset(ones[:, :], 1.0)
                        dve.memset(ones3[:, :], 1.0)
                        for b_ in (BDc, BDj, BD2, BD3):
                            dve.memset(b_[:, :], 0.0)
                        step(dve.memset(rF[:, 4], 0.0))
                        dve.sem_inc(s_zero, 1)
                        dve.wait_ge(s_in, 16 * 12)
                        step(dve.tensor_copy(rF[:, 0:3].rearrange("p a c j -> p (a c j)"),
                                             rI[:, :].rearrange("p a c j -> p (a c j)")))
                        dve.sem_inc(s_fl, 1)
                        for k, end in enumerate((0, P - 1)):
                            for c in range(2):
                                dve.tensor_copy(kb[:, k, c, :],
                                                rF[:, 1, c, end:end + 1].broadcast_to([HALF, P]))
                        step(dve.tensor_tensor(rF[:, 4].rearrange("p c j -> p (c j)"),
                                               rF[:, 1].rearrange("p c j -> p (c j)"),
                                               rF[:, 2].rearrange("p c j -> p (c j)"), ALU.not_equal))
                        dve.sem_inc(s_kb, 1)
                        dve.wait_ge(s_tp, 1)
                        for n, to in enumerate((srcF, dstF, ewF, repF)):
                            dve.tensor_copy(to[:, :], pI[:, n, 0:NT])
                        dve.tensor_copy(kFr[:, :], pK[:, 0, 0:NT])
                        step(dve.tensor_copy(kLr[:, :], pK[:, 1, 0:NT]))
                        for c in range(2):
                            dve.tensor_scalar(BLF[:, c, :], kFr[0:HALF, :], rF[:, 1, c, P - 1:P], None, ALU.is_equal)
                            dve.tensor_scalar(BFL[:, c, :], kLr[0:HALF, :], rF[:, 1, c, 0:1], None, ALU.is_equal)
                        dve.tensor_tensor(SFL[:, :, 0], dstF[:, :], kFr[:, :], ALU.is_equal)
                        step(dve.tensor_tensor(SFL[:, :, 1], dstF[:, :], kLr[:, :], ALU.is_equal))
                        dve.sem_inc(s_b, 1)
                        for f, g in ((srcF, srcG), (dstF, dstG)):
                            step(dve.tensor_scalar(bd[:, 0, :], f[:, :], float(N), None, ALU.is_lt))
                            step(dve.tensor_tensor(bd[:, 1, :], bd[:, 0, :], f[:, :], ALU.mult))
                            step(dve.tensor_copy(g[:, :], bd[:, 1, :]))
                        step(dve.tensor_scalar(bd[:, 0, :], repF[:, :], -float(FAR), float(FAR), ALU.mult, ALU.add))
                        step(dve.tensor_tensor(bd[:, 1, :], bd[:, 0, :], dstF[:, :], ALU.add))
                        step(dve.tensor_copy(dstS[:, :], bd[:, 1, :]))
                        dve.wait_ge(s_w, 16 * NLOAD)
                        dve.wait_ge(s_id, 2)
                        I64 = ident[0:D, 0:D]

                        def centre(ap, acc):
                            step(dve.tensor_reduce(acc, ap, AX.X, ALU.add))
                            step(dve.tensor_scalar(acc, acc, -1.0 / D, None, ALU.mult))
                            step(dve.tensor_scalar(ap, ap, acc, None, ALU.add))

                        def mean_heads(to, of):
                            step(dve.tensor_tensor(to, of[:, 0, :], of[:, 1, :], ALU.add))
                            for h in range(2, H):
                                step(dve.tensor_tensor(to, to, of[:, h, :], ALU.add))
                            step(dve.tensor_scalar(to, to, 1.0 / H, None, ALU.mult))

                        def diagonal(bd_, ap):
                            dve.tensor_copy(bd_[0:D, 0:D], ap)
                            step(dve.tensor_copy(bd_[D:P, D:P], ap))

                        mean_heads(w[:, 0, :], wl)
                        step(dve.tensor_tensor(w[:, 0, :], w[:, 0, :], I64, ALU.add))
                        centre(w[:, 0, :], wst[:, 0, :])
                        diagonal(BDc, w[:, 0, :])
                        step(dve.tensor_copy(w[:, 1, :], I64))
                        centre(w[:, 1, :], wst[:, 1, :])
                        diagonal(BDj, w[:, 1, :])
                        diagonal(BD3, w3[:, :])
                        mean_heads(rows[:, 4, :], blr)
                        step(dve.tensor_tensor(rows[:, 4, :], rows[:, 4, :], rows[:, 0, :], ALU.add))
                        centre(rows[:, 4, :], rst[:, 0:1])
                        for k in range(3):
                            centre(WlS[:, k, :], bd[:, 2, k:k + 1])
                        step(dve.tensor_tensor(WS[0:D, :], wl[:, :, :].rearrange("k h c -> k (h c)"),
                                               wr[:, :, :].rearrange("k h c -> k (h c)"), ALU.add))
                        step(dve.tensor_tensor(mb[:, :], bcolsl[:, :], bcolsr[:, :], ALU.add))
                        dve.tensor_copy(cD[:, 0, :], b1b[:, :])
                        step(dve.tensor_scalar(cD[:, 2, :], b3b[:, :], 0.0, None, ALU.max))
                        step(dve.tensor_tensor(cD[:, 1, :], cD[:, 2, :], b1b[:, :], ALU.add))
                        dve.wait_ge(s_w1, 1)
                        step(dve.tensor_copy(fwT[:, :], pW[:, 0, 0:D]))
                        dve.sem_inc(s_w2, 1)
                        dve.wait_ge(s_w1, 2)
                        step(dve.tensor_tensor(w[:, 2, :], pW[0:D, 0, D:P], I64, ALU.add))
                        dve.sem_inc(s_w2, 1)
                        dve.wait_ge(s_w1, 3)
                        step(dve.tensor_tensor(rows[:, 5, :], pW[0:1, 1, 0:D], rows[:, 1, :], ALU.add))
                        centre(rows[:, 5, :], rst[:, 1:2])
                        centre(w[:, 2, :], wst[:, 2, :])
                        step(dve.tensor_scalar(w[:, 3, :], w[:, 2, :], gcol[:, :], None, ALU.mult))
                        diagonal(BD2, w[:, 3, :])
                        step(dve.tensor_copy(g1B[:, :], g1b[:, :]))
                        for n, r in enumerate((4, 5, 3)):
                            step(dve.tensor_copy(bsum[:, n, :], rows[:, r, :]))
                        for k in range(3):
                            step(dve.tensor_copy(bpart[:, k, :, :], bsum[:, :, :]))
                            step(dve.tensor_copy(bback[:, :, :], bpart[:, k, :, :]))
                            step(dve.tensor_tensor(bsum[:, :, :], bsum[:, :, :], bback[:, :, :], ALU.subtract))
                        dve.sem_inc(s_bp, 1)

                    @block.tensor
                    def _(pe):
                        pe.wait_ge(s_id, 2)
                        pe.wait_ge(s_kb, 1)
                        for n, r in enumerate((0, 1, 3, 4)):
                            for c in range(2):
                                pe.transpose(pI[:, n, c * HALF:(c + 1) * HALF], rF[:, r, c, :],
                                             ident[0:HALF, 0:HALF])
                        for k in range(2):
                            for c in range(2):
                                last = pe.matmul(pK[:, k, c * HALF:(c + 1) * HALF], kb[:, k, c, :],
                                                 ident[0:HALF, 0:HALF], start=True, stop=True)
                        last.then_inc(s_tp, 1)
                        pe.wait_ge(s_w, 16 * NLOAD)
                        pe.transpose(pW[:, 0, 0:D], fw[:, :], ident[0:D, 0:D]).then_inc(s_w1, 1)
                        pe.wait_ge(s_w2, 1)
                        pe.matmul(pW[0:D, 0, D:P], fwT[:, :], f1[:, :], start=True, stop=True).then_inc(s_w1, 1)
                        pe.wait_ge(s_w2, 2)
                        pe.matmul(pW[0:1, 1, 0:D], fbc[:, :], f1[:, :], start=True, stop=False)
                        pe.matmul(pW[0:1, 1, 0:D], bcol[:, :], w[:, 2, :], start=False, stop=True).then_inc(s_w1, 1)

        setup()

        def gather_setup(st, name, width, slots=2):
            return dict(ring=sb_in(st, name + "_ring", [P, slots, G, width]),
                        idx=sb_in(st, name + "_idx", [P, slots, G], i32),
                        sems=[sem(f"{name}_rows{u}") for u in range(slots)], free=sem(name + "_free"),
                        pool=sem(name + "_pool"), go=sem(name + "_go"), width=width)

        def gather_chunk(pool, i, u, g, table, index, bound):
            c = i * 2 + u
            pool.wait_ge(g["free"], c + 1)
            wait_past(pool, g["sems"][u], i * (16 * G))
            pool.tensor_copy(g["idx"][:, u, :], index[:, bass.ds(c * G, G)]).then_inc(g["pool"], 1)
            pool.wait_ge(g["pool"], c + 1)
            pool.sem_inc(g["go"], 1)
            for j in range(G):
                pool.indirect_dma_start(
                    out=g["ring"][:, u, j, :], out_offset=None, in_=table,
                    in_offset=bass.IndirectOffsetOnAxis(ap=g["idx"][:, u, j:j + 1], axis=0),
                    bounds_check=bound, oob_is_err=False).then_inc(g["sems"][u], 16)

        def tables():
            st = phase()
            with st:
                t = lambda name, shape, dt=f32: sb_in(st, name, shape, dt)
                iN = t("iN", [P, NN], i32); loI = t("loI", [P, NN], f16)
                iH = t("iH", [P, P], i32); hiI = t("hiI", [P, P], f16)
                iT = t("iT", [P, NT], i32); iP = t("iP", [P, NT], i32)
                room = borrowed()
                tnum = room([P, NT]); pnum = room([P, NT])
                hi32 = t("hi32", [P, NT], i32)
                hi = room([P, 2, NT]); lo = room([P, 2, NT]); tmp = room([P, NT])
                U = 2
                ohl = t("ohl", [P, 2, U, 2, NN], f16)
                ohh = t("ohh", [P, 2, U, 3, P], f16)
                pT = ps_in(st, "pT", [P, 3, 512])
                lower = t("lower", [P, NP]); total = t("total", [P, 1]); offs = t("offs", [P, 1])
                has = room([P, 2, NN])
                pO = ps_in(st, "pO", [P, 512])
                s_lo = sem("tb_lower"); s_tot = sem("tb_total"); s_of = sem("tb_offsets")
                s_z = sem("tb_zero"); s_y = sem("tb_yzero")
                s_i = sem("tb_iota"); s_oh = sem("tb_onehots"); s_fr = sem("tb_free"); s_t = sem("tb_tables")
                TURNS = NT // U // 2
                with nc.Block() as block:
                    @block.gpsimd
                    def _(pool):
                        pool.iota(iN[:, :], [[1, NN]], channel_multiplier=0)
                        pool.iota(iH[:, :], [[1, P]], channel_multiplier=0)
                        pool.iota(iT[:, :], [[1, NT]], channel_multiplier=0)
                        pool.iota(iP[:, :], [[0, NT]], base=1, channel_multiplier=1).then_inc(s_i, 1)
                        pool.memset(lower[:, :], 1.0).then_inc(s_lo, 1)
                        pool.wait_ge(s_lo, 1)
                        pool.affine_select(out=lower[:, :], in_=lower[:, :], compare_op=ALU.is_gt, fill=0.0,
                                           base=0, pattern=[[1, NP]], channel_multiplier=-1).then_inc(s_lo, 1)

                    @block.sync
                    def _(sp):
                        sp.wait_ge(s_z, 1)
                        zeros = M[:, :, :].rearrange("p t d -> p (t d)")[:, 0:YR // P * D]
                        for k in range(NY):
                            sp.dma_start(Yk[k].rearrange("(p r) d -> p (r d)", p=P), zeros).then_inc(s_y, 16)
                        sp.wait_ge(s_y, 16 * NY)

                    @block.vector
                    def _(dve):
                        step = Steps(dve, "tb_dve")
                        step(dve.memset(M[:, :, :], 0.0))
                        dve.sem_inc(s_z, 1)
                        dve.wait_ge(s_i, 1)
                        dve.tensor_copy(loI[:, :], iN[:, :])
                        dve.tensor_copy(hiI[:, :], iH[:, :])
                        dve.tensor_copy(tnum[:, :], iT[:, :])
                        step(dve.tensor_copy(pnum[:, :], iP[:, :]))
                        for k, f in enumerate((srcF, dstF)):
                            step(dve.tensor_scalar(tmp[:, :], f[:, :], (1.0 - NN) / 2, 1.0 / NN, ALU.add, ALU.mult))
                            step(dve.tensor_copy(hi32[:, :], tmp[:, :]))
                            step(dve.tensor_copy(hi[:, k, :], hi32[:, :]))
                            step(dve.tensor_scalar(tmp[:, :], hi[:, k, :], -float(NN), None, ALU.mult))
                            step(dve.tensor_tensor(lo[:, k, :], tmp[:, :], f[:, :], ALU.add))
                        step(dve.tensor_tensor(tnum[:, :], tnum[:, :], repF[:, :], ALU.mult))
                        step(dve.tensor_tensor(pnum[:, :], pnum[:, :], repF[:, :], ALU.mult))

                        def body(i, u):
                            c = i * 2 + u
                            dve.wait_ge(s_fr, c + 1)
                            for j in range(U):
                                t_ = c * U + j
                                for k in range(2):
                                    dve.tensor_scalar(ohl[:, u, j, k, :], loI[:, :], lo[:, k, bass.ds(t_, 1)],
                                                      None, ALU.is_equal)
                                dve.tensor_scalar(ohh[:, u, j, 0, :], hiI[:, :], hi[:, 0, bass.ds(t_, 1)],
                                                  None, ALU.is_equal)
                                dve.tensor_scalar(ohh[:, u, j, 1, :], hiI[:, :], hi[:, 1, bass.ds(t_, 1)],
                                                  tnum[:, bass.ds(t_, 1)], ALU.is_equal, ALU.mult)
                                last = dve.tensor_scalar(ohh[:, u, j, 2, :], hiI[:, :], hi[:, 1, bass.ds(t_, 1)],
                                                         pnum[:, bass.ds(t_, 1)], ALU.is_equal, ALU.mult)
                            last.then_inc(s_oh, 1)
                        with dve.Fori(0, TURNS) as i:
                            body(i, 0)
                            body(i, 1)
                        dve.wait_ge(s_t, 1)
                        dve.tensor_copy(TAB[:, 1, :], pT[:, 0, 0:NN])
                        step(dve.tensor_scalar(TAB[:, 2, :], pT[:, 1, 0:NN], float(P), None, ALU.mult))
                        step(dve.tensor_tensor(TAB[:, 0, :], pT[:, 2, 0:NN], TAB[:, 2, :], ALU.add))
                        step(dve.tensor_scalar(has[:, 0, :], TAB[:, 1, :], 0.0, None, ALU.is_gt))
                        step(dve.memset(has[:, 1, :], 1.0))
                        step(dve.tensor_tensor_scan(TAB[:, 2, :], has[:, 1, :], has[:, 0, :], 0.0, ALU.mult, ALU.add))
                        step(dve.tensor_copy(total[:, :], TAB[:, 2, NN - 1:NN]))
                        dve.sem_inc(s_tot, 1)
                        dve.wait_ge(s_of, 1)
                        step(dve.tensor_copy(offs[0:NP, :], pO[0:NP, 0:1]))
                        step(dve.tensor_scalar(TAB[0:NP, 2, :], TAB[0:NP, 2, :], offs[0:NP, :], -1.0, ALU.add, ALU.add))
                        step(dve.tensor_scalar(has[:, 1, :], has[:, 0, :], -float(FAR), float(FAR), ALU.mult, ALU.add))
                        step(dve.tensor_tensor(TAB[:, 2, :], TAB[:, 2, :], has[:, 1, :], ALU.add))

                    @block.tensor
                    def _(pe):
                        pe.sem_inc(s_fr, 2)
                        def body(i, u, first=False, stop=False):
                            c = i * 2 + u
                            pe.wait_ge(s_oh, c + 1)
                            for j in range(U):
                                for n, (a, b) in enumerate(((0, 0), (1, 1), (2, 1))):
                                    last = pe.matmul(pT[:, n, 0:NN], ohh[:, u, j, a, :], ohl[:, u, j, b, :],
                                                     start=first and j == 0, stop=stop and j == U - 1)
                            last.then_inc(s_fr, 1)
                            return last
                        body(0, 0, first=True)
                        body(0, 1)
                        with pe.Fori(1, TURNS - 1) as i:
                            body(i, 0)
                            body(i, 1)
                        body(TURNS - 1, 0)
                        body(TURNS - 1, 1, stop=True)
                        pe.wait_ge(s_fr, 2 * TURNS + 2)
                        pe.sem_inc(s_t, 1)
                        pe.wait_ge(s_lo, 2)
                        pe.wait_ge(s_tot, 1)
                        pe.matmul(pO[0:NP, 0:1], lower[0:NP, :], total[0:NP, :], start=True, stop=True).then_inc(s_of, 1)

        tables()

        NB = NN // (2 * G)
        assert NB == NCH
        x_v = x.rearrange("(p n) d -> p n d", p=NP)
        out_v = out.rearrange("(p n) d -> p n d", p=NP)
        XT_v = XT.rearrange("(p n) d -> p n d", p=NP)
        CUT = 112

        def node_dma(eng, to, of, s):
            eng.dma_start(to[0:CUT], of[0:CUT]).then_inc(s, 16)
            eng.dma_start(to[CUT:NP], of[CUT:NP]).then_inc(s, 16)

        def widen():
            st = phase()
            with st:
                W = sb_in(st, "wd_W", [P, 2, 2 * G, RW])
                s_l = [sem(f"wd_load{u}") for u in range(2)]; s_s = [sem(f"wd_store{u}") for u in range(2)]
                s_z = sem("wd_zero"); s_c = sem("wd_cols")
                with nc.Block() as block:
                    @block.vector
                    def _(dve):
                        dve.memset(W[:, :, :, D + 3:RW], 0.0).then_inc(s_z, 1)
                        def body(eng, i, u):
                            c = i * 2 + u
                            wait_past(eng, s_s[u], i * 32)
                            for k in range(3):
                                last = eng.tensor_scalar(W[:, u, :, D + k], TAB[:, k, bass.ds(c * 2 * G, 2 * G)],
                                                         1.0, None, ALU.mult)
                            last.then_inc(s_c, 1)
                        chunks(body)(dve)

                    @block.sync
                    def _(sp):
                        def body(eng, i, u):
                            c = i * 2 + u
                            wait_past(eng, s_s[u], i * 32)
                            node_dma(eng, W[0:NP, u, :, 0:D], x_v[:, bass.ds(c * 2 * G, 2 * G), :], s_l[u])
                        chunks(body)(sp)

                    @block.scalar
                    def _(act):
                        act.wait_ge(s_z, 1)
                        def body(eng, i, u):
                            c = i * 2 + u
                            eng.wait_ge(s_c, c + 1)
                            eng.wait_ge(s_l[u], (i + 1) * 32)
                            node_dma(eng, XT_v[:, bass.ds(c * 2 * G, 2 * G), :], W[0:NP, u, :, :], s_s[u])
                        chunks(body)(act)
                        act.wait_ge(s_s[0], 32 * (NCH // 2 + 1))
                        act.wait_ge(s_s[1], 32 * (NCH // 2))

        widen()
        tab_st.close()

        def norm_setup(st, name, tiles, xc=None, sq=None):
            return dict(s=sb_in(st, name + "_s", [P, 4, tiles]),
                        xc=sb_in(st, name + "_xc", [P, tiles, D]) if xc is None else xc,
                        sq=sb_in(st, name + "_sq", [P, tiles, D]) if sq is None else sq, v=sem(name + "_var"), sd=sem(name + "_sd"))

        NORM_STEPS = 5

        def norm_dve(dve, step, n, c, xin, emit, p=P, tiles=G, w=0):
            s, xc, sq = n["s"], n["xc"], n["sq"]
            step(dve.tensor_reduce(s[0:p, 0, :], xin, AX.X, ALU.add))
            step(dve.tensor_scalar(s[0:p, 1, :], s[0:p, 0, :], -1.0 / D, None, ALU.mult))
            step(dve.tensor_tensor(xc[0:p], xin, bc(s[0:p, 1, :], 2, [p, tiles, D]), ALU.add))
            step(dve.tensor_tensor(sq[0:p], xc[0:p], xc[0:p], ALU.mult))
            dve.tensor_reduce(s[0:p, 2, :], sq[0:p], AX.X, ALU.add).then_inc(n["v"], 1)
            dve.wait_ge(n["sd"], w + 1)
            step(dve.reciprocal(s[0:p, 0, :], s[0:p, 3, :]))
            emit(xc[0:p], bc(s[0:p, 0, :], 2, [p, tiles, D]))

        def norm_part(dve, step, part, n, xin, to, w):
            s, xc, sq = n["s"], n["xc"], n["sq"]
            if part == 0:
                step(dve.tensor_reduce(s[:, 0, :], xin, AX.X, ALU.add))
                step(dve.tensor_scalar(s[:, 1, :], s[:, 0, :], -1.0 / D, None, ALU.mult))
                step(dve.tensor_tensor(xc, xin, bc(s[:, 1, :], 2, [P, G, D]), ALU.add))
            if part == 1:
                step(dve.tensor_tensor(sq, xc, xc, ALU.mult))
                dve.tensor_reduce(s[:, 2, :], sq, AX.X, ALU.add).then_inc(n["v"], 1)
            if part == 2:
                dve.wait_ge(n["sd"], w + 1)
                step(dve.reciprocal(s[:, 0, :], s[:, 3, :]))
                step(dve.scalar_tensor_tensor(to, xc, 0.0, bc(s[:, 0, :], 2, [P, G, D]), ALU.max, ALU.mult))

        def norm_act(act, n, p=P, w=0):
            act.wait_ge(n["v"], w + 1)
            act.activation(n["s"][0:p, 3, :], n["s"][0:p, 2, :], ACT.Sqrt, bias=eps[0:p, 0:1],
                           scale=1.0 / D).then_inc(n["sd"], 1)

        def relu_into(dve, to):
            return lambda xc, r: dve.scalar_tensor_tensor(to, xc, 0.0, r, ALU.max, ALU.mult)

        def tail_setup(st, name, get=None):
            get = get or (lambda k, shape: sb_in(st, f"{name}_{k}", shape)[:])
            q = {k: get(k, [P, G, D]) for k in ("xc", "sq0", "h", "sq1", "n", "sq2", "t")}
            q.update({k: get(k, [P, 4, P]) for k in ("hT", "nT")})
            q["XB"] = get("XB", [P, 2, G, D])
            q.update({k: sb_in(st, f"{name}_{k}", [P, 4, G]) for k in ("s0", "s1", "s2")})
            q.update({k: ps_in(st, f"{name}_{k}", [P, 512]) for k in ("ph", "pn")})
            q.update({k: ps_in(st, f"{name}_{k}", [P, 2, 512]) for k in ("py", "pz")})
            q.update({k: sem(f"{name}_{k}") for k in (
                "centred", "squared0", "var0", "dev0", "h_ready", "h_transposed", "hT_ready", "y_ready",
                "squared1", "var1", "dev1", "n_ready", "n_transposed", "nT_ready", "z_ready",
                "squared2", "var2", "dev2", "z_read", "xb_ready", "xb_used")})
            return q

        def turns(turn):
            def run(eng):
                turn(eng, 0, 0, 0, True, False, False)
                turn(eng, 0, 0, 1, True, True, False)
                with eng.Fori(0, NCH // 2 - 1) as i:
                    for v in range(2):
                        for k in range(2):
                            turn(eng, i + v, 1 - v, k, True, True, True)
                for v in range(2):
                    for k in range(2):
                        turn(eng, NCH // 2 - 1 + v, 1 - v, k, True, True, True)
                turn(eng, NCH // 2, 1, 0, False, True, True)
                turn(eng, NCH // 2, 1, 1, False, False, True)
            return run

        def tail_pe(pe, q, w, k, flags, first, p=P, opened=False):
            one, two, _ = flags
            tr = lambda to, of: [pe.transpose(to[:, j * P:j * P + p],
                                              of[0:p, 2 * j:2 * j + 2, :].rearrange("p a d -> p (a d)"),
                                              ident[0:p, 0:p]) for j in range(4)][-1]
            if two:
                pe.wait_ge(q["n_ready"], w)
                tr(q["pn"], q["n"]).then_inc(q["n_transposed"], 1)
            if one:
                pe.wait_ge(q["h_ready"], w + 1)
                tr(q["ph"], q["h"]).then_inc(q["h_transposed"], 1)
            if two:
                pe.wait_ge(q["nT_ready"], w)
                pe.wait_ge(q["z_read"], w)
                to = q["pz"][:, 1 - k, :]
                pe.matmul(to[0:p, :], ones3[:, 0:p], bias8(1), start=True, stop=False)
                for j in range(4):
                    last = pe.matmul(to[0:p, j * P:(j + 1) * P], q["nT"][:, j, 0:p], BD2[:, :],
                                     start=False, stop=j == 3)
                last.then_inc(q["z_ready"], 1)
            if one:
                pe.wait_ge(q["hT_ready"], w + 1)
                to = q["py"][:, k, :]
                if not opened:
                    pe.matmul(to[0:p, :], ones3[:, 0:p], bias8(0), start=True, stop=False)
                for j in range(4):
                    last = pe.matmul(to[0:p, j * P:(j + 1) * P], q["hT"][:, j, 0:p], first[:, :],
                                     start=False, stop=j == 3)
                last.then_inc(q["y_ready"], 1)

        def tail_act(act, q, w, k, flags, p=P):
            one, two, three = flags
            g3 = lambda a: a[0:p, :].rearrange("p (g d) -> p g d", d=D)
            c3 = lambda a: a[:, :].rearrange("q (j p) -> q j p", p=P)[:, :, 0:p]

            def root(s, n, at):
                act.wait_ge(q["var" + n], at)
                act.activation(s[0:p, 3, :], s[0:p, 2, :], ACT.Sqrt, bias=eps[0:p, 0:1],
                               scale=1.0 / D).then_inc(q["dev" + n], 1)
            if one:
                act.wait_ge(q["centred"], w + 1)
                act.activation(q["sq0"][0:p], q["xc"][0:p], ACT.Square).then_inc(q["squared0"], 1)
            if two:
                root(q["s1"], "1", w)
            if three:
                root(q["s2"], "2", w - 1)
            if one:
                root(q["s0"], "0", w + 1)
            if two:
                act.wait_ge(q["n_transposed"], w)
                act.activation(q["nT"][:, :, 0:p], c3(q["pn"]), ACT.Copy).then_inc(q["nT_ready"], 1)
            if one:
                act.wait_ge(q["h_transposed"], w + 1)
                act.activation(q["hT"][:, :, 0:p], c3(q["ph"]), ACT.Copy).then_inc(q["hT_ready"], 1)
            if two:
                act.wait_ge(q["z_ready"], w)
                act.activation(q["sq2"][0:p], g3(q["pz"][:, 1 - k, :]), ACT.Square).then_inc(q["squared2"], 1)
            if one:
                act.wait_ge(q["y_ready"], w + 1)
                act.activation(q["sq1"][0:p], g3(q["py"][:, k, :]), ACT.Square).then_inc(q["squared1"], 1)

        TAIL_STEPS = 9

        def tail_dve(dve, step, q, w, k, flags, xin, to, const=None, p=P):
            one, two, three = flags
            g3 = lambda a: a[0:p, :].rearrange("p (g d) -> p g d", d=D)
            s0, s1, s2 = q["s0"], q["s1"], q["s2"]
            by = lambda s, n: bc(s[0:p, n, :], 2, [p, G, D])
            if one:
                wait_past(dve, q["h_ready"], w)
                step(dve.tensor_reduce(s0[0:p, 0, :], xin, AX.X, ALU.add))
                step(dve.tensor_scalar(s0[0:p, 1, :], s0[0:p, 0, :], -1.0 / D, None, ALU.mult))
                dve.tensor_tensor(q["xc"][0:p], xin, by(s0, 1), ALU.add).then_inc(q["centred"], 1)
            if two:
                dve.wait_ge(q["squared1"], w)
                dve.tensor_reduce(s1[0:p, 2, :], q["sq1"][0:p], AX.X, ALU.add).then_inc(q["var1"], 1)
            if three:
                dve.wait_ge(q["squared2"], w - 1)
                dve.tensor_reduce(s2[0:p, 2, :], q["sq2"][0:p], AX.X, ALU.add).then_inc(q["var2"], 1)
            if one:
                dve.wait_ge(q["squared0"], w + 1)
                dve.tensor_reduce(s0[0:p, 2, :], q["sq0"][0:p], AX.X, ALU.add).then_inc(q["var0"], 1)
            if two:
                dve.wait_ge(q["dev1"], w)
                step(dve.reciprocal(s1[0:p, 0, :], s1[0:p, 3, :]))
                dve.tensor_tensor(q["n"][0:p], g3(q["py"][:, 1 - k, :]), by(s1, 0), ALU.mult).then_inc(q["n_ready"], 1)
            if one:
                dve.wait_ge(q["dev0"], w + 1)
                step(dve.reciprocal(s0[0:p, 0, :], s0[0:p, 3, :]))
                dve.scalar_tensor_tensor(q["h"][0:p], q["xc"][0:p], 0.0, by(s0, 0), ALU.max, ALU.mult)\
                    .then_inc(q["h_ready"], 1)
            if three:
                dve.wait_ge(q["dev2"], w - 1)
                step(dve.reciprocal(s2[0:p, 0, :], s2[0:p, 3, :]))
                step(dve.tensor_tensor(q["t"][0:p], g3(q["pz"][:, k, :]), by(s2, 0), ALU.mult))
                dve.sem_inc(q["z_read"], 1)
                step(dve.tensor_tensor(q["t"][0:p], q["t"][0:p], bc(g1B[0:p, :], 1, [p, G, D]), ALU.mult))
                if const is None:
                    dve.wait_ge(q["xb_ready"], w - 1)
                step(dve.tensor_tensor(to, q["t"][0:p], q["XB"][0:p, k], ALU.add))
                dve.sem_inc(q["xb_used"], 1)
            if one and const is not None:
                step(dve.tensor_tensor(q["XB"][0:p, k], xin, bc(cD[0:p, const, :], 1, [p, G, D]), ALU.add))

        def dense():
            st = phase()
            with st:
                g1 = gather_setup(st, "g1", RW)
                g0 = gather_setup(st, "g0", RW)
                flat = M[:, :, :].rearrange("p t d -> p (t d)")
                XR = flat[:, 0:8 * G * D].rearrange("p (a u g d) -> p a u g d", a=2, u=2, d=D)
                X, R = XR[:, 0], XR[:, 1]
                used = [8 * G * D]

                def get(key, shape):
                    n = 1
                    for v in shape[1:]:
                        n *= v
                    used[0] += n
                    ap = flat[:, used[0] - n:used[0]]
                    names = "abc"[:len(shape) - 1]
                    return ap.rearrange(f"p ({' '.join(names)}) -> p {' '.join(names)}",
                                        **dict(zip(names[1:], shape[2:])))
                q = tail_setup(st, "dn", get)
                s_l = [sem(f"dn_load{u}") for u in range(2)]; s_st = [sem(f"dn_store{u}") for u in range(2)]
                s_x = sem("dn_xfree"); s_r = sem("dn_result")
                with nc.Block() as block:
                    @block.gpsimd
                    def _(pool):
                        last_row = pool.to_reg(N - 1)
                        def body(eng, i, u):
                            gather_chunk(eng, i, u, g1, XT, srcG, last_row)
                            gather_chunk(eng, i, u, g0, XT, dstG, last_row)
                        chunks(body)(pool)

                    @block.sync
                    def _(sp):
                        nodes = lambda v, c: v[:, bass.ds(c * 2 * G, 2 * G), :]
                        for c in range(2):
                            node_dma(sp, X[0:NP, c], nodes(x_v, c), s_l[c])
                        def body(c, u, load=True):
                            if load:
                                sp.wait_ge(s_x, c - 1)
                                node_dma(sp, X[0:NP, u], nodes(x_v, c), s_l[u])
                            sp.wait_ge(s_r, c - 1)
                            node_dma(sp, nodes(out_v, c - 2), R[0:NP, u], s_st[u])
                        with sp.Fori(0, NCH // 2 - 1) as i:
                            for u in range(2):
                                body(i * 2 + 2 + u, u)
                        body(NCH - 1, 0)
                        body(NCH, 1, load=False)
                        body(NCH + 1, 0, load=False)
                        sp.wait_ge(s_st[0], 32 * (NCH // 2 + 2))
                        sp.wait_ge(s_st[1], 32 * (NCH // 2 + 1))

                    @block.vector
                    def _(dve):
                        step = Steps(dve, "dn_dve")
                        dve.sem_inc(q["z_read"], 2)
                        for u in range(2):
                            dve.sem_inc(s_st[u], 32)
                        def turn(eng, i, u, k, *flags):
                            w = (i * 2 + u) * 2 + k
                            step.turn(w, TAIL_STEPS, flags[2] and (flags[0] or k == 0))
                            if flags[0] and k == 0:
                                eng.wait_ge(s_l[u], (i + 1) * 32)
                            if flags[2] and k == 0:
                                eng.wait_ge(s_st[1 - u], (i + u) * 32)
                            tail_dve(eng, step, q, w, k, flags, X[0:NP, u, k * G:(k + 1) * G, :],
                                     R[0:NP, 1 - u, k * G:(k + 1) * G, :], 1, p=NP)
                            if k == 1:
                                if flags[0]:
                                    eng.sem_inc(s_x, 1)
                                if flags[2]:
                                    eng.sem_inc(s_r, 1)
                        turns(turn)(dve)

                    @block.scalar
                    def _(act):
                        act.sem_inc(g1["free"], 2)
                        act.sem_inc(g0["free"], 2)
                        def turn(eng, i, u, k, *flags):
                            c = i * 2 + u
                            tail_act(eng, q, c * 2 + k, k, flags, p=NP)
                            if flags[0]:
                                g = (g1, g0)[k]
                                eng.wait_ge(g["sems"][u], (i + 1) * (16 * G))
                                ring = g["ring"][:, u]
                                t_ = bass.ds(c * G, G)
                                if k == 0:
                                    eng.activation(XS[:, t_, :], ring[:, :, 0:D], ACT.Copy)
                                    eng.activation(RI[:, t_], ring[:, :, D], ACT.Copy)
                                    eng.activation(OD[:, t_], ring[:, :, D + 1], ACT.Copy)
                                    eng.activation(CS[:, t_], ring[:, :, D + 2], ACT.Copy).then_inc(g["free"], 1)
                                else:
                                    eng.activation(XD[:, t_, :], ring[:, :, 0:D], ACT.Copy)
                                    eng.activation(CD[:, t_], ring[:, :, D + 2], ACT.Copy).then_inc(g["free"], 1)
                        turns(turn)(act)

                    @block.tensor
                    def _(pe):
                        turns(lambda eng, i, u, k, *flags: tail_pe(eng, q, (i * 2 + u) * 2 + k, k, flags, BDc, p=NP))(pe)

        dense()

        def ends_setup(st, name):
            return dict(fl=sb_in(st, name + "_sfl", [P, 2, G, 2]), ev=sb_in(st, name + "_ev", [2, 2, G * W1]),
                        ps=ps_in(st, name + "_ps", [P, 2, 2, 512]), m=sem(name + "_m"), cp=sem(name + "_cp"), go=sem(name + "_go"),
                        d=sem(name + "_sums"), e=sem(name + "_evac"), st=[sem(f"{name}_st{u}") for u in range(2)])

        def ends_pe(pe, i, u, q, w=W1):
            c = i * 2 + u
            pe.wait_ge(q["m"], c + 1)
            pe.wait_ge(q["cp"], c + 1)
            pe.sem_inc(q["go"], 1)
            for j in range(G):
                last = pe.matmul(q["ps"][0:2, u, j // 4, (j % 4) * w:(j % 4 + 1) * w], q["fl"][:, u, j, :],
                                 M[:, bass.ds(c * G + j, 1), 0:w].rearrange("p a d -> p (a d)"),
                                 start=True, stop=True)
            last.then_inc(q["d"], 1)

        def ends_act_before(act, i, u, q):
            c = i * 2 + u
            act.activation(q["fl"][:, u], SFL[:, bass.ds(c * G, G), :], ACT.Copy).then_inc(q["cp"], 1)

        def ends_act(act, i, u, q, w=W1):
            c = i * 2 + u
            act.wait_ge(q["d"], c + 1)
            wait_past(act, q["st"][u], i * 16)
            act.activation(q["ev"][:, u, 0:G * w].rearrange("k (b n) -> k b n", b=2), q["ps"][0:2, u, :, 0:4 * w], ACT.Copy).then_inc(q["e"], 1)

        def ends_sp(sp, i, u, q, w=W1):
            c = i * 2 + u
            sp.wait_ge(q["e"], c + 1)
            sp.dma_start(FLd[:, bass.ds(c * G, G), 0:w],
                         q["ev"][:, u, 0:G * w].rearrange("k (g d) -> k g d", d=w)).then_inc(q["st"][u], 16)

        def ends_sp_done(sp, q):
            sp.wait_ge(q["st"][0], 16 * (NCH // 2 + 1))
            sp.wait_ge(q["st"][1], 16 * (NCH // 2))

        def carries(name, w=W1):
            st = phase()
            with st:
                fl = sb_in(st, name + "_fl", [HALF, 2, 2, w])
                ca = sb_in(st, name + "_ca", [HALF, 2, 2, w])
                ps = ps_in(st, name + "_ps", [P, 2, 512])
                s_l, s_m, s_e, s_o = sem(name + "_l"), sem(name + "_m"), sem(name + "_e"), sem(name + "_o")
                with nc.Block() as block:
                    @block.sync
                    def _(sp):
                        for k in range(2):
                            sp.dma_start(fl[:, k], FLd[k, :, 0:w].rearrange("(c p) d -> p c d", c=2)).then_inc(s_l, 16)
                        sp.wait_ge(s_e, 1)
                        for k in range(2):
                            sp.dma_start(CAd[k, :, 0:w].rearrange("(c p) d -> p c d", c=2), ca[:, k]).then_inc(s_o, 16)
                        sp.wait_ge(s_o, 32)

                    @block.tensor
                    def _(pe):
                        pe.wait_ge(s_l, 32)
                        for k, (masks, end) in enumerate(((BLF, 1), (BFL, 0))):
                            for c in range(2):
                                for cc in range(2):
                                    last = pe.matmul(ps[0:HALF, k, c * w:(c + 1) * w],
                                                     masks[:, cc, c * HALF:(c + 1) * HALF], fl[:, end, cc, :],
                                                     start=cc == 0, stop=cc == 1)
                        last.then_inc(s_m, 1)

                    @block.vector
                    def _(dve):
                        dve.wait_ge(s_m, 1)
                        dve.tensor_copy(ca[:, :, :, :], ps[0:HALF, :, 0:2 * w].rearrange("p k (c d) -> p k c d", d=w))\
                            .then_inc(s_e, 1)

        def sums_setup(st, name):
            return dict(S=sb_in(st, name + "_S", [P, 2, G, P]),
                        C=sb_in(st, name + "_C", [P, 2, G, W1]), ps=ps_in(st, name + "_ps", [P, 2, 2, 512]),
                        z=sem(name + "_z"), ld=[sem(f"{name}_ld{u}") for u in range(2)], s=sem(name + "_S"),
                        d=sem(name + "_d"))

        def sums_sp(sp, i, u, q, w=W1, carry=True):
            c = i * 2 + u
            if "fr" in q:
                sp.wait_ge(q["fr"], c + 1)
            else:
                wait_past(sp, q["d"], c - 1)
            sp.dma_start(q["S"][:, u].rearrange("p g j -> p (g j)"),
                         dstP[bass.ds(c * G * P, G * P)].rearrange("(a n) -> a n", a=1).broadcast_to([P, G * P]))\
                .then_inc(q["ld"][u], 16)
            if carry:
                for k, row in enumerate((0, P - 1)):
                    sp.dma_start(q["C"][row:row + 1, u, :, 0:w],
                                 CAd[k:k + 1, bass.ds(c * G, G), 0:w]).then_inc(q["ld"][u], 16)

        def sums_start(dve, step, q):
            step(dve.memset(q["C"][:, :, :, :], 0.0))
            dve.sem_inc(q["z"], 1)

        def sums_dve(dve, i, u, q, carry=True):
            c = i * 2 + u
            dve.wait_ge(q["ld"][u], (i + 1) * (48 if carry else 16))
            dve.tensor_tensor(q["S"][:, u], q["S"][:, u], bc(dstF[:, bass.ds(c * G, G)], 2, [P, G, P]),
                              ALU.is_equal).then_inc(q["s"], 1)

        def sums_pe(pe, i, u, q, w=W1):
            c = i * 2 + u
            pe.wait_ge(q["s"], c + 1)
            for j in range(G):
                to = q["ps"][:, u, j // 4, (j % 4) * w:(j % 4 + 1) * w]
                pe.matmul(to, q["S"][:, u, j, :], M[:, bass.ds(c * G + j, 1), 0:w].rearrange("p a d -> p (a d)"),
                          start=True, stop=False)
                last = pe.matmul(to, q["S"][:, u, j, :], q["C"][:, u, j, 0:w], start=False, stop=True)
            last.then_inc(q["d"], 1)

        def sums_view(q, u, w=W1, a=0, b=D):
            return q["ps"][:, u, :, 0:4 * w].rearrange("p k (g d) -> p k g d", d=w)[:, :, :, a:b]

        def v4(ap):
            return ap.rearrange("p (k g) d -> p k g d", k=2)

        def first_messages():
            st = phase()
            with st:
                s_all = sb_in(st, "l0a_s", [P, 2, 4, G])
                xc_all = sb_in(st, "l0a_xc", [P, 2, G, D])
                sq = sb_in(st, "l0a_sq", [P, G, D])
                v, sd = sem("l0a_var"), sem("l0a_dev")
                nms = [dict(s=s_all[:, u], xc=xc_all[:, u], sq=sq[:, :, :], v=v, sd=sd) for u in range(2)]
                q = ends_setup(st, "l0a_en")
                with nc.Block() as block:
                    @block.vector
                    def _(dve):
                        step = Steps(dve, "l0a_dve")
                        def part(eng, n, i, u):
                            c = i * 2 + u
                            t_ = bass.ds(c * G, G)
                            norm_part(eng, step, n, nms[u], XS[:, t_, :], M[:, t_, 0:D], c)

                        def turn(eng, i, u):
                            i_next, u_next = (i + 1, 0) if u else (i, 1)
                            step.chunk(i * 2 + u, 6, 4)
                            part(eng, 0, i_next, u_next)
                            part(eng, 2, i, u)
                            eng.sem_inc(q["m"], 1)
                            part(eng, 1, i_next, u_next)
                            step.end()
                        part(dve, 0, 0, 0)
                        part(dve, 1, 0, 0)
                        with dve.Fori(0, NCH // 2) as i:
                            turn(dve, i, 0)
                            turn(dve, i, 1)
                        step.chunk(NCH - 1, 6, 4)
                        part(dve, 2, NCH // 2, 0)
                        dve.sem_inc(q["m"], 1)

                    @block.scalar
                    def _(act):
                        def root(eng, i, u):
                            ends_act_before(eng, i, u, q)
                            norm_act(eng, nms[u], w=i * 2 + u)
                        chunks_ahead(root, lambda eng, i, u: ends_act(eng, i, u, q))(act)

                    @block.tensor
                    def _(pe):
                        chunks(lambda eng, i, u: ends_pe(eng, i, u, q))(pe)

                    @block.sync
                    def _(sp):
                        chunks(lambda eng, i, u: ends_sp(eng, i, u, q))(sp)
                        ends_sp_done(sp, q)

        def after_gather(dve, step):
            step(dve.tensor_scalar(RC[:, :], RI[:, :], 0.0, None, ALU.is_equal))
            step(dve.tensor_scalar(RC[:, :], RC[:, :], float(FAR), -1.0, ALU.mult, ALU.add))
            step(dve.tensor_tensor(RI[:, :], RI[:, :], RC[:, :], ALU.add))
            step(dve.tensor_copy(riI[:, :], RI[:, :]))
            step(dve.tensor_copy(csI[:, :], CS[:, :]))
            step(dve.tensor_scalar(CD[:, :], CD[:, :], float(NT * P), None, ALU.add))
            step(dve.tensor_copy(cdI[:, :], CD[:, :]))
            step(dve.tensor_scalar(RC[:, :], RI[:, :], float(NT * P), float(FAR), ALU.is_lt, ALU.mult))
            step(dve.tensor_tensor(RC[:, :], RC[:, :], srcF[:, :], ALU.add))
            step(dve.tensor_copy(srcS[:, :], RC[:, :]))
            step(dve.tensor_scalar(OD[:, :], OD[:, :], 1.0, None, ALU.max))

        with phase(), nc.Block() as block:
            @block.vector
            def _(dve):
                step = Steps(dve, "ri_dve")
                after_gather(dve, step)
                step(dve.memset(M[:, :, D:W1], 1.0))
        early.close()
        first_messages()
        carries("l0b")

        def means_and_squares():
            st = phase()
            with st:
                q = sums_setup(st, "l0c_s")
                e = ends_setup(st, "l0c_e")
                mean = sb_in(st, "l0c_mean", [P, G, D])
                d = sb_in(st, "l0c_d", [P, 2, G, D])
                cnt = sb_in(st, "l0c_cnt", [P, 2, G])
                s_d = sem("l0c_dev"); s_df = sem("l0c_devfree")
                PER = 5
                with nc.Block() as block:
                    @block.sync
                    def _(sp):
                        sp.wait_ge(q["z"], 1)
                        chunks(lambda eng, i, u: sums_sp(eng, i, u, q))(sp)

                    @block.vector
                    def _(dve):
                        step = Steps(dve, "l0c_dve")
                        dve.sem_inc(s_df, 2)
                        sums_start(dve, step, q)
                        def body(eng, i, u):
                            c = i * 2 + u
                            step.chunk(c, PER, 1)
                            eng.wait_ge(q["d"], c + 1)
                            cc = sums_view(q, u, W1, D, W1)
                            t2 = lambda a: a[:, bass.ds(c * G, G)]
                            eng.tensor_scalar(v4(cnt[:, u, :].unsqueeze(2)), cc, 1.0, None, ALU.is_gt)
                            step(eng.reciprocal(v4(t2(RC).unsqueeze(2)), cc))
                            step(eng.tensor_tensor(t2(RCM), t2(RC), cnt[:, u, :], ALU.mult))
                            step(eng.tensor_tensor(v4(mean[:, :, :]), sums_view(q, u),
                                                   v4(bc(t2(RC), 2, [P, G, D])), ALU.mult))
                            eng.wait_ge(s_df, c + 1)
                            step(eng.tensor_tensor(d[:, u], M[:, bass.ds(c * G, G), 0:D], mean[:, :, :], ALU.subtract))
                            step(eng.tensor_tensor(M[:, bass.ds(c * G, G), 0:D], d[:, u], d[:, u], ALU.mult))
                            eng.sem_inc(s_df, 1)
                            eng.sem_inc(e["m"], 1)
                            step.end()
                        chunks_ahead(lambda eng, i, u: sums_dve(eng, i, u, q), body)(dve)

                    @block.scalar
                    def _(act):
                        def ends(eng, i, u):
                            ends_act(eng, i, u, e, D)
                            ends_sp(eng, i, u, e, D)
                        chunks_ahead(lambda eng, i, u: ends_act_before(eng, i, u, e), ends)(act)
                        ends_sp_done(act, e)

                    @block.tensor
                    def _(pe):
                        chunks_ahead(lambda eng, i, u: sums_pe(eng, i, u, q),
                                     lambda eng, i, u: ends_pe(eng, i, u, e, D))(pe)

        means_and_squares()
        carries("l0d", D)

        def update(name, table, emit, per, act_fn=None, w=D):
            st = phase()
            with st:
                q = sums_setup(st, name + "_s")
                t = sb_in(st, name + "_t", [P, 2, G, D])
                s_x = sem(name + "_xd"); s_a = sem(name + "_a"); s_b = sem(name + "_b")
                s_st = sem(name + "_st"); s_io = sem(name + "_iota")
                S2 = sb_in(st, name + "_S2", [P, G, P])
                jI = sb_in(st, name + "_jI", [P, P], i32); jF = sb_in(st, name + "_jF", [P, P])
                pI_ = sb_in(st, name + "_pI", [P, 1], i32); pF = sb_in(st, name + "_pF", [P, 2])
                lastR = sb_in(st, name + "_last", [P, NT]); tmp = sb_in(st, name + "_tmp", [P, NT])
                tmp2 = sb_in(st, name + "_tmp2", [P, NT])
                s_sr = sem(name + "_src"); s_sf = sem(name + "_srcfree")
                with nc.Block() as block:
                    @block.gpsimd
                    def _(pool):
                        pool.iota(jI[:, :], [[1, P]], channel_multiplier=0)
                        pool.iota(pI_[:, :], [[1, 1]], channel_multiplier=1).then_inc(s_io, 1)

                    @block.sync
                    def _(sp):
                        sp.wait_ge(q["z"], 1)
                        def src_rows(eng, i, u):
                            c = i * 2 + u
                            eng.wait_ge(s_sf, c + 1)
                            eng.dma_start(S2[:, :, :].rearrange("p g j -> p (g j)"),
                                          srcP[bass.ds(c * G * P, G * P)].rearrange("(a n) -> a n", a=1)
                                          .broadcast_to([P, G * P])).then_inc(s_sr, 16)
                        chunks_ahead(lambda eng, i, u: sums_sp(eng, i, u, q, w), src_rows)(sp)

                    @block.vector
                    def _(dve):
                        step = Steps(dve, name + "_dve")
                        sums_start(dve, step, q)
                        dve.sem_inc(s_sf, 1)
                        dve.wait_ge(s_io, 1)
                        dve.tensor_copy(jF[:, :], jI[:, :])
                        step(dve.tensor_copy(pF[:, 0:1], pI_[:, :]))
                        def body(eng, i, u):
                            c = i * 2 + u
                            step.chunk(c, per + 3, 2)
                            eng.wait_ge(q["d"], c + 1)
                            emit(eng, step, i, u, q, t, s_a, s_b)
                            eng.sem_inc(s_x, 1)
                            eng.wait_ge(s_sr, c * 16 + 16)
                            step(eng.tensor_tensor(S2[:, :, :], S2[:, :, :], bc(srcF[:, bass.ds(c * G, G)], 2, [P, G, P]),
                                                   ALU.is_equal))
                            step(eng.tensor_tensor(S2[:, :, :], S2[:, :, :], bc(jF[:, :], 1, [P, G, P]), ALU.mult))
                            step(eng.tensor_reduce(lastR[:, bass.ds(c * G, G)], S2[:, :, :], AX.X, ALU.max))
                            eng.sem_inc(s_sf, 1)
                            step.end()
                        chunks_ahead(lambda eng, i, u: sums_dve(eng, i, u, q), body)(dve)
                        step.base, step.k = (per + 3) * NCH + 2, 0
                        step(dve.tensor_scalar(lastR[:, :], lastR[:, :], pF[:, 0:1], None, ALU.is_equal))
                        step(dve.tensor_scalar(tmp[:, :], srcF[:, :], float(N), None, ALU.is_lt))
                        step(dve.tensor_tensor(lastR[:, :], lastR[:, :], tmp[:, :], ALU.mult))
                        step(dve.tensor_scalar(pF[:, 1:2], pF[:, 0:1], float(NT * P), None, ALU.add))
                        step(dve.tensor_copy(tmp[:, :], csI[:, :]))
                        step(dve.tensor_scalar(tmp[:, :], tmp[:, :], pF[:, 1:2], None, ALU.subtract))
                        step(dve.tensor_tensor(tmp[:, :], tmp[:, :], lastR[:, :], ALU.mult))
                        step(dve.tensor_scalar(tmp[:, :], tmp[:, :], pF[:, 1:2], None, ALU.add))
                        step(dve.tensor_copy(idY[:, :], tmp[:, :]))
                        step(dve.tensor_copy(tmp[:, :], csI[:, :]))
                        step(dve.tensor_scalar(tmp[:, :], tmp[:, :], float(NT * P), float(2 * NT * P), ALU.add, ALU.min))
                        step(dve.tensor_copy(tmp2[:, :], riI[:, :]))
                        step(dve.tensor_scalar(RCM[:, :], tmp2[:, :], float(NT * P), None, ALU.is_ge))
                        step(dve.tensor_tensor(tmp[:, :], tmp[:, :], tmp2[:, :], ALU.subtract))
                        step(dve.tensor_tensor(tmp[:, :], tmp[:, :], RCM[:, :], ALU.mult))
                        step(dve.tensor_tensor(tmp[:, :], tmp[:, :], tmp2[:, :], ALU.add))
                        step(dve.tensor_copy(csI[:, :], tmp[:, :]))
                        step(dve.tensor_scalar(lastR[:, :], lastR[:, :], -float(FAR), float(FAR), ALU.mult, ALU.add))
                        step(dve.tensor_copy(tmp[:, :], srcS[:, :]))
                        step(dve.tensor_tensor(tmp[:, :], tmp[:, :], lastR[:, :], ALU.add))
                        step(dve.tensor_copy(srcS[:, :], tmp[:, :]))

                    @block.tensor
                    def _(pe):
                        chunks(lambda eng, i, u: sums_pe(eng, i, u, q, w))(pe)

                    @block.scalar
                    def _(act):
                        def body(eng, i, u):
                            c = i * 2 + u
                            if act_fn is not None:
                                act_fn(eng, i, u, t, s_a, s_b)
                            eng.wait_ge(s_x, c + 1)
                            eng.dma_start(table[bass.ds(c * G * P, G * P), :].rearrange("(g p) d -> p g d", p=P),
                                          XD[:, bass.ds(c * G, G), :]).then_inc(s_st, 16)
                        chunks(body)(act)
                        act.wait_ge(s_st, 16 * NCH)

        def deviation(eng, step, i, u, q, t, s_a, s_b):
            c = i * 2 + u
            xd = XD[:, bass.ds(c * G, G), :]
            eng.tensor_tensor(v4(t[:, u]), sums_view(q, u, D), v4(bc(RCM[:, bass.ds(c * G, G)], 2, [P, G, D])),
                              ALU.mult).then_inc(s_a, 1)
            eng.wait_ge(s_b, c + 1)
            step(eng.tensor_tensor(xd, xd, t[:, u], ALU.add))

        def deviation_root(act, i, u, t, s_a, s_b):
            c = i * 2 + u
            act.wait_ge(s_a, c + 1)
            act.activation(t[:, u], t[:, u], ACT.Sqrt).then_inc(s_b, 1)

        update("l0e", T1, deviation, 1, deviation_root)

        def attributes():
            st = phase()
            with st:
                q = ends_setup(st, "l1a_en")
                s_e = [sem(f"l1a_ea{n}") for n in range(5)]; s_z = sem("l1a_z"); s_el = sem("l1a_ealast")
                PARTS = 5
                with nc.Block() as block:
                    @block.vector
                    def _(dve):
                        dve.memset(M[:, full_rows:NT, 0:D], 0.0).then_inc(s_z, 1)
                        for n in range(PARTS):
                            dve.wait_ge(s_e[n], 16)
                            if n == PARTS - 1:
                                dve.wait_ge(s_el, 16)
                            dve.sem_inc(q["m"], NCH // PARTS)

                    @block.scalar
                    def _(act):
                        chunks_ahead(lambda eng, i, u: ends_act_before(eng, i, u, q),
                                     lambda eng, i, u: ends_act(eng, i, u, q, D))(act)

                    @block.tensor
                    def _(pe):
                        chunks(lambda eng, i, u: ends_pe(eng, i, u, q, D))(pe)

                    @block.sync
                    def _(sp):
                        per = NT // PARTS
                        for n in range(PARTS):
                            lo, hi = n * per, min((n + 1) * per, full_rows)
                            sp.dma_start(M[:, lo:hi, 0:D],
                                         edge_attr[lo * P:hi * P, :].rearrange("(t p) d -> p t d", p=P)).then_inc(s_e[n], 16)
                        sp.wait_ge(s_z, 1)
                        sp.dma_start(M[0:rest, full_rows, 0:D], edge_attr[full_rows * P:E, :]).then_inc(s_el, 16)
                        chunks(lambda eng, i, u: ends_sp(eng, i, u, q, D))(sp)
                        ends_sp_done(sp, q)

        attributes()
        move_columns(columns, True)
        columns_st.close()
        carries("l1b", D)

        alive = ExitStack()
        with alive:
            LG = sb_in(alive, "LG", [P, 2, NT, H])

            def logits():
                st = phase()
                with st:
                    B4 = G // 2
                    TN = 2 * NCH
                    S = sb_in(st, "l1c_S", [P, 2, B4, P])
                    C = sb_in(st, "l1c_C", [P, 2, B4, D])
                    AB = sb_in(st, "l1c_AB", [P, 2, 2, B4, P])
                    ABT = sb_in(st, "l1c_ABT", [P, 2, 2, B4, P])
                    LK = sb_in(st, "l1c_LK", [P, 3, B4 * P])
                    ring = sb_in(st, "l1c_ring", [P, 2, B4, D])
                    idx = sb_in(st, "l1c_idx", [P, 2, B4], i32)
                    s4 = sb_in(st, "l1c_s4", [P, 4, 2 * B4])
                    pS = ps_in(st, "l1c_pS", [P, 2, 512])
                    pX = ps_in(st, "l1c_pX", [P, 2, 512])
                    pM = ps_in(st, "l1c_pM", [P, 2, 512])
                    pL = ps_in(st, "l1c_pL", [P, 2, 512])
                    s_z = sem("l1c_zeroed"); s_fr = sem("l1c_sfree"); s_ld = [sem(f"l1c_ld{u}") for u in range(2)]
                    s_S = sem("l1c_S"); s_d = sem("l1c_sums"); s_v = sem("l1c_var"); s_sd = sem("l1c_dev")
                    s_rows = [sem(f"l1c_rows{u}") for u in range(2)]; s_rf = sem("l1c_ringfree")
                    s_i = sem("l1c_idx"); s_go = sem("l1c_go")
                    s_ab = sem("l1c_ab"); s_t = sem("l1c_t"); s_tc = sem("l1c_tc")
                    s_m = sem("l1c_m"); s_sum = sem("l1c_m_biased"); s_lk = sem("l1c_lk")
                    s_l = sem("l1c_l"); s_le = sem("l1c_le")
                    PER = 13

                    def pairs(body):
                        def run(eng):
                            with eng.Fori(0, TN // 2) as i:
                                for u in range(2):
                                    body(eng, i * 2 + u, i, u)
                        return run

                    def pairs_ahead(turn):
                        def run(eng):
                            with eng.Fori(0, TN // 2 - 1) as i:
                                for u in range(2):
                                    turn(eng, i * 2 + u, u, True, True, i)
                            turn(eng, TN - 2, 0, True, False, TN // 2 - 1)
                            turn(eng, TN - 1, 1, False, False, TN // 2 - 1)
                        return run

                    with nc.Block() as block:
                        @block.sync
                        def _(sp):
                            sp.wait_ge(s_z, 1)
                            def body(eng, n, i, u):
                                eng.wait_ge(s_fr, n + 1)
                                eng.dma_start(S[:, u].rearrange("p g j -> p (g j)"),
                                              dstP[bass.ds(n * B4 * P, B4 * P)].rearrange("(a n) -> a n", a=1)
                                              .broadcast_to([P, B4 * P])).then_inc(s_ld[u], 16)
                                for k, row in enumerate((0, P - 1)):
                                    eng.dma_start(C[row:row + 1, u, :, :],
                                                  CAd[k:k + 1, bass.ds(n * B4, B4), 0:D]).then_inc(s_ld[u], 16)
                            pairs(body)(sp)

                        @block.vector
                        def _(dve):
                            step = Steps(dve, "l1c_dve")
                            dve.sem_inc(s_fr, 2)
                            step(dve.memset(C[:, :, :, :], 0.0))
                            dve.sem_inc(s_z, 1)
                            def operands(eng, part, n, i, u):
                                t_ = bass.ds(n * B4, B4)
                                ab = AB[:, u].rearrange("p k j e -> p (k j) e")[:, :, 0:D]
                                sq = AB[:, u].rearrange("p k j e -> p (k j) e")[:, :, D:P]
                                if part == 0:
                                    eng.wait_ge(s_ld[u], i * 48 + 48)
                                    eng.tensor_tensor(S[:, u], S[:, u], bc(dstF[:, t_], 2, [P, B4, P]),
                                                      ALU.is_equal).then_inc(s_S, 1)
                                    eng.wait_ge(s_rows[u], i * (16 * B4) + 16 * B4)
                                    step(eng.tensor_scalar(XS[:, t_, :], ring[:, u], 1.0, None, ALU.mult))
                                    eng.sem_inc(s_rf, 1)
                                    for k, X in enumerate((XS, XD)):
                                        step(eng.tensor_reduce(s4[:, 0, k * B4:(k + 1) * B4], X[:, t_, :], AX.X, ALU.add))
                                if part == 1:
                                    eng.wait_ge(s_tc, n * 2 + 2)
                                    step(eng.tensor_scalar(s4[:, 1, :], s4[:, 0, :], -1.0 / D, None, ALU.mult))
                                    for k, X in enumerate((XS, XD)):
                                        step(eng.tensor_tensor(AB[:, u, k, :, 0:D], X[:, t_, :],
                                                               bc(s4[:, 1, k * B4:(k + 1) * B4], 2, [P, B4, D]), ALU.add))
                                if part == 2:
                                    step(eng.tensor_tensor(sq, ab, ab, ALU.mult))
                                    step(eng.tensor_reduce(s4[:, 2, :], sq, AX.X, ALU.add))
                                    eng.sem_inc(s_v, 1)
                                if part == 3:
                                    step(eng.tensor_scalar(AB[:, u, 0, :, D:P], M[:, t_, 0:D], 1.0, None, ALU.mult))
                                if part == 4:
                                    eng.wait_ge(s_d, n + 1)
                                    eng.sem_inc(s_fr, 1)
                                    step(eng.tensor_tensor(AB[:, u, 1, :, D:P],
                                                           pS[:, u, 0:B4 * D].rearrange("p (g d) -> p g d", d=D),
                                                           bc(RC[:, t_], 2, [P, B4, D]), ALU.mult))
                                    eng.wait_ge(s_sd, n + 1)
                                    step(eng.reciprocal(s4[:, 0, :], s4[:, 3, :]))
                                if part == 5:
                                    step(eng.scalar_tensor_tensor(ab, ab, 0.0, bc(s4[:, 0, :], 2, [P, 2 * B4, D]),
                                                                  ALU.max, ALU.mult))
                                    eng.sem_inc(s_ab, 1)
                                    step(eng.tensor_scalar(M[:, t_, 0:D], AB[:, u, 0, :, 0:D], 1.0, None, ALU.mult))

                            def turn(eng, n, u, next_, second, i):
                                if second:
                                    step.chunk(n + 2, PER, 1)
                                for kf in range(6):
                                    z = min(P, HC - kf % 3 * P)
                                    m = LK[0:z, kf % 3, :]
                                    eng.wait_ge(s_sum, n * 6 + kf + 1)
                                    eng.scalar_tensor_tensor(m, m, 0.2, m, ALU.mult, ALU.max).then_inc(s_lk, 1)
                                    if second:
                                        operands(eng, kf, n + 2, i + 1, u)
                                if second:
                                    step.end()
                            for n in range(2):
                                for part in range(6):
                                    operands(dve, part, n, 0, n)
                            pairs_ahead(turn)(dve)

                        @block.tensor
                        def _(pe):
                            def sums(eng, n, u):
                                eng.wait_ge(s_S, n + 1)
                                for j in range(B4):
                                    to = pS[:, u, j * D:(j + 1) * D]
                                    eng.matmul(to, S[:, u, j, :],
                                               M[:, bass.ds(n * B4 + j, 1), 0:D].rearrange("p a d -> p (a d)"),
                                               start=True, stop=False)
                                    last = eng.matmul(to, S[:, u, j, :], C[:, u, j, :], start=False, stop=True)
                                last.then_inc(s_d, 1)

                            def transposes(eng, n, u):
                                eng.wait_ge(s_ab, n + 1)
                                for k in range(2):
                                    eng.wait_ge(s_tc, n * 2 + 3 + k)
                                    for j in range(B4):
                                        last = eng.transpose(pX[:, k, j * P:(j + 1) * P], AB[:, u, k, j, :],
                                                             ident[:, :])
                                    last.then_inc(s_t, 1)

                            def product(eng, n, u, kf):
                                k, f = kf // 3, kf % 3
                                lo, hi = f * P, min(HC, (f + 1) * P)
                                if kf == 0:
                                    eng.wait_ge(s_tc, n * 2 + 6)
                                if kf >= 2:
                                    eng.wait_ge(s_sum, n * 6 + kf - 1)
                                to = pM[0:hi - lo, kf % 2, :]
                                rA = ABT[:, u, 0].rearrange("p j e -> p (j e)")
                                rB = ABT[:, u, 1].rearrange("p j e -> p (j e)")
                                if k == 0:
                                    eng.matmul(to, WA[:, lo:hi], rA, start=True, stop=False)
                                    last = eng.matmul(to, WBr[:, lo:hi], rB[0:D, :], start=False, stop=True)
                                else:
                                    last = eng.matmul(to, WS[:, lo:hi], rB, start=True, stop=True)
                                last.then_inc(s_m, 1)

                            def dots(eng, n, u, kf):
                                k, f = kf // 3, kf % 3
                                z = min(P, HC - f * P)
                                eng.wait_ge(s_lk, n * 6 + kf + 1)
                                if kf == 0:
                                    eng.wait_ge(s_le, n + 1)
                                for j in range(B4):
                                    to = pL[:, u, (k * B4 + j) * H:(k * B4 + j + 1) * H]
                                    last = eng.matmul(to, LK[0:z, f, j * P:(j + 1) * P], attC[0:z, f, :],
                                                      start=kf + j == 0, stop=kf == 5 and j == B4 - 1,
                                                      skip_group_check=True)
                                last.then_inc(s_l, 1)

                            def turn(eng, n, u, next_, second, i):
                                for kf in range(6):
                                    if kf == 3:
                                        if next_:
                                            transposes(eng, n + 1, 1 - u)
                                        if second:
                                            sums(eng, n + 2, u)
                                    product(eng, n, u, kf)
                                    if kf >= 2:
                                        dots(eng, n, u, kf - 2)
                                dots(eng, n, u, 4)
                                dots(eng, n, u, 5)
                            sums(pe, 0, 0)
                            sums(pe, 1, 1)
                            transposes(pe, 0, 0)
                            pairs_ahead(turn)(pe)

                        @block.gpsimd
                        def _(pool):
                            last_row = pool.to_reg(NT * P - 1)
                            pool.sem_inc(s_rf, 2)
                            def body(eng, n, i, u):
                                eng.wait_ge(s_rf, n + 1)
                                eng.tensor_copy(idx[:, u, :], riI[:, bass.ds(n * B4, B4)])
                                eng.tensor_copy(ring[:, u], XS[:, bass.ds(n * B4, B4), :]).then_inc(s_i, 1)
                                eng.wait_ge(s_i, n + 1)
                                eng.sem_inc(s_go, 1)
                                for j in range(B4):
                                    eng.indirect_dma_start(
                                        out=ring[:, u, j, :], out_offset=None, in_=T1,
                                        in_offset=bass.IndirectOffsetOnAxis(ap=idx[:, u, j:j + 1], axis=0),
                                        bounds_check=last_row, oob_is_err=False).then_inc(s_rows[u], 16)
                            pairs(body)(pool)

                        @block.scalar
                        def _(act):
                            act.sem_inc(s_tc, 4)
                            act.sem_inc(s_le, 2)

                            def root(eng, n):
                                eng.wait_ge(s_v, n + 1)
                                eng.activation(s4[:, 3, :], s4[:, 2, :], ACT.Sqrt, bias=eps[:, 0:1],
                                               scale=1.0 / D).then_inc(s_sd, 1)

                            def copies(eng, n, u):
                                for k in range(2):
                                    eng.wait_ge(s_t, n * 2 + k + 1)
                                    eng.activation(ABT[:, u, k].rearrange("p j e -> p (j e)"), pX[:, k, :],
                                                   ACT.Copy).then_inc(s_tc, 1)

                            def turn(eng, n, u, next_, second, i):
                                for kf in range(6):
                                    if kf == 3 and next_:
                                        copies(eng, n + 1, 1 - u)
                                    f = kf % 3
                                    z = min(P, HC - f * P)
                                    eng.wait_ge(s_m, n * 6 + kf + 1)
                                    if kf >= 3:
                                        eng.wait_ge(s_l, n * 6 + kf - 2)
                                    eng.activation(LK[0:z, f, :], pM[0:z, kf % 2, :], ACT.Identity,
                                                   bias=mb[0:z, f:f + 1]).then_inc(s_sum, 1)
                                    if kf == 3 and second:
                                        root(eng, n + 2)
                                eng.wait_ge(s_l, n * 6 + 6)
                                eng.activation(LG[:, :, bass.ds(n * B4, B4), :],
                                               pL[:, u, 0:2 * B4 * H].rearrange("p (k g h) -> p k g h", k=2, h=H),
                                               ACT.Copy).then_inc(s_le, 1)

                            root(act, 0)
                            root(act, 1)
                            copies(act, 0, 0)
                            pairs_ahead(turn)(act)

            logits()

            NR = 25 * H
            NA = NT // 25

            def softmax():
                st = phase()
                with st:
                    t = lambda name, shape, dt=f32: sb_in(st, name, shape, dt)
                    room = M[0:NR, :, :].rearrange("p t d -> p (t d)")
                    part = lambda a, n: room[:, a * NA * P:(a + n) * NA * P].rearrange(
                        "p (n a j) -> p n a j", n=n, j=P)
                    L = part(0, 3)
                    same = part(3, 2)
                    isF0 = part(5, 1)[:, 0]
                    Aall = t("sm_A", [P, 3, NA, P])
                    A = Aall[0:NR]
                    d5 = Aall[:, 2].rearrange("p a j -> p (a j)")[:, 0:NT * H].rearrange("p (t h) -> p t h", h=H)
                    ends = t("sm_ends", [NR, 2, NA])
                    car = t("sm_car", [NR, 2, NA])
                    e5 = t("sm_e5", [H, 2, NT]); c5 = t("sm_c5", [H, 2, NT])
                    m0 = t("sm_m0", [H, NT]); one = t("sm_one", [H, NT]); m1 = t("sm_m1", [H, NT])
                    m1b = t("sm_m1b", [H, NT])
                    u5 = t("sm_u5", [H, NT]); b5 = t("sm_b5", [H, NT])
                    pL = ps_in(st, "sm_pL", [P, 6, 512])
                    kFr = t("sm_kF", [H, NT]); kLr = t("sm_kL", [H, NT])
                    s_k = sem("sm_keys"); s_sp = sem("sm_spill"); s_d = sem("sm_d5"); s_t = sem("sm_t"); s_en = sem("sm_ends"); s_e5 = sem("sm_e5")
                    s_c5 = sem("sm_c5"); s_car = sem("sm_car"); s_o = sem("sm_o"); s_o2 = sem("sm_o2")
                    s_x = sem("sm_x"); s_z = sem("sm_z"); s_al = sem("sm_al"); s_alT = sem("sm_alT")
                    flat = lambda a: a.rearrange("p a j -> p (a j)")
                    with nc.Block() as block:
                        @block.tensor
                        def _(pe):
                            pe.wait_ge(s_d, 1)
                            for n in range(3):
                                of = d5 if n == 2 else LG[:, n]
                                for a in range(NA):
                                    last = pe.transpose(pL[0:NR, 2 * n + a // 4, (a % 4) * P:(a % 4 + 1) * P],
                                                        of[:, 25 * a:25 * (a + 1), :].rearrange("p t h -> p (t h)"),
                                                        ident[:, :])
                            last.then_inc(s_t, 1)
                            pe.wait_ge(s_al, 1)
                            for n in range(2):
                                for a in range(NA):
                                    last = pe.transpose(pL[:, 2 * n + a // 4, (a % 4) * P:(a % 4) * P + NR],
                                                        A[:, n, a, :], ident[0:NR, 0:NR])
                            last.then_inc(s_alT, 1)

                        @block.sync
                        def _(sp):
                            sp.dma_start(Msp, M[:, 0:SPT, :]).then_inc(s_sp, 16)
                            keys = dstP.rearrange("(a t j) -> a t j", a=1, j=P)
                            rows_of = lambda v: v.rearrange("(a p) -> p a", a=NA)
                            heads_of = lambda v: v.rearrange("(t h) -> h t", h=H)
                            with nc.allow_non_contiguous_dma(reason="a few values of each tile"):
                                for to, end in ((kFr, 0), (kLr, P - 1)):
                                    sp.dma_start(to[:, :], keys[:, :, end].broadcast_to([H, NT])).then_inc(s_k, 16)
                                for k in range(2):
                                    sp.wait_ge(s_en, k + 1)
                                    for e_ in range(2):
                                        sp.dma_start(rows_of(SMd[e_]), ends[:, e_, :]).then_inc(s_o, 16)
                                    sp.wait_ge(s_o, 32 * (k + 1))
                                    for e_ in range(2):
                                        sp.dma_start(e5[:, e_, :], heads_of(SMd[e_])).then_inc(s_e5, 16)
                                    sp.wait_ge(s_c5, k + 1)
                                    for e_ in range(2):
                                        sp.dma_start(heads_of(SCd[e_]), c5[:, e_, :]).then_inc(s_o2, 16)
                                    sp.wait_ge(s_o2, 32 * (k + 1))
                                    for e_ in range(2):
                                        sp.dma_start(car[:, e_, :], rows_of(SCd[e_])).then_inc(s_car, 16)
                            sp.wait_ge(s_al, 1)
                            sp.dma_start(M[:, 0:SPT, :], Msp).then_inc(s_sp, 16)
                            sp.wait_ge(s_sp, 32)

                        @block.scalar
                        def _(act):
                            act.wait_ge(s_x, 1)
                            act.activation(A[:, 0:2].rearrange("p n a j -> p (n a j)"),
                                           L[:, 0:2].rearrange("p n a j -> p (n a j)"), ACT.Exp).then_inc(s_z, 1)

                        @block.vector
                        def _(dve):
                            step = Steps(dve, "sm_dve")
                            tt = lambda o, a, b, op: step(dve.tensor_tensor(o, a, b, op))
                            ts = lambda o, a, s1, s2, o1, o2=None: step(
                                dve.tensor_scalar(o, a, s1, s2, o1, o2) if o2 is not None else
                                dve.tensor_scalar(o, a, s1, s2, o1))
                            scan = lambda o, a, b, i0, o1, o2: step(dve.tensor_tensor_scan(o, a, b, i0, o1, o2))
                            dve.wait_ge(s_sp, 16)
                            step(dve.tensor_copy(d5[:, :, :], bc(dstF[:, :], 2, [P, NT, H])))
                            dve.sem_inc(s_d, 1)
                            dve.wait_ge(s_t, 1)
                            for n in range(3):
                                step(dve.tensor_copy(flat(L[:, n]), pL[0:NR, 2 * n:2 * n + 2, :].rearrange("p b j -> p (b j)")))
                            DR = L[:, 2]
                            dve.memset(same[:, 0, :, 0:1], 0.0)
                            dve.memset(same[:, 1, :, P - 1:P], 0.0)
                            tt(same[:, 0, :, 1:P], DR[:, :, 1:P], DR[:, :, 0:P - 1], ALU.is_equal)
                            tt(same[:, 1, :, 0:P - 1], DR[:, :, 1:P], DR[:, :, 0:P - 1], ALU.is_equal)
                            tt(isF0, DR, DR[:, :, 0:1].broadcast_to([NR, NA, P]), ALU.is_equal)
                            step(dve.tensor_copy(ends[:, 0, :], DR[:, :, P - 1]))
                            tt(DR, DR, bc(ends[:, 0, :], 2, [NR, NA, P]), ALU.is_equal)
                            isF = (isF0, DR)
                            dve.wait_ge(s_k, 32)
                            dve.memset(m0[:, 0:1], 0.0)
                            dve.memset(m1[:, 0:1], 0.0)
                            dve.memset(m1b[:, NT - 1:NT], 0.0)
                            tt(m0[:, 1:NT], kFr[0:H, 1:NT], kLr[0:H, 0:NT - 1], ALU.is_equal)
                            tt(one[:, :], kFr[0:H, :], kLr[0:H, :], ALU.is_equal)
                            tt(m1[:, 1:NT], m0[:, 1:NT], one[:, 0:NT - 1], ALU.mult)
                            tt(m1b[:, 0:NT - 1], m0[:, 1:NT], one[:, 1:NT], ALU.mult)

                            def backwards(o, f, mask):
                                ts(o, mask, -1.0, 1.0, ALU.mult, ALU.add)
                                tt(f, o, f, ALU.mult)
                                scan(flat(o)[:, ::-1], flat(mask)[:, ::-1], flat(f)[:, ::-1], 0.0,
                                     ALU.mult, ALU.add)

                            def across(k, op, off):
                                dve.sem_inc(s_en, 1)
                                dve.wait_ge(s_e5, 32 * (k + 1))
                                if k == 1:
                                    dve.wait_ge(s_o2, 32)
                                for e_ in range(2):
                                    step(dve.memset(u5[:, :], off))
                                    a, b = (slice(1, NT), slice(0, NT - 1)) if e_ == 0 else (slice(0, NT - 1), slice(1, NT))
                                    keep = (m1 if e_ == 0 else m1b)
                                    val = e5[:, 1 - e_, b]
                                    if off:
                                        ts(b5[:, a], m0[:, 1:NT], BIG, -BIG, ALU.mult, ALU.add)
                                        tt(u5[:, a], b5[:, a], val, ALU.add)
                                        ts(b5[:, :], keep[:, :], BIG, -BIG, ALU.mult, ALU.add)
                                    else:
                                        tt(u5[:, a], m0[:, 1:NT], val, ALU.mult)
                                        step(dve.tensor_copy(b5[:, :], keep[:, :]))
                                    r = slice(None, None, 1 if e_ == 0 else -1)
                                    scan(c5[:, e_, r], b5[:, r], u5[:, r], off, ALU.add if off else ALU.mult, op)
                                dve.sem_inc(s_c5, 1)
                                dve.wait_ge(s_car, 32 * (k + 1))

                            ts(A[:, 0], same[:, 0], BIG, -BIG, ALU.mult, ALU.add)
                            scan(flat(A[:, 1]), flat(A[:, 0]), flat(L[:, 0]), -BIG, ALU.add, ALU.max)
                            backwards(A[:, 2], A[:, 1], same[:, 1])
                            step(dve.tensor_copy(ends[:, 0, :], A[:, 2, :, 0]))
                            step(dve.tensor_copy(ends[:, 1, :], A[:, 2, :, P - 1]))
                            across(0, ALU.max, -BIG)
                            for e_ in range(2):
                                ts(A[:, 0], isF[e_], BIG, -BIG, ALU.mult, ALU.add)
                                tt(A[:, 0], A[:, 0], bc(car[:, e_, :], 2, [NR, NA, P]), ALU.add)
                                tt(A[:, 2], A[:, 2], A[:, 0], ALU.max)
                            tt(A[:, 2], A[:, 2], L[:, 1], ALU.max)
                            tt(L[:, 0], L[:, 0], A[:, 2], ALU.subtract)
                            tt(L[:, 1], L[:, 1], A[:, 2], ALU.subtract)
                            dve.sem_inc(s_x, 1)
                            dve.wait_ge(s_z, 1)
                            scan(flat(A[:, 2]), flat(same[:, 0]), flat(A[:, 0]), 0.0, ALU.mult, ALU.add)
                            backwards(L[:, 0], A[:, 2], same[:, 1])
                            step(dve.tensor_copy(ends[:, 0, :], L[:, 0, :, 0]))
                            step(dve.tensor_copy(ends[:, 1, :], L[:, 0, :, P - 1]))
                            across(1, ALU.add, 0.0)
                            for e_ in range(2):
                                tt(A[:, 2], isF[e_], bc(car[:, e_, :], 2, [NR, NA, P]), ALU.mult)
                                tt(L[:, 0], L[:, 0], A[:, 2], ALU.add)
                            tt(L[:, 0], L[:, 0], A[:, 1], ALU.add)
                            step(dve.reciprocal(L[:, 1], L[:, 0]))
                            ts(L[:, 1], L[:, 1], 1.0 / H, None, ALU.mult)
                            tt(A[:, 0], A[:, 0], L[:, 1], ALU.mult)
                            tt(A[:, 1], A[:, 1], L[:, 1], ALU.mult)
                            dve.sem_inc(s_al, 1)
                            dve.wait_ge(s_alT, 1)
                            for n in range(2):
                                for b in range(2):
                                    to = LG[:, n, 100 * b:100 * (b + 1), :].rearrange("p (a t) h -> p a (t h)", a=4)
                                    of = pL[:, 2 * n + b, :].rearrange("p (a r) -> p a r", a=4)[:, :, 0:NR]
                                    step(dve.tensor_copy(to, of))
                            tt(LG[:, 1], LG[:, 1], bc(repF[:, :], 2, [P, NT, H]), ALU.mult)

            softmax()

            def weighted():
                st = phase()
                with st:
                    nm = norm_setup(st, "l1e_nm", G)
                    e = ends_setup(st, "l1e_en")
                    hd = sb_in(st, "l1e_hd", [P, 2, G, D])
                    Gs = sb_in(st, "l1e_G", [P, 2, 2, H, D])
                    Gd = sb_in(st, "l1e_Gd", [P, 2, 2, H, D])
                    GT = sb_in(st, "l1e_GT", [P, 2, 3, P])
                    pG = ps_in(st, "l1e_pG", [P, 2, 512])
                    pC = ps_in(st, "l1e_pC", [P, 512])
                    s_hd = sem("l1e_hd"); s_g = sem("l1e_g"); s_gd = sem("l1e_gd"); s_ge = sem("l1e_ge")
                    s_gf = sem("l1e_gf"); s_t = sem("l1e_t"); s_te = sem("l1e_te"); s_c = sem("l1e_c")
                    s_ce = sem("l1e_ce")

                    def last_chunk(i, u):
                        return (i, 0) if u else (i - 1, 1)

                    with nc.Block() as block:
                        @block.vector
                        def _(dve):
                            step = Steps(dve, "l1e_dve")
                            def h_dst(eng, part, i, u):
                                c = i * 2 + u
                                if part == 0:
                                    step.chunk(c, NORM_STEPS + 1)
                                norm_part(eng, step, part, nm_, XD[:, bass.ds(c * G, G), :], hd[:, u], c)
                                if part == 2:
                                    eng.sem_inc(s_hd, 1)
                                    step.end()

                            def heads(eng, i, u, ahead=True):
                                c = i * 2 + u
                                for hf in range(4):
                                    n = c * 4 + hf
                                    eng.wait_ge(s_gf, n + 1)
                                    for j in range(2):
                                        t_ = c * G + hf * 2 + j
                                        last = eng.tensor_tensor(
                                            Gs[:, hf % 2, j, :, :], M[:, bass.ds(t_, 1), 0:D].broadcast_to([P, H, D]),
                                            LG[:, 0, bass.ds(t_, 1), :].rearrange("p a h -> p h a").broadcast_to([P, H, D]),
                                            ALU.mult)
                                    last.then_inc(s_ge, 1)
                                    eng.wait_ge(s_ge, n + 1)
                                    eng.wait_ge(s_gd, n + 1)
                                    eng.tensor_tensor(Gs[:, hf % 2], Gs[:, hf % 2], Gd[:, hf % 2], ALU.add)\
                                        .then_inc(s_g, 1)
                                    if ahead and hf < 3:
                                        h_dst(eng, hf, *((i + 1, 0) if u else (i, 1)))
                            nm_ = dict(nm, xc=nm["xc"][:, :, :], sq=nm["sq"][:, :, :])
                            for part in range(3):
                                h_dst(dve, part, 0, 0)
                            heads(dve, 0, 0)
                            heads(dve, 0, 1)
                            with dve.Fori(1, NCH // 2) as i:
                                heads(dve, i, 0)
                                heads(dve, i, 1)
                            heads(dve, NCH // 2, 0, ahead=False)

                        @block.gpsimd
                        def _(pool):
                            pool.sem_inc(s_g, 2)
                            def body(eng, i, u):
                                c = i * 2 + u
                                eng.wait_ge(s_hd, c + 1)
                                for hf in range(4):
                                    n = c * 4 + hf
                                    eng.wait_ge(s_g, n + 1)
                                    for j in range(2):
                                        t_ = c * G + hf * 2 + j
                                        last = eng.tensor_tensor(
                                            Gd[:, hf % 2, j, :, :],
                                            hd[:, u, hf * 2 + j:hf * 2 + j + 1, :].broadcast_to([P, H, D]),
                                            LG[:, 1, bass.ds(t_, 1), :].rearrange("p a h -> p h a").broadcast_to([P, H, D]),
                                            ALU.mult)
                                    last.then_inc(s_gd, 1)
                            chunks(body)(pool)

                        @block.tensor
                        def _(pe):
                            pe.sem_inc(s_gf, 2)
                            def body(eng, i, u):
                                c = i * 2 + u
                                for j in range(G):
                                    hf, k = j // 2, c * G + j
                                    if j % 2 == 0:
                                        eng.wait_ge(s_g, c * 4 + hf + 3)
                                    if j >= 2:
                                        eng.wait_ge(s_te, k - 1)
                                    for f in range(3):
                                        z = min(2, H - 2 * f)
                                        last = eng.transpose(
                                            pG[0:z * D, j % 2, f * P:(f + 1) * P],
                                            Gs[:, hf % 2, j % 2, 2 * f:2 * f + z, :].rearrange("p h d -> p (h d)"),
                                            ident[:, :])
                                    last.then_inc(s_t, 1)
                                    if j >= 1:
                                        product(eng, c, j - 1)
                                    if j == 2 and not (isinstance(c, int) and c == 0):
                                        ends_pe(eng, *last_chunk(i, u), e, D)
                                product(eng, c, G - 1)

                            def product(eng, c, j):
                                eng.wait_ge(s_te, c * G + j + 1)
                                if j == 0:
                                    wait_past(eng, s_ce, c)
                                for f in range(3):
                                    z = min(P, HC - f * P)
                                    last = eng.matmul(pC[:, j * D:(j + 1) * D], GT[0:z, j % 2, f, :], WlS[0:z, f, :],
                                                      start=f == 0, stop=f == 2)
                                    if f == 0 and j % 2 == 0:
                                        last.then_inc(s_gf, 1)
                                if j == G - 1:
                                    last.then_inc(s_c, 1)
                            chunks(body)(pe)
                            ends_pe(pe, NCH // 2, 0, e, D)

                        @block.scalar
                        def _(act):
                            def body(eng, i, u):
                                c = i * 2 + u
                                ends_act_before(eng, i, u, e)
                                for j in range(G):
                                    k = c * G + j
                                    if j == 4 and not (isinstance(c, int) and c == NCH - 1):
                                        norm_act(eng, nm, w=c + 1)
                                    eng.wait_ge(s_t, k + 1)
                                    eng.activation(GT[:, j % 2, 0:2].rearrange("p f e -> p (f e)"),
                                                   pG[:, j % 2, 0:2 * P], ACT.Copy)
                                    eng.activation(GT[0:D, j % 2, 2, :], pG[0:D, j % 2, 2 * P:3 * P],
                                                   ACT.Copy).then_inc(s_te, 1)
                                    if j == 4 and not (isinstance(c, int) and c == 0):
                                        ends_act(eng, *last_chunk(i, u), e, D)
                                eng.wait_ge(s_c, c + 1)
                                eng.activation(M[:, bass.ds(c * G, G), 0:D],
                                               pC[:, :].rearrange("p (g d) -> p g d", d=D), ACT.Copy).then_inc(s_ce, 1)
                                eng.wait_ge(s_ce, c + 1)
                                eng.sem_inc(e["m"], 1)
                            norm_act(act, nm, w=0)
                            chunks(body)(act)
                            ends_act(act, NCH // 2, 0, e, D)

                        @block.sync
                        def _(sp):
                            chunks(lambda eng, i, u: ends_sp(eng, i, u, e, D))(sp)
                            ends_sp_done(sp, e)

            weighted()
        carries("l1f", D)

        def tails():
            st = phase()
            with st:
                q = tail_setup(st, "l1g_t")
                s = dict(S=sb_in(st, "l1g_S", [P, 2, G, P]),
                         C=sb_in(st, "l1g_C", [P, 2, G, W1]),
                         z=sem("l1g_z"), ld=[sem(f"l1g_ld{u}") for u in range(2)], s=sem("l1g_S"),
                         fr=sem("l1g_fr"))
                s_x = sem("l1g_x"); s_st = sem("l1g_st")

                def next_chunk(i, u):
                    return (i + 1, 0) if u else (i, 1)
                with nc.Block() as block:
                    @block.sync
                    def _(sp):
                        sp.wait_ge(s["z"], 1)
                        chunks(lambda eng, i, u: sums_sp(eng, i, u, s, D))(sp)

                    @block.vector
                    def _(dve):
                        step = Steps(dve, "l1g_dve")
                        dve.sem_inc(s["fr"], 2)
                        dve.sem_inc(q["z_read"], 2)
                        sums_start(dve, step, s)
                        def turn(eng, i, u, k, *flags):
                            w = (i * 2 + u) * 2 + k
                            step.turn(w, TAIL_STEPS - 1, flags[2] and (flags[0] or k == 0))
                            X = (XD, XS)[k]
                            tail_dve(eng, step, q, w, k, flags,
                                     X[:, bass.ds((i * 2 + u) * G, G), :] if flags[0] else None,
                                     X[:, bass.ds((i * 2 + u) * G - G, G), :] if flags[2] else None)
                            if k == 1 and flags[1] and flags[0]:
                                eng.sem_inc(s["fr"], 1)
                            if k == 0 and flags[0] and not (isinstance(i, int) and 2 * i + u == NCH - 1):
                                sums_dve(eng, *next_chunk(i, u), s)
                            if k == 0 and flags[2]:
                                eng.sem_inc(s_x, 1)
                        sums_dve(dve, 0, 0, s)
                        turns(turn)(dve)

                    @block.gpsimd
                    def _(pool):
                        pool.sem_inc(q["xb_used"], 2)
                        def body(eng, i, u):
                            for k, X in enumerate((XD, XS)):
                                w = (i * 2 + u) * 2 + k
                                eng.wait_ge(q["xb_used"], w + 1)
                                eng.tensor_tensor(q["XB"][:, k], X[:, bass.ds((i * 2 + u) * G, G), :],
                                                  bc(cD[:, 0, :], 1, [P, G, D]), ALU.add).then_inc(q["xb_ready"], 1)
                        chunks(body)(pool)

                    @block.scalar
                    def _(act):
                        def turn(eng, i, u, k, *flags):
                            c = i * 2 + u
                            tail_act(eng, q, c * 2 + k, k, flags)
                            if k == 1 and flags[2]:
                                wait_past(eng, s_x, c)
                                eng.dma_start(TY[bass.ds(c * G * P - G * P, G * P), :].rearrange("(g p) d -> p g d", p=P),
                                              XD[:, bass.ds(c * G - G, G), :]).then_inc(s_st, 16)
                        turns(turn)(act)
                        act.wait_ge(s_st, 16 * NCH)

                    @block.tensor
                    def _(pe):
                        def conv(eng, i, u):
                            c = i * 2 + u
                            eng.wait_ge(s["s"], c + 1)
                            eng.matmul(q["py"][:, 0, :], ones3[:, :], bias8(0), start=True, stop=False)
                            for j in range(G):
                                to = q["py"][:, 0, j * D:(j + 1) * D]
                                eng.matmul(to, s["S"][:, u, j, :],
                                           M[:, bass.ds(c * G + j, 1), 0:D].rearrange("p a d -> p (a d)"),
                                           start=False, stop=False)
                                eng.matmul(to, s["S"][:, u, j, :], s["C"][:, u, j, 0:D], start=False, stop=False)

                        def turn(eng, i, u, k, *flags):
                            c = i * 2 + u
                            tail_pe(eng, q, c * 2 + k, k, flags, (BDj, BDc)[k], opened=k == 0)
                            if k == 1 and flags[0] and not (isinstance(i, int) and c == NCH - 1):
                                conv(eng, *next_chunk(i, u))
                        conv(pe, 0, 0)
                        turns(turn)(pe)

        tails()

        columns = source_columns(top, 2)
        srcF, ewF, OD, idY, csI, cdI, srcS, dstS = columns
        move_columns(columns, False)

        def scatter_sums():
            st = phase()
            with st:
                nm = norm_setup(st, "l2a_nm", G)
                S2 = sb_in(st, "l2a_S", [P, 2, G, P])
                m = sb_in(st, "l2a_m", [P, 2, G, D])
                R = sb_in(st, "l2a_R", [P, 2, G, D])
                idx = sb_in(st, "l2a_idx", [P, 2, G], i32)
                pS = ps_in(st, "l2a_pS", [P, 2, 512])
                s_sr = [sem(f"l2a_src{u}") for u in range(2)]; s_sf = sem("l2a_sfree"); s_m = sem("l2a_m")
                s_d = sem("l2a_sums"); s_r = sem("l2a_rows"); s_i = sem("l2a_idx"); s_go = sem("l2a_go")
                s_y = [sem(f"l2a_y{k}") for k in range(NY)]
                PER_Y = 16 * G // NY
                with nc.Block() as block:
                    @block.sync
                    def _(sp):
                        def body(eng, i, u):
                            c = i * 2 + u
                            eng.wait_ge(s_sf, c + 1)
                            eng.dma_start(S2[:, u].rearrange("p g j -> p (g j)"),
                                          srcP[bass.ds(c * G * P, G * P)].rearrange("(a n) -> a n", a=1)
                                          .broadcast_to([P, G * P])).then_inc(s_sr[u], 16)
                        chunks(body)(sp)

                    @block.vector
                    def _(dve):
                        step = Steps(dve, "l2a_dve")
                        def body(eng, i, u):
                            c = i * 2 + u
                            step.chunk(c, NORM_STEPS + 3)
                            norm_dve(eng, step, nm, c, XD[:, bass.ds(c * G, G), :],
                                     lambda xc, r: step(relu_into(eng, m[:, u])(xc, r)), w=c)
                            step(eng.tensor_tensor(m[:, u], m[:, u], bc(ewF[:, bass.ds(c * G, G)], 2, [P, G, D]), ALU.mult))
                            eng.wait_ge(s_sr[u], (i + 1) * 16)
                            step(eng.tensor_tensor(S2[:, u], S2[:, u], bc(srcF[:, bass.ds(c * G, G)], 2, [P, G, P]),
                                                   ALU.is_equal))
                            eng.sem_inc(s_m, 1)
                            step.end()
                        chunks(body)(dve)

                    @block.tensor
                    def _(pe):
                        pe.sem_inc(s_sf, 2)
                        def body(eng, i, u):
                            c = i * 2 + u
                            eng.wait_ge(s_m, c + 1)
                            wait_past(eng, s_go, c)
                            for j in range(G):
                                last = eng.matmul(pS[:, u, j * D:(j + 1) * D], S2[:, u, j, :], m[:, u, j, :],
                                                  start=True, stop=True)
                            last.then_inc(s_d, 1)
                            eng.wait_ge(s_d, c + 1)
                            eng.sem_inc(s_sf, 1)
                        chunks(body)(pe)

                    @block.scalar
                    def _(act):
                        def body(eng, i, u):
                            c = i * 2 + u
                            norm_act(eng, nm, w=c)
                            eng.wait_ge(s_d, c + 1)
                            for k in range(NY):
                                wait_past(eng, s_y[k], i * (2 * PER_Y))
                            eng.activation(R[:, u], pS[:, u, :].rearrange("p (g d) -> p g d", d=D),
                                           ACT.Copy).then_inc(s_go, 1)
                        chunks(body)(act)

                    @block.gpsimd
                    def _(pool):
                        def body(eng, i, u):
                            c = i * 2 + u
                            for k in range(NY):
                                wait_past(eng, s_y[k], i * (2 * PER_Y))
                            eng.tensor_copy(idx[:, u, :], idY[:, bass.ds(c * G, G)]).then_inc(s_i, 1)
                            eng.wait_ge(s_i, c + 1)
                            eng.wait_ge(s_go, c + 1)
                            for j in range(G):
                                k = j % NY
                                wait_past(eng, s_y[k], c * PER_Y + j // NY * 16)
                                eng.sem_inc(s_r, 1)
                                eng.indirect_dma_start(
                                    out=Yk[k], out_offset=bass.IndirectOffsetOnAxis(ap=idx[:, u, j:j + 1], axis=0),
                                    in_=R[:, u, j, :], in_offset=None, compute_op=ALU.add).then_inc(s_y[k], 16)
                        chunks(body)(pool)
                        for k in range(NY):
                            pool.wait_ge(s_y[k], PER_Y * NCH)

        scatter_sums()

        def combine():
            with phase(), nc.Block() as block:
                s_a = sem("cb_add"); s_o = sem("cb_out")
                part = M[:, :, :].rearrange("p t d -> p (t d)")[:, 0:YR // P * D]

                @block.gpsimd
                def _(pool):
                    for k in range(NY):
                        of = Yk[k].rearrange("(p r) d -> p (r d)", p=P)
                        if k == 0:
                            pool.dma_start(part, of, max_dma_last_dim=8192).then_inc(s_a, 16)
                        else:
                            pool.dma_start(part, of, accum_op=ALU.add, max_dma_last_dim=8192).then_inc(s_a, 16)
                        pool.wait_ge(s_a, 16 * (k + 1))
                    pool.dma_start(TY[NT * P:NT * P + YR].rearrange("(p r) d -> p (r d)", p=P), part).then_inc(s_o, 16)
                    pool.wait_ge(s_o, 16)

        combine()

        def degrees():
            with phase(), nc.Block() as block:
                s_a, s_b = sem("dg_a"), sem("dg_b")

                @block.scalar
                def _(act):
                    act.activation(RC[:, :], RC[:, :], ACT.Sqrt).then_inc(s_a, 1)
                    act.activation(OD[:, :], OD[:, :], ACT.Sqrt).then_inc(s_a, 1)

                @block.vector
                def _(dve):
                    dve.wait_ge(s_a, 2)
                    dve.reciprocal(OD[:, :], OD[:, :]).then_inc(s_b, 1)

        degrees()
        LH = G // 2

        def add_dst():
            st = phase()
            with st:
                ring = sb_in(st, "l2d_ring", [P, 2, G, D])
                idx = sb_in(st, "l2d_idx", [P, 2, G], i32)
                zero = sb_in(st, "l2d_zero", [P, D])
                s_rows = [sem(f"l2d_rows{u}") for u in range(2)]; s_z = sem("l2d_zeroed")
                s_free = sem("l2d_free"); s_fill = sem("l2d_filled"); s_i = sem("l2d_idx")
                s_go = sem("l2d_go"); s_x = sem("l2d_x"); s_st = sem("l2d_stored")
                with nc.Block() as block:
                    @block.gpsimd
                    def _(pool):
                        last_row = pool.to_reg(NT * P + YR - 1)
                        def body(eng, i, u):
                            c = i * 2 + u
                            eng.wait_ge(s_fill, c + 1)
                            eng.tensor_copy(idx[:, u, :], cdI[:, bass.ds(c * G, G)]).then_inc(s_i, 1)
                            eng.wait_ge(s_i, c + 1)
                            eng.sem_inc(s_go, 1)
                            for j in range(G):
                                eng.indirect_dma_start(
                                    out=ring[:, u, j, :], out_offset=None, in_=TY,
                                    in_offset=bass.IndirectOffsetOnAxis(ap=idx[:, u, j:j + 1], axis=0),
                                    bounds_check=last_row, oob_is_err=False).then_inc(s_rows[u], 16)
                        chunks(body)(pool)

                    @block.vector
                    def _(dve):
                        dve.sem_inc(s_free, 2)
                        dve.memset(zero[:, :], 0.0).then_inc(s_z, 1)
                        def body(eng, i, u):
                            c = i * 2 + u
                            eng.wait_ge(s_rows[u], (i + 1) * (16 * G))
                            xd = XD[:, bass.ds(c * G, G), :]
                            eng.tensor_tensor(xd, xd, ring[:, u], ALU.add).then_inc(s_x, 1)
                            eng.wait_ge(s_x, c + 1)
                            eng.sem_inc(s_free, 1)
                        chunks(body)(dve)

                    @block.scalar
                    def _(act):
                        act.wait_ge(s_z, 1)
                        def body(eng, i, u):
                            eng.wait_ge(s_free, i * 2 + u + 1)
                            eng.activation(ring[:, u], bc(zero[:, :], 1, [P, G, D]), ACT.Copy).then_inc(s_fill, 1)
                        chunks(body)(act)

                    @block.sync
                    def _(sp):
                        def body(eng, i, u):
                            c = i * 2 + u
                            eng.wait_ge(s_x, c + 1)
                            eng.dma_start(TY[bass.ds(c * G * P, G * P), :].rearrange("(g p) d -> p g d", p=P),
                                          XD[:, bass.ds(c * G, G), :]).then_inc(s_st, 16)
                        chunks(body)(sp)
                        sp.wait_ge(s_st, 16 * NCH)

        add_dst()

        def add_rows():
            st = phase()
            with st:
                ring = sb_in(st, "l3a_ring", [P, 2, G, D])
                idx = sb_in(st, "l3a_idx", [P, 2, 2, G], i32)
                R = sb_in(st, "l3a_R", [P, 2, LH, D])
                nm = norm_setup(st, "l3a_nm", G)
                q = ends_setup(st, "l3a_en")
                s_rows = [sem(f"l3a_rows{u}") for u in range(2)]
                s_free = sem("l3a_free"); s_i = sem("l3a_idx"); s_go = sem("l3a_go"); s_r = sem("l3a_r")
                s_sc = sem("l3a_written"); s_rf = sem("l3a_rfree")
                with nc.Block() as block:
                    @block.gpsimd
                    def _(pool):
                        last_row = pool.to_reg(NT * P + YR - 1)
                        last_node = pool.to_reg(N - 1)

                        def turn(c, u, gather=True, write=True):
                            t_, tw = bass.ds(c * G, G), bass.ds(c * G - 2 * G, G)
                            if gather:
                                pool.wait_ge(s_free, c + 1)
                                last = pool.tensor_copy(idx[:, u, 0, :], csI[:, t_])
                            if write:
                                pool.wait_ge(s_r, c - 1)
                                last = pool.tensor_copy(idx[:, u, 1, :], srcS[:, tw])
                            last.then_inc(s_i, 1)
                            pool.wait_ge(s_i, c + 1)
                            if gather:
                                pool.sem_inc(s_go, 1)
                            for j in range(G):
                                if gather:
                                    pool.indirect_dma_start(
                                        out=ring[:, u, j, :], out_offset=None, in_=TY,
                                        in_offset=bass.IndirectOffsetOnAxis(ap=idx[:, u, 0, j:j + 1], axis=0),
                                        bounds_check=last_row, oob_is_err=False).then_inc(s_rows[u], 16)
                                if write and j % 2:
                                    n = j // 2
                                    if n or not isinstance(c, int) or c > 2:
                                        pool.wait_ge(s_sc, c * (16 * LH) + (16 * n - 32 * LH))
                                        if n == 0:
                                            pool.sem_inc(s_rf, 1)
                                    pool.sem_inc(s_go, 1)
                                    pool.indirect_dma_start(
                                        out=out, out_offset=bass.IndirectOffsetOnAxis(ap=idx[:, u, 1, n:n + 1], axis=0),
                                        in_=R[:, u, n, :], in_offset=None, bounds_check=last_node,
                                        oob_is_err=False).then_inc(s_sc, 16)
                        turn(0, 0, write=False)
                        turn(1, 1, write=False)
                        turn(2, 0)
                        turn(3, 1)
                        with pool.Fori(2, NCH // 2) as i:
                            for u in range(2):
                                turn(i * 2 + u, u)
                        turn(NCH - 1, 0)
                        turn(NCH, 1, gather=False)
                        turn(NCH + 1, 0, gather=False)
                        pool.wait_ge(s_sc, 16 * LH * NCH)

                    @block.vector
                    def _(dve):
                        step = Steps(dve, "l3a_dve")
                        dve.sem_inc(s_rf, 2)
                        dve.sem_inc(s_free, 2)
                        def body(eng, i, u):
                            c = i * 2 + u
                            t_ = bass.ds(c * G, G)
                            xs = XS[:, t_, :]
                            step.chunk(c, NORM_STEPS + 5)
                            step(eng.tensor_tensor(xs, xs, bc(RCM[:, t_], 2, [P, G, D]), ALU.mult))
                            eng.wait_ge(s_rows[u], (i + 1) * (16 * G))
                            step(eng.tensor_tensor(xs, xs, ring[:, u], ALU.add))
                            eng.sem_inc(s_free, 1)
                            eng.wait_ge(s_rf, c + 1)
                            step(eng.tensor_tensor(R[:, u], XS[:, bass.ds(c * G, LH), :],
                                                   bc(cD[:, 2, :], 1, [P, LH, D]), ALU.add))
                            eng.sem_inc(s_r, 1)
                            to = M[:, t_, 0:D]
                            norm_dve(eng, step, nm, c, xs, lambda xc, r: step(relu_into(eng, to)(xc, r)), w=c)
                            step(eng.tensor_tensor(to, to, bc(OD[:, t_], 2, [P, G, D]), ALU.mult))
                            eng.sem_inc(q["m"], 1)
                            step.end()
                        chunks(body)(dve)

                    @block.scalar
                    def _(act):
                        def root(eng, i, u):
                            ends_act_before(eng, i, u, q)
                            norm_act(eng, nm, w=i * 2 + u)
                        chunks_ahead(root, lambda eng, i, u: ends_act(eng, i, u, q, D))(act)

                    @block.tensor
                    def _(pe):
                        chunks(lambda eng, i, u: ends_pe(eng, i, u, q, D))(pe)

                    @block.sync
                    def _(sp):
                        chunks(lambda eng, i, u: ends_sp(eng, i, u, q, D))(sp)
                        ends_sp_done(sp, q)

        add_rows()
        carries("l3b", D)

        def last_layer():
            st = phase()
            with st:
                q = sums_setup(st, "l3c_s")
                a = sb_in(st, "l3c_a", [P, G, D])
                aT = sb_in(st, "l3c_aT", [P, 4 * P])
                R = sb_in(st, "l3c_R", [P, 2, G, D])
                idx = sb_in(st, "l3c_idx", [P, 2, G], i32)
                RL = sb_in(st, "l3c_RL", [P, 2, G - LH, D])
                idxL = sb_in(st, "l3c_idxL", [P, 2, G - LH], i32)
                s_ln = sem("l3c_lone")
                pT = ps_in(st, "l3c_pT", [P, 512]); pY = ps_in(st, "l3c_pY", [P, 2, 512])
                s_a = sem("l3c_a"); s_t = sem("l3c_t"); s_tc = sem("l3c_tc"); s_y = sem("l3c_y"); s_re = sem("l3c_relu")
                s_r = sem("l3c_r"); s_i = sem("l3c_i"); s_go = sem("l3c_go"); s_sc = [sem(f"l3c_sc{u}") for u in range(2)]
                with nc.Block() as block:
                    @block.sync
                    def _(sp):
                        sp.wait_ge(q["z"], 1)
                        chunks(lambda eng, i, u: sums_sp(eng, i, u, q, D))(sp)

                    @block.vector
                    def _(dve):
                        step = Steps(dve, "l3c_dve")
                        sums_start(dve, step, q)
                        def mean(eng, i, u):
                            c = i * 2 + u
                            step.chunk(c, 1, 1)
                            eng.wait_ge(q["d"], c + 1)
                            if not isinstance(c, int) or c:
                                wait_past(eng, s_t, c)
                            step(eng.tensor_tensor(v4(a[:, :, :]), sums_view(q, u, D),
                                                   v4(bc(RC[:, bass.ds(c * G, G)], 2, [P, G, D])), ALU.mult))
                            eng.sem_inc(s_a, 1)

                        def result(eng, i, u):
                            c = i * 2 + u
                            eng.wait_ge(s_y, c + 1)
                            if not isinstance(i, int) or i:
                                wait_past(eng, s_sc[u], i * (16 * G))
                            eng.tensor_scalar(R[:, u], pY[:, u, :].rearrange("p (g d) -> p g d", d=D), 0.0, None,
                                              ALU.max).then_inc(s_re, 1)
                            wait_past(eng, s_ln, c * (16 * (G - LH)) - 16 * (G - LH))
                            eng.tensor_tensor(RL[:, u], XS[:, bass.ds(c * G + LH, G - LH), :],
                                              bc(cD[:, 2, :], 1, [P, G - LH, D]), ALU.add)
                            eng.wait_ge(s_re, c + 1)
                            eng.tensor_tensor(R[:, u], R[:, u], XD[:, bass.ds(c * G, G), :], ALU.add).then_inc(s_r, 1)
                        sums_dve(dve, 0, 0, q)
                        sums_dve(dve, 0, 1, q)
                        mean(dve, 0, 0)
                        def turn(i, u):
                            sums_dve(dve, i + 1, u, q)
                            mean(dve, i + u, 1 - u)
                            result(dve, i, u)
                        turn(0, 0)
                        turn(0, 1)
                        with dve.Fori(1, NCH // 2 - 1) as i:
                            turn(i, 0)
                            turn(i, 1)
                        sums_dve(dve, NCH // 2, 0, q)
                        mean(dve, NCH // 2 - 1, 1)
                        result(dve, NCH // 2 - 1, 0)
                        mean(dve, NCH // 2, 0)
                        result(dve, NCH // 2 - 1, 1)
                        result(dve, NCH // 2, 0)

                    @block.scalar
                    def _(act):
                        def body(eng, i, u):
                            c = i * 2 + u
                            eng.wait_ge(s_t, c + 1)
                            eng.activation(aT[:, :], pT[:, :], ACT.Copy).then_inc(s_tc, 1)
                        chunks(body)(act)

                    @block.tensor
                    def _(pe):
                        def body(eng, i, u):
                            c = i * 2 + u
                            eng.wait_ge(s_a, c + 1)
                            for j in range(4):
                                last = eng.transpose(pT[:, j * P:(j + 1) * P],
                                                     a[:, 2 * j:2 * j + 2, :].rearrange("p a d -> p (a d)"), ident[:, :])
                            last.then_inc(s_t, 1)
                            eng.wait_ge(s_tc, c + 1)
                            eng.wait_ge(s_r, c + 1)
                            eng.matmul(pY[:, u, :], ones3[:, :], bias8(2),
                                       start=True, stop=False)
                            for j in range(4):
                                last = eng.matmul(pY[:, u, j * P:(j + 1) * P], aT[:, j * P:(j + 1) * P], BD3[:, :],
                                                  start=False, stop=j == 3)
                            last.then_inc(s_y, 1)
                        pe.sem_inc(s_r, 2)
                        chunks_ahead(lambda eng, i, u: sums_pe(eng, i, u, q, D), body)(pe)

                    @block.gpsimd
                    def _(pool):
                        last_row = pool.to_reg(N - 1)
                        def body(eng, i, u):
                            c = i * 2 + u
                            if not isinstance(i, int) or i:
                                wait_past(eng, s_sc[u], i * (16 * G))
                            wait_past(eng, s_ln, c * (16 * (G - LH)) - 16 * (G - LH))
                            eng.tensor_copy(idxL[:, u, :], srcS[:, bass.ds(c * G + LH, G - LH)])
                            eng.tensor_copy(idx[:, u, :], dstS[:, bass.ds(c * G, G)]).then_inc(s_i, 1)
                            eng.wait_ge(s_i, c + 1)
                            eng.wait_ge(s_r, c + 3)
                            eng.sem_inc(s_go, 1)
                            for j in range(G):
                                eng.indirect_dma_start(
                                    out=out, out_offset=bass.IndirectOffsetOnAxis(ap=idx[:, u, j:j + 1], axis=0),
                                    in_=R[:, u, j, :], in_offset=None, bounds_check=last_row,
                                    oob_is_err=False).then_inc(s_sc[u], 16)
                                if j % 2:
                                    n = j // 2
                                    wait_past(eng, s_ln, c * (16 * (G - LH)) + 16 * n)
                                    eng.sem_inc(s_go, 1)
                                    eng.indirect_dma_start(
                                        out=out, out_offset=bass.IndirectOffsetOnAxis(ap=idxL[:, u, n:n + 1], axis=0),
                                        in_=RL[:, u, n, :], in_offset=None, bounds_check=last_row,
                                        oob_is_err=False).then_inc(s_ln, 16)
                        body(pool, 0, 0)
                        body(pool, 0, 1)
                        with pool.Fori(1, NCH // 2) as i:
                            body(pool, i, 0)
                            body(pool, i, 1)
                        body(pool, NCH // 2, 0)
                        pool.wait_ge(s_sc[0], 16 * G * (NCH // 2 + 1))
                        pool.wait_ge(s_sc[1], 16 * G * (NCH // 2))
                        pool.wait_ge(s_ln, 16 * (G - LH) * NCH)

        last_layer()


def kernel(**inputs):
    import numpy as _np
    import concourse.bacc as _bacc
    from concourse import mybir as _mybir
    from concourse.bass_utils import run_bass_kernel_spmd as _run

    nc = _bacc.Bacc("TRN2", target_bir_lowering=False, num_devices=1)
    arrays, args = {}, []
    for name in _INS:
        a = _np.ascontiguousarray(inputs[name])
        arrays[f"in_{name}_dram"] = a
        args.append(nc.dram_tensor(f"in_{name}_dram", a.shape, _mybir.dt.from_np(a.dtype), kind="ExternalInput").ap())
    shape = inputs["x"].shape
    args.append(nc.dram_tensor("out_0_dram", shape, _mybir.dt.float32, kind="ExternalOutput").ap())
    gnn_program(nc, *args)
    r = _run(nc, [arrays], core_ids=[0])
    return r.results[0]["out_0_dram"]
```
